# Optimizing a Trainium2 kernel written in Bass

```python
import numpy as np
import jax
import jax.numpy as jnp

def _softmax(x, axis=-1):
    return jax.nn.softmax(x, axis=axis)

def _gelu(x):
    return jax.nn.gelu(x, approximate=True)

def _silu(x):
    return jax.nn.silu(x)

def _sigmoid(x):
    return jax.nn.sigmoid(x)

def _layernorm(x, axis=-1, eps=1e-05):
    m = jnp.mean(x, axis=axis, keepdims=True)
    v = jnp.var(x, axis=axis, keepdims=True)
    return (x - m) / jnp.sqrt(v + eps)

def _scatter_add(tgt, idx, src, axis=0):
    return tgt.at[idx].add(src)

def _segment_sum(src, seg, n):
    return jax.ops.segment_sum(src, seg, n)
kernel_name = 'mk_perceiver_d2_seqx_r4_b0e014'

def setup_inputs(seed: int=0):
    np.random.seed(seed)
    _w = jnp.asarray

    def _rec_inputs():
        import jax
        import jax.numpy as jnp
        _rk = jax.random.key(seed)
        x = 7.22e-05 + 1 * jax.random.normal(jax.random.fold_in(_rk, 1), (64, 32, 256), jnp.float32)
        _lenS = 32 - jax.random.randint(jax.random.fold_in(_rk, 7), (64,), 0, max(1, 32 // 4) + 1, jnp.int32)
        _lenS2 = 257 - jax.random.randint(jax.random.fold_in(_rk, 8), (64,), 0, max(1, 257 // 4) + 1, jnp.int32)
        _ctx_1024P = jax.random.normal(jax.random.fold_in(_rk, 11), (64, 16, 256), jnp.float32)
        _ctx_1024c = jax.random.dirichlet(jax.random.fold_in(_rk, 511), 0.3 * jnp.ones((16,), jnp.float32), (64, 257))
        _ctx_1024t = jnp.einsum('bsk,bkd->bsd', _ctx_1024c, _ctx_1024P)
        _ctx_1024t = _ctx_1024t * jax.lax.rsqrt(jnp.mean(jnp.square(_ctx_1024t)) + 1e-12) * 0.953939
        ctx_1024 = 4.13588e-05 + 0.999923 * (_ctx_1024t + 0.3 * jax.random.normal(jax.random.fold_in(_rk, 611), (64, 257, 256), jnp.float32))
        return (x, ctx_1024)
    x, ctx_1024 = _rec_inputs()

    def _L0_xattn_setup():
        import jax, jax.numpy as jnp
        import numpy as np
        D = 256
        H = 16
        HD = D // H
        key = jax.random.key(seed)
        ks = jax.random.split(key, 11)
        B, T = (4, 512)
        s = 1.0 / np.sqrt(D)
        inp = {'q': jax.random.normal(ks[0], (B, T, D), jnp.float32), 'k': jax.random.normal(ks[1], (B, T, D), jnp.float32), 'v': jax.random.normal(ks[2], (B, T, D), jnp.float32), 'Wq': jax.random.normal(ks[3], (D, D), jnp.float32) * s, 'bq': jnp.zeros((D,), jnp.float32), 'Wk': jax.random.normal(ks[4], (D, D), jnp.float32) * s, 'bk': jnp.zeros((D,), jnp.float32), 'Wv': jax.random.normal(ks[5], (D, D), jnp.float32) * s, 'bv': jnp.zeros((D,), jnp.float32), 'Wo': jax.random.normal(ks[6], (D, D), jnp.float32) * s, 'bo': jnp.zeros((D,), jnp.float32)}
        return inp
    _L0_xattn_all = _L0_xattn_setup()
    _L0_xattn_in = {k: v for k, v in _L0_xattn_all.items() if k in ('Wq', 'bq', 'Wk', 'bk', 'Wv', 'bv', 'Wo', 'bo')}
    del _L0_xattn_all

    def _L0_attn_setup():
        import jax, jax.numpy as jnp
        import numpy as np
        DIM = 256
        N_HEADS = 16
        HEAD_DIM = DIM // N_HEADS
        SCALE = HEAD_DIM ** (-0.5)
        key = jax.random.key(seed)
        kx, kq, kk, kv = jax.random.split(key, 4)
        x = jax.random.normal(kx, (2, 512, DIM), dtype=jnp.float32)
        bv_q = jax.random.normal(kq, (N_HEADS, HEAD_DIM), dtype=jnp.float32) * 0.02
        bv_k = jax.random.normal(kk, (N_HEADS, HEAD_DIM), dtype=jnp.float32) * 0.02
        bv_v = jax.random.normal(kv, (N_HEADS, HEAD_DIM), dtype=jnp.float32) * 0.02
        return {'x': x, 'bv_q': bv_q, 'bv_k': bv_k, 'bv_v': bv_v}
    _L0_attn_all = _L0_attn_setup()
    _L0_attn_in = {k: v for k, v in _L0_attn_all.items() if k in ('bv_q', 'bv_k', 'bv_v')}
    del _L0_attn_all

    def _L0_ffn_setup():
        import jax, jax.numpy as jnp
        import numpy as np
        D = 256
        E = 12
        HS = 2 * D
        HR = 3 * D
        TAU = 1.5

        def _geglu(h):
            a, g = jnp.split(h, 2, axis=-1)
            return a * jax.nn.gelu(g, approximate=False)
        key = jax.random.key(seed)
        ks = jax.random.split(key, 12)

        def xavier(k, shape):
            fan_in, fan_out = (shape[-2], shape[-1])
            lim = jnp.sqrt(6.0 / (fan_in + fan_out))
            return jax.random.uniform(k, shape, jnp.float32, -lim, lim)
        x = jax.random.normal(ks[0], (2, 256, D), jnp.float32)
        Ws1 = xavier(ks[1], (D, 2 * HS))
        bs1 = jnp.zeros((2 * HS,), jnp.float32)
        Ws2 = xavier(ks[2], (HS, D))
        bs2 = jnp.zeros((D,), jnp.float32)
        We1 = xavier(ks[3], (E, D, 2 * HR))
        be1 = jnp.zeros((E, 2 * HR), jnp.float32)
        We2 = xavier(ks[4], (E, HR, D))
        be2 = jnp.zeros((E, D), jnp.float32)
        Wr = xavier(ks[5], (D, E))
        br = jnp.zeros((E,), jnp.float32)
        return {'x': x, 'Ws1': Ws1, 'bs1': bs1, 'Ws2': Ws2, 'bs2': bs2, 'We1': We1, 'be1': be1, 'We2': We2, 'be2': be2, 'Wr': Wr, 'br': br}
    _L0_ffn_all = _L0_ffn_setup()
    _L0_ffn_in = {k: v for k, v in _L0_ffn_all.items() if k in ('Ws1', 'bs1', 'Ws2', 'bs2', 'We1', 'be1', 'We2', 'be2', 'Wr', 'br')}
    del _L0_ffn_all

    def _L1_xattn_setup():
        import jax, jax.numpy as jnp
        import numpy as np
        N_HEAD = 16
        key = jax.random.key(seed)
        ks = jax.random.split(key, 5)
        b, l, d = (4, 512, 256)
        dh = d // N_HEAD
        return {'q': jax.random.normal(ks[0], (b, l, d), dtype=jnp.float32), 'kv': jax.random.normal(ks[1], (b, l, d), dtype=jnp.float32), 'Wq': jax.random.normal(ks[2], (d, d), dtype=jnp.float32) * 0.02, 'Wkv': jax.random.normal(ks[3], (2 * dh, d), dtype=jnp.float32) * 0.02, 'Wc': jax.random.normal(ks[4], (d, d), dtype=jnp.float32) * 0.02}
    _L1_xattn_all = _L1_xattn_setup()
    _L1_xattn_in = {k: v for k, v in _L1_xattn_all.items() if k in ('Wq', 'Wkv', 'Wc')}
    del _L1_xattn_all

    def _L1_attn_setup():
        import jax, jax.numpy as jnp
        import numpy as np
        N_HEADS = 16
        ROPE_BASE = 10000.0

        def _rope(x):
            B, H, S, D = x.shape
            inv_freq = 1.0 / ROPE_BASE ** (jnp.arange(0, D, 2, dtype=jnp.float32) / D)
            ang = jnp.arange(S, dtype=jnp.float32)[:, None] * inv_freq[None, :]
            cos, sin = (jnp.cos(ang), jnp.sin(ang))
            x1 = x[..., 0::2]
            x2 = x[..., 1::2]
            r1 = x1 * cos - x2 * sin
            r2 = x1 * sin + x2 * cos
            return jnp.stack([r1, r2], axis=-1).reshape(B, H, S, D)
        key = jax.random.key(seed)
        k0, k1, k2, k3, k4 = jax.random.split(key, 5)
        B, S, E, Hd = (2, 512, 256, 256)
        scale = 0.02
        return {'x': jax.random.normal(k0, (B, S, E), dtype=jnp.float32), 'Wq': jax.random.normal(k1, (E, Hd), dtype=jnp.float32) * scale, 'Wk': jax.random.normal(k2, (E, Hd), dtype=jnp.float32) * scale, 'Wv': jax.random.normal(k3, (E, Hd), dtype=jnp.float32) * scale, 'Wo': jax.random.normal(k4, (Hd, E), dtype=jnp.float32) * scale}
    _L1_attn_all = _L1_attn_setup()
    _L1_attn_in = {k: v for k, v in _L1_attn_all.items() if k in ('Wq', 'Wk', 'Wv', 'Wo')}
    del _L1_attn_all

    def _L1_ffn_setup():
        import jax, jax.numpy as jnp
        import numpy as np
        DIM = 256
        HID = 512
        OUT = 256
        NE = 8
        TOPK = 2

        def _xavier(key, shape):
            fan_in, fan_out = (shape[-2], shape[-1])
            lim = jnp.sqrt(6.0 / (fan_in + fan_out))
            return jax.random.uniform(key, shape, jnp.float32, -lim, lim)
        key = jax.random.key(seed)
        ks = jax.random.split(key, 8)
        X = jax.random.normal(ks[0], (4, 256, DIM), jnp.float32)
        W1 = _xavier(ks[1], (NE, DIM, HID))
        W3 = _xavier(ks[2], (NE, DIM, HID))
        W2 = _xavier(ks[3], (NE, HID, OUT))
        b1 = jnp.zeros((NE, HID), jnp.float32)
        b3 = jnp.zeros((NE, HID), jnp.float32)
        b2 = jnp.zeros((NE, OUT), jnp.float32)
        Wg = _xavier(ks[4], (DIM, NE))
        bg = jnp.zeros((NE,), jnp.float32)
        Wf = _xavier(ks[5], (OUT, OUT))
        bf = jnp.zeros((OUT,), jnp.float32)
        return {'X': X, 'W1': W1, 'b1': b1, 'W3': W3, 'b3': b3, 'W2': W2, 'b2': b2, 'Wg': Wg, 'bg': bg, 'Wf': Wf, 'bf': bf}
    _L1_ffn_all = _L1_ffn_setup()
    _L1_ffn_in = {k: v for k, v in _L1_ffn_all.items() if k in ('W1', 'b1', 'W3', 'b3', 'W2', 'b2', 'Wg', 'bg', 'Wf', 'bf')}
    del _L1_ffn_all
    return {'x': x, 'ctx_1024': ctx_1024, 'L0_xattn_Wq': _L0_xattn_in['Wq'], 'L0_xattn_bq': _L0_xattn_in['bq'], 'L0_xattn_Wk': _L0_xattn_in['Wk'], 'L0_xattn_bk': _L0_xattn_in['bk'], 'L0_xattn_Wv': _L0_xattn_in['Wv'], 'L0_xattn_bv': _L0_xattn_in['bv'], 'L0_xattn_Wo': _L0_xattn_in['Wo'], 'L0_xattn_bo': _L0_xattn_in['bo'], 'L0_attn_bv_q': _L0_attn_in['bv_q'], 'L0_attn_bv_k': _L0_attn_in['bv_k'], 'L0_attn_bv_v': _L0_attn_in['bv_v'], 'L0_ffn_Ws1': _L0_ffn_in['Ws1'], 'L0_ffn_bs1': _L0_ffn_in['bs1'], 'L0_ffn_Ws2': _L0_ffn_in['Ws2'], 'L0_ffn_bs2': _L0_ffn_in['bs2'], 'L0_ffn_We1': _L0_ffn_in['We1'], 'L0_ffn_be1': _L0_ffn_in['be1'], 'L0_ffn_We2': _L0_ffn_in['We2'], 'L0_ffn_be2': _L0_ffn_in['be2'], 'L0_ffn_Wr': _L0_ffn_in['Wr'], 'L0_ffn_br': _L0_ffn_in['br'], 'L1_xattn_Wq': _L1_xattn_in['Wq'], 'L1_xattn_Wkv': _L1_xattn_in['Wkv'], 'L1_xattn_Wc': _L1_xattn_in['Wc'], 'L1_attn_Wq': _L1_attn_in['Wq'], 'L1_attn_Wk': _L1_attn_in['Wk'], 'L1_attn_Wv': _L1_attn_in['Wv'], 'L1_attn_Wo': _L1_attn_in['Wo'], 'L1_ffn_W1': _L1_ffn_in['W1'], 'L1_ffn_b1': _L1_ffn_in['b1'], 'L1_ffn_W3': _L1_ffn_in['W3'], 'L1_ffn_b3': _L1_ffn_in['b3'], 'L1_ffn_W2': _L1_ffn_in['W2'], 'L1_ffn_b2': _L1_ffn_in['b2'], 'L1_ffn_Wg': _L1_ffn_in['Wg'], 'L1_ffn_bg': _L1_ffn_in['bg'], 'L1_ffn_Wf': _L1_ffn_in['Wf'], 'L1_ffn_bf': _L1_ffn_in['bf']}

def reference(x, ctx_1024, L0_xattn_Wq, L0_xattn_bq, L0_xattn_Wk, L0_xattn_bk, L0_xattn_Wv, L0_xattn_bv, L0_xattn_Wo, L0_xattn_bo, L0_attn_bv_q, L0_attn_bv_k, L0_attn_bv_v, L0_ffn_Ws1, L0_ffn_bs1, L0_ffn_Ws2, L0_ffn_bs2, L0_ffn_We1, L0_ffn_be1, L0_ffn_We2, L0_ffn_be2, L0_ffn_Wr, L0_ffn_br, L1_xattn_Wq, L1_xattn_Wkv, L1_xattn_Wc, L1_attn_Wq, L1_attn_Wk, L1_attn_Wv, L1_attn_Wo, L1_ffn_W1, L1_ffn_b1, L1_ffn_W3, L1_ffn_b3, L1_ffn_W2, L1_ffn_b2, L1_ffn_Wg, L1_ffn_bg, L1_ffn_Wf, L1_ffn_bf):
    import jax
    import jax.numpy as jnp

    def _L0_xattn_ref(q, k, v, Wq, bq, Wk, bk, Wv, bv, Wo, bo):
        import jax, jax.numpy as jnp
        import numpy as np
        D = 256
        H = 16
        HD = D // H
        B, Tq, _ = q.shape
        Tk = k.shape[1]
        qw = q @ Wq + bq
        kw = k @ Wk + bk
        vw = v @ Wv + bv
        qh = qw.reshape(B, Tq, H, HD)
        kh = kw.reshape(B, Tk, H, HD)
        vh = vw.reshape(B, Tk, H, HD)
        scale = 1.0 / np.sqrt(HD).astype(np.float32)
        logits = jnp.einsum('bqhd,bkhd->bhqk', qh, kh) * scale
        causal = jnp.tril(jnp.ones((Tq, Tk), bool))
        logits = jnp.where(causal, logits, -jnp.inf)
        attn = jax.nn.softmax(logits, axis=-1)
        out = jnp.einsum('bhqk,bkhd->bqhd', attn, vh).reshape(B, Tq, D)
        return out @ Wo + bo

    def _L0_attn_ref(x, bv_q, bv_k, bv_v):
        import jax, jax.numpy as jnp
        import numpy as np
        DIM = 256
        N_HEADS = 16
        HEAD_DIM = DIM // N_HEADS
        SCALE = HEAD_DIM ** (-0.5)
        B, T, D = x.shape
        H, HD = (N_HEADS, HEAD_DIM)
        x_h = x.reshape(B, T, H, HD)
        Q = x_h * jnp.sign(bv_q)
        K = x_h * jnp.sign(bv_k)
        V = x_h * jnp.sign(bv_v)
        scores = jnp.einsum('bqhd,bkhd->bhqk', Q, K) * SCALE
        causal = jnp.tril(jnp.ones((T, T), dtype=bool))
        attn = jnp.where(causal, jax.nn.sigmoid(scores * 4.0), 0.0)
        out = jnp.einsum('bhqk,bkhd->bqhd', attn, V)
        return out.reshape(B, T, D)

    def _L0_ffn_ref(x, Ws1, bs1, Ws2, bs2, We1, be1, We2, be2, Wr, br):
        import jax, jax.numpy as jnp
        import numpy as np
        D = 256
        E = 12
        HS = 2 * D
        HR = 3 * D
        TAU = 1.5

        def _geglu(h):
            a, g = jnp.split(h, 2, axis=-1)
            return a * jax.nn.gelu(g, approximate=False)
        B, T, Dm = x.shape
        xf = x.reshape(-1, Dm)
        ys = _geglu(xf @ Ws1 + bs1) @ Ws2 + bs2
        logits = (xf @ Wr + br) / TAU
        top_val, top_idx = jax.lax.top_k(logits, 2)
        top_w = jax.nn.softmax(top_val, axis=-1)
        onehot = jax.nn.one_hot(top_idx, E, dtype=x.dtype)
        w = jnp.einsum('nke,nk->ne', onehot, top_w)
        h = jnp.einsum('nd,edh->enh', xf, We1) + be1[:, None, :]
        act = _geglu(h)
        yE = jnp.einsum('enh,ehd->end', act, We2) + be2[:, None, :]
        yr = jnp.einsum('end,ne->nd', yE, w)
        return (ys + yr).reshape(B, T, Dm)

    def _L1_xattn_ref(q, kv, Wq, Wkv, Wc):
        import jax, jax.numpy as jnp
        import numpy as np
        N_HEAD = 16
        b, l, d = q.shape
        h = N_HEAD
        dh = d // h
        qp = jnp.einsum('bld,ed->ble', q, Wq)
        scores = jnp.einsum('bld,bmd->blm', qp, kv)
        idx = jnp.argmax(scores, axis=-1)
        mem = jnp.take_along_axis(kv, idx[..., None], axis=1)
        mkv = jnp.einsum('bld,ed->ble', mem, Wkv)
        mk, mv = jnp.split(mkv, 2, axis=-1)
        qh = qp.reshape(b, l, h, dh).transpose(0, 2, 1, 3)
        scale = 1.0 / np.sqrt(dh).astype(np.float32)
        logits = jnp.einsum('bhld,bmd->bhlm', qh, mk) * scale
        attn = jax.nn.softmax(logits, axis=-1)
        out = jnp.einsum('bhlm,bmd->bhld', attn, mv)
        out = out.transpose(0, 2, 1, 3).reshape(b, l, d)
        return jnp.einsum('bld,ed->ble', out, Wc)

    def _L1_attn_ref(x, Wq, Wk, Wv, Wo):
        import jax, jax.numpy as jnp
        import numpy as np
        N_HEADS = 16
        ROPE_BASE = 10000.0

        def _rope(x):
            B, H, S, D = x.shape
            inv_freq = 1.0 / ROPE_BASE ** (jnp.arange(0, D, 2, dtype=jnp.float32) / D)
            ang = jnp.arange(S, dtype=jnp.float32)[:, None] * inv_freq[None, :]
            cos, sin = (jnp.cos(ang), jnp.sin(ang))
            x1 = x[..., 0::2]
            x2 = x[..., 1::2]
            r1 = x1 * cos - x2 * sin
            r2 = x1 * sin + x2 * cos
            return jnp.stack([r1, r2], axis=-1).reshape(B, H, S, D)
        B, S, E = x.shape
        Hd = Wq.shape[1]
        D = Hd // N_HEADS
        attn_scale = 1.0 / jnp.sqrt(jnp.asarray(D, x.dtype))
        q = jnp.einsum('bse,eh->bsh', x, Wq).reshape(B, S, N_HEADS, D).transpose(0, 2, 1, 3)
        k = jnp.einsum('bse,eh->bsh', x, Wk).reshape(B, S, N_HEADS, D).transpose(0, 2, 1, 3)
        v = jnp.einsum('bse,eh->bsh', x, Wv).reshape(B, S, N_HEADS, D).transpose(0, 2, 1, 3)
        q = _rope(q)
        k = _rope(k)
        scores = jnp.einsum('bhsd,bhtd->bhst', q, k) * attn_scale
        causal = jnp.triu(jnp.ones((S, S), dtype=bool), 1)
        scores = jnp.where(causal, jnp.asarray(-jnp.inf, scores.dtype), scores)
        probs = jax.nn.softmax(scores, axis=-1)
        out = jnp.einsum('bhst,bhtd->bhsd', probs, v)
        out = out.transpose(0, 2, 1, 3).reshape(B, S, Hd)
        return jnp.einsum('bsh,he->bse', out, Wo)

    def _L1_ffn_ref(X, W1, b1, W3, b3, W2, b2, Wg, bg, Wf, bf):
        import jax, jax.numpy as jnp
        import numpy as np
        DIM = 256
        HID = 512
        OUT = 256
        NE = 8
        TOPK = 2

        def _xavier(key, shape):
            fan_in, fan_out = (shape[-2], shape[-1])
            lim = jnp.sqrt(6.0 / (fan_in + fan_out))
            return jax.random.uniform(key, shape, jnp.float32, -lim, lim)
        gating = jax.nn.softmax(X @ Wg + bg, axis=-1)
        top_k_indices = jnp.argsort(gating, axis=-1)[..., -TOPK:]
        h1 = jnp.einsum('bsd,edh->bseh', X, W1) + b1
        h3 = jnp.einsum('bsd,edh->bseh', X, W3) + b3
        h = jax.nn.silu(h1 * h3)
        expert_outputs = jnp.einsum('bseh,eho->bseo', h, W2) + b2
        topk_out = jnp.take_along_axis(expert_outputs, top_k_indices[..., None], axis=2)
        topk_w = jnp.take_along_axis(gating, top_k_indices, axis=-1)
        mixed = jnp.sum(topk_w[..., None] * topk_out, axis=2)
        return mixed @ Wf + bf
    x = x + _L0_xattn_ref(_layernorm(x, axis=-1), ctx_1024, ctx_1024, L0_xattn_Wq, L0_xattn_bq, L0_xattn_Wk, L0_xattn_bk, L0_xattn_Wv, L0_xattn_bv, L0_xattn_Wo, L0_xattn_bo)
    x = x + _L0_attn_ref(_layernorm(x, axis=-1), L0_attn_bv_q, L0_attn_bv_k, L0_attn_bv_v)
    x = x + _L0_ffn_ref(_layernorm(x, axis=-1), L0_ffn_Ws1, L0_ffn_bs1, L0_ffn_Ws2, L0_ffn_bs2, L0_ffn_We1, L0_ffn_be1, L0_ffn_We2, L0_ffn_be2, L0_ffn_Wr, L0_ffn_br)
    x = x + _L1_xattn_ref(_layernorm(x, axis=-1), ctx_1024, L1_xattn_Wq, L1_xattn_Wkv, L1_xattn_Wc)
    x = x + _L1_attn_ref(_layernorm(x, axis=-1), L1_attn_Wq, L1_attn_Wk, L1_attn_Wv, L1_attn_Wo)
    x = x + _L1_ffn_ref(_layernorm(x, axis=-1), L1_ffn_W1, L1_ffn_b1, L1_ffn_W3, L1_ffn_b3, L1_ffn_W2, L1_ffn_b2, L1_ffn_Wg, L1_ffn_bg, L1_ffn_Wf, L1_ffn_bf)
    return x

_drawn_inputs = setup_inputs


def setup_inputs(seed=0):
    import zlib

    import numpy as np

    out = dict(_drawn_inputs(seed))
    spreads = {'L0_xattn_bq': (0.0, 0.1),
     'L0_xattn_bk': (0.0, 0.8),
     'L0_xattn_bv': (0.0, 0.1),
     'L0_xattn_bo': (0.0, 0.1),
     'L0_ffn_bs1': (0.0, 0.692),
     'L0_ffn_bs2': (0.0, 0.42),
     'L0_ffn_be1': (0.0, 0.8),
     'L0_ffn_be2': (0.0, 0.59),
     'L0_ffn_br': (0.0, 0.746),
     'L1_ffn_b1': (0.0, 0.8),
     'L1_ffn_b3': (0.0, 0.8),
     'L1_ffn_b2': (0.0, 0.8),
     'L1_ffn_bg': (0.0, 0.8),
     'L1_ffn_bf': (0.0, 0.456)}
    factors = {'L1_xattn_Wq': 4.575,
     'L1_xattn_Wkv': 3.66,
     'L1_xattn_Wc': 3.695,
     'L1_attn_Wq': 8.0,
     'L1_attn_Wk': 8.0,
     'L1_attn_Wv': 3.84,
     'L1_attn_Wo': 3.872}
    for name, (base, spread) in spreads.items():
        noise = np.random.default_rng([zlib.crc32(name.encode()), seed]).standard_normal(out[name].shape)
        drawn = base * np.exp(spread * noise) if base else spread * noise
        out[name] = jnp.asarray(drawn.astype(out[name].dtype))
    for name, factor in factors.items():
        out[name] = (out[name] * factor).astype(out[name].dtype)
    return out
```

```python
from contextlib import ExitStack

import numpy as np
import concourse.bass as bass
from concourse import mybir

F32 = mybir.dt.float32
BF16 = mybir.dt.bfloat16
I32 = mybir.dt.int32
U32 = mybir.dt.uint32
ALU = mybir.AluOpType
ACT = mybir.ActivationFunctionType
AX = mybir.AxisListType

B, T, D = 64, 32, 256
S = 257
H, HD = 16, 16
P = 128
NT = B * T // P
BT = P // T
C2 = D // P
HC = P // HD
EPS = 1e-5
NEG = -1e30
E0, HR, HS = 12, 768, 512
E1, HX = 8, 512
PAIRS = 2 * B * T
M0_TILES = PAIRS // P + E0
M1_TILES = PAIRS // P + E1
TAU = 1.5
STOP = None


def constants():
    p = np.arange(P)
    ident = np.eye(P, dtype=np.float32)
    head_mask = (p[:, None] // HD == np.arange(HC)[None, :]).astype(np.float32)
    block_ones = (p[:, None] // T == np.arange(BT)[None, :]).astype(np.float32)
    key, tok = np.arange(T)[None, :], (p % T)[:, None]
    causal = np.tile(np.where(key <= tok, 0.0, NEG).astype(np.float32), (1, H))
    before = (p[:, None] < p[None, :]).astype(np.float32)
    dd = p % HD
    inv = (np.float32(1.0) / np.float32(10000.0) ** (np.arange(0, HD, 2, dtype=np.float32) / np.float32(HD))).astype(np.float32)
    ang = np.arange(T, dtype=np.float32)[None, :] * inv[dd // 2][:, None]
    cos = np.cos(ang).astype(np.float32)
    sin = (np.sin(ang) * np.where(dd % 2 == 0, -1.0, 1.0)[:, None]).astype(np.float32)
    row0 = ((np.arange(NT)[None, :] * BT + (p // T)[:, None]) * S).astype(np.float32)
    experts = np.zeros((P, E0, E0), np.float32)
    experts[:] = np.tril(np.ones((E0, E0), np.float32))[None]
    ranks = np.broadcast_to(np.concatenate([E0 - np.arange(E0), 1.0 + np.arange(E1)]).astype(np.float32), (P, E0 + E1))
    slots = np.broadcast_to(np.arange(M0_TILES, dtype=np.float32), (P, M0_TILES))
    cols = [("ident", ident), ("head_mask", head_mask), ("block_ones", block_ones), ("causal", causal),
            ("before", before), ("cos", cos), ("sin", sin), ("row0", row0), ("tril", experts.reshape(P, -1)),
            ("ranks", ranks), ("slots", slots)]
    at, where = 0, {}
    for name, a in cols:
        where[name] = (at, at + a.shape[1])
        at += a.shape[1]
    return np.ascontiguousarray(np.concatenate([a for _, a in cols], axis=1)), where


CONST, WHERE = constants()

ATTN = (0, 1, 2, 3)
USES = {
    "stat": ATTN, "mv": ATTN, "var": ATTN, "rstd": ATTN, "xn": ATTN, "xt_ps": ATTN, "xt_sb": ATTN,
    "ctx": (0,), "qk_ps": (0, 3), "q_ps": (2,), "q_sb": (2,), "k_ps": (2,), "qk_sb": (0, 2, 3), "rope": (3,),
    "v_ps": (0, 2, 3), "v_sb": ATTN, "vb": ATTN, "kb": ATTN, "sc_ps": ATTN, "mx": (0, 2, 3), "sub": (0, 2, 3),
    "prob": ATTN, "pt_ps": ATTN, "pt_sb": ATTN, "o_ps": ATTN, "rc": (0, 2, 3), "o_sb": ATTN,
    "ot_ps": (0, 2, 3), "ot_sb": (0, 2, 3), "y_ps": (0, 2, 3), "res": ATTN, "vd": ATTN,
    "cxt": (2,), "cs_ps": (2,), "top": (2,), "idx": (2,), "row": (2,), "mem": (2,), "mt_ps": (2,), "mt_sb": (2,),
}
PER = {"ctx": 16, "cxt": 16, "vd": 16, "vb": 64, "mem": 16}
LOOP_FROM = 4


def build(nc, a, out):
    ctx = ExitStack()
    with ctx:
        def sb(name, shape, dt=F32):
            return ctx.enter_context(nc.sbuf_tensor(name, shape, dt))

        def psum(name, shape, dt=F32):
            return ctx.enter_context(nc.psum_tensor(name, shape, dt))

        def new_sem(name):
            return ctx.enter_context(nc.semaphore(name))

        sorted_rows = [nc.dram_tensor(f"sorted_rows{m}", (n * P, D), F32).ap() for m, n in enumerate((M0_TILES, M1_TILES))]
        expert_rows = [nc.dram_tensor(f"expert_rows{m}", (n * P, D), F32).ap() for m, n in enumerate((M0_TILES, M1_TILES))]

        v_rows = nc.dram_tensor("v_rows", (2, P, D), F32).ap()

        cst = sb("cst", [P, CONST.shape[1]])

        def const(name, parts=P):
            lo, hi = WHERE[name]
            return cst[0:parts, lo:hi]

        X = sb("X", [P, NT, D])
        XN = sb("XN", [P, 2, D])
        XT = sb("XT", [P, 2, C2, P])
        QK = sb("QK", [P, 2, 4, P])
        KB = sb("KB", [P, 2, C2, HC, P])
        VS = sb("VS", [P, 2, D])
        VB = sb("VB", [P, 2, BT, 4, 64])
        PR = sb("PR", [P, 2, H * T])
        PT = sb("PT", [P, 2, 4, P])
        OS = sb("OS", [P, 2, D])
        OT = sb("OT", [P, C2, P])
        CT = sb("CT", [P, 2, C2, P])
        CXT = sb("CXT", [P, 2, C2, BT, S])
        MEM = sb("MEM", [P, 2, D])
        RT = sb("RT", [P, 2, 4 * P])
        stats = sb("stats", [P, 2, 6])
        mv = sb("mv", [P, 2, 2])
        var = sb("var", [P, 2, 1])
        rstd = sb("rstd", [P, 2, 1])
        minus_half = sb("minus_half", [P, 1])
        mx = sb("mx", [P, H])
        rc = sb("rc", [P, H])
        hold = sb("hold", [P, 1])
        top8 = sb("top8", [P, 8])
        idx8 = sb("idx8", [P, 8], U32)
        idxf = sb("idxf", [P, 1])
        row = sb("row", [P, 2], I32)
        ones = sb("ones", [1, P])
        ident_bf = sb("ident_bf", [P, P], BF16)
        causal_bf = sb("causal_bf", [P, H * T], BF16)
        sign_cols = sb("sign_cols", [P, 2, C2])
        sign_qk = sb("sign_qk", [P, C2])
        sign_mask = sb("sign_mask", [P, C2, HC])
        sign_v = sb("sign_v", [P, D])
        wname = ["Wq0", "Wk0", "Wv0", "Wo0", "Wq2", "Wk2", "Wv2", "Wo2", "Wq3", "Wk3", "Wqs3", "Wks3", "Wv3", "Wo3"]
        first_w = sb("first_w", [P, 4, C2, D])
        W = {n: first_w[:, i] for i, n in enumerate(wname[:4])} | {n: sb(n, [P, C2, D])[:] for n in wname[4:]}
        qk_bias = sb("qk_bias", [P, 4])
        rows0 = sb("rows0", [1, 2, D])
        XNA = sb("XNA", [P, NT, D])
        LG = sb("LG", [P, NT, E0])
        Wr = [sb(f"Wr{m}", [P, C2, e]) for m, e in enumerate((E0, E1))]
        br = [sb(f"br{m}", [1, e]) for m, e in enumerate((E0, E1))]
        wts = sb("wts", [P, 2, NT])
        pos = sb("pos", [P, 2, NT], I32)
        slot_e = sb("slot_e", [1, M0_TILES], I32)
        zeros = sb("zeros", [P, D])
        W1F, W1X = C2 * 2 * HR + 2 * HR // P, C2 * 2 * HX + 2 * HX // P
        W1 = sb("W1", [P, 2, max(W1F, W1X)])
        W2 = sb("W2", [P, 2, HR // P, D])
        b2 = sb("b2", [1, 2, D])
        XS = sb("XS", [P, 2, D])
        GS = sb("GS", [P, 2, 2, P])
        HB = sb("HB", [P, 2, HR // P, P])
        YS = sb("YS", [P, 2, D])
        GY = sb("GY", [P, 2, 2, D])
        Wf = sb("Wf", [P, C2, D])
        bf = sb("bf", [1, D])
        XTA = CXT[:].rearrange("p a c b s -> p (a c b s)")[:, 0:C2 * NT * P].rearrange("p (c n) -> p c n", c=C2)
        Ws1 = first_w[:].rearrange("p i c n -> p (i c n)").rearrange("p (c n) -> p c n", c=C2)
        Ws2 = sb("Ws2", [P, HS // P, D])
        bs1 = sb("bs1", [P, 2 * HS // P])
        bs2 = sb("bs2", [1, D])
        kb_flat = KB[:].rearrange("p a c h n -> p (a c h n)")
        SG = kb_flat[:, 0:1024].rearrange("p (a n) -> p a n", a=2)
        SH = kb_flat[:, 1024:1024 + 4 * HS].rearrange("p (a n) -> p a n", n=512)
        pt_flat, pr_flat = PT[:].rearrange("p a g n -> p (a g n)"), PR[:].rearrange("p a n -> p (a n)")

        def scratch(buf, at, n, e):
            return buf[:, at:at + n * e].rearrange("p (n e) -> p n e", e=e)

        RA, RB, RO = (scratch(pt_flat, i * NT * E0, NT, E0) for i in range(3))
        RX = scratch(pt_flat, 3 * NT * E0, E0, E0)
        RE = scratch(pr_flat, 0, M0_TILES, E0)
        RM = sb("RM", [P, 2, NT, E0])
        RC = sb("RC", [P, NT, E0])
        r16 = [sb(f"r16_{i}", [P, NT]) for i in range(4)]
        re_ = [sb(f"re_{i}", [P, E0]) for i in range(3)]
        rei = sb("rei", [P, E0], I32)
        rsl = sb("rsl", [P, M0_TILES])

        ones_sq = sb("ones_sq", [P, P])
        MLP_LOADS = ((Wr[0][:], "Wr0"), (br[0][:], "br0"), (Wr[1][:], "Wr1"), (br[1][:], "br1"), (Ws1, "Ws1"), (Ws2[:], "Ws2"),
                     (bs1[:], "bs1"), (bs2[:], "bs2"), (Wf[:], "Wf"), (bf[:], "bf"))

        bank = [psum(f"bank{i}", [P, 512]) for i in range(8)]

        s = {n: [new_sem(f"s_{n}{i}") for i in range(2)] if n in PER else new_sem("s_" + n) for n in USES}

        def need(eng, sem, v):
            if not isinstance(v, int) or v > 0:
                eng.wait_ge(sem, v)

        def n_before(name, k):
            return NT * len([q for q in USES[name] if q < k])

        def wait(eng, name, k, count):
            need(eng, s[name], n_before(name, k) + count)

        def dma_count(name, k, at, d):
            return (n_before(name, k) // 2 + at.half(d) + 1) * PER[name]

        def wait_dma(eng, name, k, at, d):
            need(eng, s[name][at.par(d)], dma_count(name, k, at, d))

        s_load = [new_sem(f"s_load{i}") for i in range(3)]
        s_dump = new_sem("s_dump")
        s_prep = new_sem("s_prep")
        s_sign = new_sem("s_sign")
        s_clear = new_sem("s_clear")
        s_zero_rows = new_sem("s_zero_rows")
        s_route_step = new_sem("s_route_step")
        s_x = [new_sem(f"s_x{i}") for i in range(4)]

        PAIRED = ["xs", "w1", "w2", "y_out", "gy"]
        MSEM = ["stat", "mv", "var", "rstd", "xn", "xt_ps", "xt_sb", "xna", "xta", "lg_ps", "lg_sb", "gate", "gate_e", "onehot", "rank_ps",
                "pos", "scat", "xs", "w1", "w2", "t_ps", "t_sb", "g_ps", "a_ps", "gate_sb", "u", "hid", "y_ps", "y_sb",
                "y_out", "gy", "mix", "comb"]
        ms = [{n: [new_sem(f"m{m}_{n}{i}") for i in range(2)] if n in PAIRED else new_sem(f"m{m}_{n}") for n in MSEM}
              for m in range(2)]
        sh = {n: new_sem("sh_" + n) for n in ("g_ps", "a_ps", "gate", "hid", "y_ps", "res")}
        fin = {n: new_sem("fin_" + n) for n in ("xt_ps", "xt_sb", "y_ps", "out", "dma")}

        def tiles_of(k, st):
            return (st + 2, st + 1, st, st - 1) if k == 2 else (st + 1, None, st, st - 1)

        class At:

            def __init__(self, st, u, h, mid):
                self.st, self.u, self.h, self.mid = st, u, h, mid

            def half(self, d):
                return self.h + (self.u + d) // 2

            def par(self, d):
                return (self.u + d) % 2

        def alone(body, *sts):
            for st in sts:
                body(At(st, st % 2, st // 2, False))

        def run_steps(eng, first, end, body, loop_end):
            alone(body, *range(first, LOOP_FROM))
            with eng.Fori(0, (loop_end - LOOP_FROM) // 2) as j:
                for u in range(2):
                    body(At(LOOP_FROM + 2 * j + u, u, LOOP_FROM // 2 + j, True))
            alone(body, *range(loop_end, end))

        def steps(eng, k, body):
            run_steps(eng, -2 if k == 2 else -1, NT + 1, body, NT - 2)

        def row_steps(eng, n, first, body):
            run_steps(eng, first, n + 1, body, n - 2)

        def token_steps(eng, body, first=0, end=NT):
            run_steps(eng, first, end, body, NT - 2)

        def live(t, mid, n=NT):
            return t is not None and (mid or 0 <= t < n)

        def one(t):
            return bass.ds(t, 1)

        def span(t, w):
            return bass.ds(t * w, w)

        ORDER = ["A0", "A1", "M0", "A2", "A3", "M1"]
        plan = ORDER[:ORDER.index(STOP) + 1] if STOP else ORDER

        MOE = [dict(E=E0, n=M0_TILES, hid=HR, R=HR // P // 2, W1=a["W1_0"], W2=a["W2_0"], b2=a["b2_0"]),
               dict(E=E1, n=M1_TILES, hid=HX, R=HX // P // 2, W1=a["W1_1"], W2=a["W2_1"], b2=a["b2_1"])]

        block = ctx.enter_context(nc.Block())

        @block.sync
        def _(sp):
            sp.dma_start(cst[:], a["cst"]).then_inc(s_load[0], 16)
            sp.dma_start(X[:, 0:4, :], a["x"][:, 0:4, :]).then_inc(s_x[0], 16)
            for n in wname[:4]:
                sp.dma_start(W[n], a[n]).then_inc(s_load[0], 16)
            sp.dma_start(qk_bias[:], a["qk_bias"]).then_inc(s_load[0], 16)
            sp.dma_start(rows0[:], a["rows0"]).then_inc(s_load[0], 16)
            sp.dma_start(sign_cols[:], a["sign_cols"]).then_inc(s_load[0], 16)
            sp.dma_start(sign_v[:], a["sign_v"].to_broadcast([P, D])).then_inc(s_load[0], 16)
            for q in range(1, 4):
                sp.dma_start(X[:, 4 * q:4 * q + 4, :], a["x"][:, 4 * q:4 * q + 4, :]).then_inc(s_x[q], 16)

            def later_loads():
                for n in wname[4:]:
                    sp.dma_start(W[n], a[n]).then_inc(s_load[1], 16)
                wait(sp, "y_ps", 0, NT)
                for dst, n in MLP_LOADS:
                    sp.dma_start(dst, a[n]).then_inc(s_load[2], 16)

            def zero_sorted_rows():
                sp.wait_ge(s_clear, 4)
                for m in range(2):
                    n = MOE[m]["n"]
                    sp.dma_start(sorted_rows[m].rearrange("(n p) d -> p n d", p=P),
                                 zeros[:, None, :].to_broadcast([P, n, D])).then_inc(s_zero_rows, 16)

            def ahead(v):
                return v if isinstance(v, int) else sp.to_reg(v)

            def attention_step(k, at):
                st, u, mid = at.st, at.u, at.mid
                tf, tc, ta, tb = tiles_of(k, st)
                if live(ta, mid):
                    n_source, n_used = ahead(n_before("v_sb", k) + ta + 1), ahead(n_before("o_ps", k) + ta - 1)
                    n_stored, n_spread = ahead(dma_count("vd", k, at, 0)), ahead(dma_count("vb", k, at, -2))
                if k == 0 and live(tf, mid):
                    wait(sp, "v_ps", 0, tf - 1)
                    sp.dma_start(CT[:, 1 - u, :, :], a["ctx32"][:, one(tf), :, :]).then_inc(s["ctx"][at.par(1)], 16)
                if k == 2 and live(tf, mid):
                    wait(sp, "cs_ps", 2, tf - 1)
                    sp.dma_start(CXT[:, u, :, :, :], a["ctxT"][:, one(tf), :, :, :]).then_inc(s["cxt"][u], 16)
                if live(ta, mid):
                    need(sp, s["v_sb"], n_source)
                    need(sp, s["vb"][u], n_spread)
                    sp.dma_start(v_rows[u], VS[:, u, :]).then_inc(s["vd"][u], 16)
                    need(sp, s["vd"][u], n_stored)
                    need(sp, s["o_ps"], n_used)
                    for h in range(4):
                        sp.dma_start(VB[32 * h:32 * h + 32, u, :, h, :],
                                     v_rows[u].rearrange("(b k) (h e) -> h k b e", b=BT, h=4)[h]).then_inc(s["vb"][u], 16)

            def expert_step(m, at):
                st, u, mid = at.st, at.u, at.mid
                q, n = ms[m], MOE[m]["n"]
                if live(st + 1, mid, n):
                    e_next = sp.value_load(slot_e[0:1, one(st + 1)], min_val=0, max_val=MOE[m]["E"] - 1)
                    n_first = ahead(MOE[m]["R"] * st)
                if live(st, mid, n):
                    e_this = sp.value_load(slot_e[0:1, one(st)], min_val=0, max_val=MOE[m]["E"] - 1)
                if live(st + 2, mid, n):
                    need(sp, q["t_ps"], st + 1)
                    sp.dma_start(XS[:, u, :], sorted_rows[m].rearrange("(n p) d -> p n d", p=P)[:, one(st + 2), :]
                                 ).then_inc(q["xs"][u], 16)
                if live(st + 1, mid, n):
                    need(sp, q["hid" if m == 0 else "u"], n_first)
                    w = MOE[m]["W1"].shape[2]
                    sp.dma_start(W1[:, 1 - u, 0:w], MOE[m]["W1"][one(e_next), :, :]).then_inc(q["w1"][1 - u], 16)
                if live(st, mid, n):
                    need(sp, q["y_ps"], st - 1)
                    hc = MOE[m]["hid"] // P
                    sp.dma_start(W2[:, u, 0:hc, :], MOE[m]["W2"][one(e_this), :, :, :]).then_inc(q["w2"][u], 16)
                    sp.dma_start(b2[0:1, u, :], MOE[m]["b2"][one(e_this), :]).then_inc(q["w2"][u], 16)
                if live(st - 2, mid, n):
                    sp.wait_ge(q["y_sb"], st - 1)
                    sp.dma_start(expert_rows[m].rearrange("(n p) d -> p n d", p=P)[:, one(st - 2), :], YS[:, u, :]
                                 ).then_inc(q["y_out"][u], 16)

            def experts(m):
                q, n = ms[m], MOE[m]["n"]
                sp.wait_ge(q["pos"], 2)
                sp.wait_ge(q["scat"], 32 * NT)
                row_steps(sp, n, -2, lambda at: expert_step(m, at))
                sp.wait_ge(q["y_sb"], n)
                sp.dma_start(expert_rows[m].rearrange("(n p) d -> p n d", p=P)[:, n - 1:n, :], YS[:, (n - 1) % 2, :]
                             ).then_inc(q["y_out"][(n - 1) % 2], 16)

            for name in plan:
                k = int(name[1])
                if name[0] == "A":
                    steps(sp, k, lambda at: attention_step(k, at))
                    if k == 0:
                        later_loads()
                        zero_sorted_rows()
                else:
                    experts(k)
            if STOP is None or STOP == "M1":
                sp.wait_ge(fin["out"], 1)
                with sp.Fori(1, NT + 1) as t1:
                    sp.wait_ge(fin["out"], t1)
                    sp.dma_start(out[:, one(t1 - 1), :], X[:, one(t1 - 1), :]).then_inc(fin["dma"], 16)
                sp.wait_ge(fin["dma"], 16 * NT)
            else:
                k = int(STOP[1])
                sp.wait_ge(s["res"] if STOP[0] == "A" else ms[k]["comb"], n_before("res", k) + NT if STOP[0] == "A" else 2 * NT)
                sp.dma_start(out, X[:]).then_inc(s_dump, 16)
                sp.wait_ge(s_dump, 16)
                sp.wait_ge(s_load[1], 16 * len(wname[4:]))
                sp.wait_ge(s_load[2], 16 * len(MLP_LOADS))
                sp.wait_ge(s_zero_rows, 32)

        @block.gpsimd
        def _(pool):
            nc.gpsimd.memset(minus_half[:], -0.5).then_inc(s_clear, 1)
            nc.gpsimd.memset(zeros[:], 0.0).then_inc(s_clear, 1)
            nc.gpsimd.memset(VB[:], 0.0).then_inc(s_clear, 1)
            nc.gpsimd.memset(ones_sq[:], 1.0).then_inc(s_clear, 1)
            pool.wait_ge(s_clear, 4)

            def root(sem_in, sem_out, sems, base, t, par):
                need(pool, sems[sem_in], base + t + 1)
                nc.gpsimd.tensor_tensor(rstd[:, par, :], var[:, par, :], minus_half[:], ALU.pow).then_inc(sems[sem_out], 1)

            def attention_step(k, at):
                st, u, mid = at.st, at.u, at.mid
                tf, tc, ta, tb = tiles_of(k, st)
                if k == 3 and live(ta, mid):
                    wait(pool, "rope", 3, ta + 1)
                    nc.gpsimd.tensor_tensor(QK[:, u, :, :].rearrange("p a n -> p (a n)"), RT[:, 0, :], RT[:, 1, :],
                                            ALU.add).then_inc(s["qk_sb"], 1)
                if k == 2 and live(tc, mid):
                    wait(pool, "row", 2, tc + 1)
                if live(tf, mid):
                    root("var", "rstd", s, n_before("var", k), tf, u if k == 2 else 1 - u)
                if k == 2 and live(tc, mid):
                    nc.gpsimd.indirect_dma_start(
                        out=MEM[:, 1 - u, :], out_offset=None, in_=a["ctx_rows"],
                        in_offset=bass.IndirectOffsetOnAxis(ap=row[:, 1 - u:2 - u], axis=0)).then_inc(s["mem"][1 - u], 16)

            def route_step(m, at):
                st, u, mid = at.st, at.u, at.mid
                if live(st + 1, mid):
                    root("var", "rstd", ms[m], 0, st + 1, 1 - u)

            def moe(m):
                q = ms[m]
                token_steps(pool, lambda at: route_step(m, at), -1)
                pool.wait_ge(q["pos"], 2)
                pool.wait_ge(q["xna"], NT)
                pool.wait_ge(s_zero_rows, 32)
                for t in range(NT):
                    for c in range(2):
                        nc.gpsimd.indirect_dma_start(
                            out=sorted_rows[m], out_offset=bass.IndirectOffsetOnAxis(ap=pos[:, c, t:t + 1], axis=0),
                            in_=XNA[:, t, :], in_offset=None).then_inc(q["scat"], 16)
                for par in range(2):
                    pool.wait_ge(q["y_out"][par], 8 * MOE[m]["n"])
                for t in range(NT):
                    if t >= 2:
                        pool.wait_ge(q["mix"], 2 * (t - 1))
                    for c in range(2):
                        nc.gpsimd.indirect_dma_start(
                            out=GY[:, t % 2, c, :], out_offset=None, in_=expert_rows[m],
                            in_offset=bass.IndirectOffsetOnAxis(ap=pos[:, c, t:t + 1], axis=0)).then_inc(q["gy"][t % 2], 16)

            for name in plan:
                k = int(name[1])
                if name[0] == "A":
                    steps(pool, k, lambda at: attention_step(k, at))
                else:
                    moe(k)

        @block.scalar
        def _(act):
            act.wait_ge(s_load[0], 16 * 9)
            nc.scalar.activation(sign_cols[:], sign_cols[:], ACT.Sign).then_inc(s_sign, 1)
            nc.scalar.activation(sign_v[:], sign_v[:], ACT.Sign).then_inc(s_sign, 1)

            def move(out_, in_):
                return nc.scalar.copy(out_, in_)

            def attention_step(k, at):
                st, u, mid = at.st, at.u, at.mid
                tf, tc, ta, tb = tiles_of(k, st)
                tx, ux = (tc, 1 - u) if k == 2 else (ta, u)
                if live(tx, mid):
                    wait(act, "xt_ps", k, tx + 1)
                    dst = QK[:, ux, 0:2, :] if k == 1 else XT[:, ux, :, :]
                    move(dst, bank[0][:, 0:2 * P].rearrange("p (c n) -> p c n", c=2)).then_inc(s["xt_sb"], 1)
                if live(tb, mid):
                    wait(act, "pt_ps", k, tb + 1)
                    move(PT[:, 1 - u, :, :], bank[5][:].rearrange("p (g n) -> p g n", g=4)).then_inc(s["pt_sb"], 1)
                if k == 2 and live(tc, mid):
                    wait(act, "q_ps", 2, tc + 1)
                    move(QK[:, 1 - u, 0:2, :], bank[1][:, 0:2 * P].rearrange("p (c n) -> p c n", c=2)).then_inc(s["q_sb"], 1)
                if k == 2 and live(ta, mid):
                    wait(act, "mt_ps", 2, ta + 1)
                    move(CT[:, u, :, :], bank[0][:, 2 * P:4 * P].rearrange("p (c n) -> p c n", c=2)).then_inc(s["mt_sb"], 1)
                    wait(act, "k_ps", 2, ta + 1)
                    move(QK[:, u, 2:4, :], bank[1][:, 2 * P:4 * P].rearrange("p (c n) -> p c n", c=2)).then_inc(s["qk_sb"], 1)
                if k == 0 and live(ta, mid):
                    wait(act, "qk_ps", 0, ta + 1)
                    for i in range(4):
                        last = nc.scalar.activation(QK[:, u, i, :], bank[1][:, i * P:(i + 1) * P], ACT.Identity,
                                                    bias=qk_bias[:, i:i + 1])
                    last.then_inc(s["qk_sb"], 1)
                if live(ta, mid):
                    wait(act, "xn" if k == 1 else "v_ps", k, ta + 1)
                    wait_dma(act, "vd", k, at, -2)
                    if k == 1:
                        move(VS[:, u, :].rearrange("p (h g d) -> p h g d", h=4, g=4),
                             XN[:, u, :].rearrange("p (g h d) -> p h g d", g=4, h=4)).then_inc(s["v_sb"], 1)
                    else:
                        move(VS[:, u, :], bank[3][:, 0:D]).then_inc(s["v_sb"], 1)
                if k != 1 and live(tb, mid):
                    wait(act, "ot_ps", k, tb + 1)
                    move(OT[:], bank[7][:, 0:2 * P].rearrange("p (c n) -> p c n", c=2)).then_inc(s["ot_sb"], 1)
                if live(ta, mid):
                    if k == 1:
                        wait(act, "sc_ps", 1, ta + 1)
                        wait(act, "pt_ps", 1, ta - 1)
                        nc.scalar.activation(PR[:, u, :], bank[4][:], ACT.Sigmoid,
                                             scale=4.0 * HD ** -0.5).then_inc(s["prob"], 1)
                    else:
                        wait(act, "sub", k, ta + 1)
                        nc.scalar.activation(PR[:, u, :], PR[:, u, :], ACT.Exp, scale=HD ** -0.5).then_inc(s["prob"], 1)

            def route_step(m, at):
                st, u, mid = at.st, at.u, at.mid
                q = ms[m]
                if live(st, mid):
                    need(act, q["xt_ps"], st + 1)
                    src = bank[0][:, 0:2 * P].rearrange("p (c n) -> p c n", c=2)
                    move(XT[:, u, :, :], src).then_inc(q["xt_sb"], 1)
                    if m == 0:
                        move(XTA[:, :, span(st, P)], src).then_inc(q["xta"], 1)
                    move(XNA[:, one(st), :], XN[:, u, :]).then_inc(q["xna"], 1)

            def shared_group(g, first):
                for j in range(4):
                    need(act, sh["g_ps"], 4 * g + j + 1)
                    if not (first and j < 2):
                        act.wait_ge(sh["hid"], 4 * g + j - 1)
                    nc.scalar.activation(SG[:, j % 2, :], bank[4 + j % 2][:], ACT.Gelu,
                                         bias=bs1[:, 4 + j:5 + j]).then_inc(sh["gate"], 1)

            def expert_step(m, at):
                st, u, mid = at.st, at.u, at.mid
                q, n, R = ms[m], MOE[m]["n"], MOE[m]["R"]
                hc = 2 * R
                if live(st + 1, mid, n):
                    need(act, q["t_ps"], st + 2)
                    move(XT[:, 1 - u, :, :], bank[0][:, 0:2 * P].rearrange("p (c n) -> p c n", c=2)).then_inc(q["t_sb"], 1)
                if live(st, mid, n):
                    b1_at = C2 * 2 * MOE[m]["hid"]
                    for r in range(R):
                        par = (R * u + r) % 2
                        need(act, q["g_ps"], R * st + r + 1)
                        need(act, q["hid"] if m == 0 else q["u"], R * st + r - 1)
                        for i in range(2):
                            bias = W1[:, u, b1_at + hc + 2 * r + i:b1_at + hc + 2 * r + i + 1]
                            last = nc.scalar.activation(GS[:, par, i, :], bank[1 + par][:, i * P:(i + 1) * P],
                                                        ACT.Gelu if m == 0 else ACT.Identity, bias=bias)
                        last.then_inc(q["gate_sb"], 1)
                    if m == 1:
                        for r in range(R):
                            need(act, q["u"], R * st + r + 1)
                            nc.scalar.activation(HB[:, u, 2 * r:2 * r + 2, :], HB[:, u, 2 * r:2 * r + 2, :],
                                                 ACT.Silu).then_inc(q["hid"], 1)
                if live(st - 1, mid, n):
                    need(act, q["y_ps"], st)
                    need(act, q["y_out"][1 - u], 16 * (at.half(-3) + 1))
                    move(YS[:, 1 - u, :], bank[5 + (1 - u)][:, 0:D]).then_inc(q["y_sb"], 1)

            def final_step(at):
                st, u, mid = at.st, at.u, at.mid
                if live(st, mid):
                    need(act, fin["xt_ps"], st + 1)
                    move(XT[:, u, :, :], bank[0][:, 0:2 * P].rearrange("p (c n) -> p c n", c=2)).then_inc(fin["xt_sb"], 1)

            def moe(m):
                q = ms[m]
                token_steps(act, lambda at: route_step(m, at), 0)
                act.wait_ge(q["gate"], 1)
                if m == 0:
                    nc.scalar.activation(r16[2][:], r16[2][:], ACT.Exp).then_inc(q["gate_e"], 1)
                    act.preload_act_table(ACT.Gelu)
                    act.wait_ge(s_load[2], 16 * len(MLP_LOADS))
                    shared_group(0, True)
                    with act.Fori(1, 4) as g:
                        shared_group(g, False)
                else:
                    nc.scalar.activation(RB[:, :, 0:E1], RB[:, :, 0:E1], ACT.Exp).then_inc(q["gate_e"], 1)
                    act.preload_act_table(ACT.Silu)
                row_steps(act, MOE[m]["n"], -1, lambda at: expert_step(m, at))
                if m == 1:
                    token_steps(act, final_step)

            for name in plan:
                k = int(name[1])
                if name[0] == "A":
                    act.preload_act_table(ACT.Sigmoid if k == 1 else ACT.Exp)
                    steps(act, k, lambda at: attention_step(k, at))
                else:
                    moe(k)

        @block.vector
        def _(dve):
            nc.vector.memset(hold[:], 0.0).then_inc(s_prep, 1)
            nc.vector.memset(ones[:], 1.0).then_inc(s_prep, 1)
            dve.wait_ge(s_load[0], 16 * 9)
            nc.vector.tensor_copy(ident_bf[:], const("ident")).then_inc(s_prep, 1)
            nc.vector.tensor_copy(causal_bf[:], const("causal")).then_inc(s_prep, 1)
            dve.wait_ge(s_sign, 2)
            nc.vector.tensor_tensor(sign_qk[:], sign_cols[:, 0, :], sign_cols[:, 1, :], ALU.mult).then_inc(s_prep, 1)
            dve.wait_ge(s_prep, 5)
            nc.vector.tensor_tensor(sign_mask[:], const("head_mask").unsqueeze(1).to_broadcast([P, C2, HC]),
                                    sign_qk[:].unsqueeze(2).to_broadcast([P, C2, HC]), ALU.mult).then_inc(s_prep, 1)
            dve.wait_ge(s_prep, 6)

            def hold_until(sem, v):
                need(dve, sem, v)
                nc.vector.tensor_copy(hold[:], hold[:])

            def norm_stats(q, base, t, par):
                nc.vector.bn_stats(stats[:, par, :], X[:, one(t), :]).then_inc(q["stat"], 1)
                hold_until(q["stat"], base + t + 1)
                nc.vector.bn_aggr(mv[:, par, :], stats[:, par, :]).then_inc(q["mv"], 1)
                dve.wait_ge(q["mv"], base + t + 1)
                nc.vector.tensor_scalar(var[:, par, :], mv[:, par, 1:2], EPS, None, ALU.add).then_inc(q["var"], 1)

            def norm_apply(q, base, t, par):
                dve.wait_ge(q["rstd"], base + t + 1)
                nc.vector.tensor_scalar(XN[:, par, :], X[:, one(t), :], mv[:, par, 0:1], rstd[:, par, 0:1],
                                        ALU.subtract, ALU.mult).then_inc(q["xn"], 1)

            def attention_step(k, at):
                st, u, mid = at.st, at.u, at.mid
                tf, tc, ta, tb = tiles_of(k, st)
                uf = u if k == 2 else 1 - u
                if k == 3 and live(ta, mid):
                    wait(dve, "qk_ps", 3, ta + 1)
                    for i, (b_, tab) in enumerate(((1, "cos"), (2, "sin"))):
                        last = nc.vector.tensor_tensor(RT[:, i, :].rearrange("p (a t) -> p a t", t=T),
                                                       bank[b_][:].rearrange("p (a t) -> p a t", t=T),
                                                       const(tab).unsqueeze(1).to_broadcast([P, 4 * BT, T]), ALU.mult)
                    last.then_inc(s["rope"], 1)
                if live(ta, mid):
                    if k == 1:
                        wait(dve, "xt_sb", 1, ta + 1)
                    else:
                        wait(dve, "qk_sb", k, ta + 1)
                    for c in range(C2):
                        src = QK[:, u, c if k == 1 else 2 + c, :]
                        m_ = sign_mask[:, c, :] if k == 1 else const("head_mask")
                        last = nc.vector.tensor_tensor(KB[:, u, c, :, :], src.unsqueeze(1).to_broadcast([P, HC, P]),
                                                       m_.unsqueeze(2).to_broadcast([P, HC, P]), ALU.mult)
                    last.then_inc(s["kb"], 1)
                if live(tb, mid):
                    wait(dve, "o_ps", k, tb + 1)
                    if k == 1:
                        nc.vector.tensor_tensor(OS[:, 1 - u, :], bank[6][:, 0:D], sign_v[:], ALU.mult).then_inc(s["o_sb"], 1)
                        wait(dve, "o_sb", 1, tb + 1)
                        nc.vector.tensor_tensor(X[:, one(tb), :], X[:, one(tb), :], OS[:, 1 - u, :].unsqueeze(1),
                                                ALU.add).then_inc(s["res"], 1)
                    else:
                        nc.vector.reciprocal(rc[:], bank[6][:, D:D + H]).then_inc(s["rc"], 1)
                        wait(dve, "rc", k, tb + 1)
                        nc.vector.tensor_tensor(OS[:, 1 - u, :].rearrange("p (h d) -> p h d", h=H),
                                                bank[6][:, 0:D].rearrange("p (h d) -> p h d", h=H),
                                                rc[:].unsqueeze(2).to_broadcast([P, H, HD]), ALU.mult).then_inc(s["o_sb"], 1)
                if live(tf, mid):
                    if k == 0:
                        if not mid:
                            for q in ([0] if tf < 4 else range(4)):
                                dve.wait_ge(s_x[q], 16)
                    elif k == 2:
                        need(dve, ms[0]["comb"], 2 * (tf + 1))
                    else:
                        wait(dve, "res", k - 1, tf + 1)
                    norm_stats(s, n_before("stat", k), tf, uf)
                if k == 2 and live(tc, mid):
                    v = n_before("cs_ps", 2) + tc + 1
                    hold_until(s["cs_ps"], v)
                    nc.vector.max(top8[:], bank[2][:, 0:S]).then_inc(s["top"], 1)
                    hold_until(s["top"], v)
                    nc.vector.max_index(idx8[:], top8[:], bank[2][:, 0:S]).then_inc(s["idx"], 1)
                    dve.wait_ge(s["idx"], v)
                    wait_dma(dve, "mem", 2, at, -1)
                    nc.vector.tensor_tensor(row[:, 1 - u:2 - u], idx8[:, 0:1], const("row0")[:, one(tc)],
                                            ALU.add).then_inc(s["row"], 1)
                if k != 1 and live(ta, mid):
                    wait(dve, "sc_ps", k, ta + 1)
                    sc = bank[4][:].rearrange("p (h t) -> p h t", h=H)
                    nc.vector.tensor_reduce(mx[:], sc, AX.X, ALU.max).then_inc(s["mx"], 1)
                    wait(dve, "mx", k, ta + 1)
                    wait(dve, "pt_ps", k, ta - 1)
                    nc.vector.tensor_tensor(PR[:, u, :].rearrange("p (h t) -> p h t", h=H), sc,
                                            mx[:].unsqueeze(2).to_broadcast([P, H, T]), ALU.subtract).then_inc(s["sub"], 1)
                if live(tf, mid):
                    if k == 1:
                        wait(dve, "v_sb", 1, tf - 1)
                    norm_apply(s, n_before("stat", k), tf, uf)
                if k != 1 and live(tb, mid):
                    wait(dve, "y_ps", k, tb + 1)
                    nc.vector.tensor_tensor(X[:, one(tb), :], X[:, one(tb), :], bank[7][:, 2 * P:4 * P].unsqueeze(1),
                                            ALU.add).then_inc(s["res"], 1)

            def route_step(m, at):
                st, u, mid = at.st, at.u, at.mid
                q = ms[m]
                if live(st + 1, mid):
                    wait(dve, "res", 1 + 2 * m, st + 2)
                    norm_stats(q, 0, st + 1, 1 - u)
                    need(dve, q["xna"], st)
                    norm_apply(q, 0, st + 1, 1 - u)
                if live(st, mid):
                    need(dve, q["lg_ps"], st + 1)
                    nc.vector.tensor_copy(LG[:, one(st), 0:MOE[m]["E"]], bank[1][:, 0:MOE[m]["E"]].unsqueeze(1)
                                          ).then_inc(q["lg_sb"], 1)

            done = [0]

            def then(ins):
                done[0] += 1
                ins.then_inc(s_route_step, 1)
                dve.wait_ge(s_route_step, done[0])

            def pick(vals, rank, c, E, m_out):
                then(nc.vector.tensor_reduce(m_out[:], vals, AX.X, ALU.max))
                then(nc.vector.tensor_tensor(RC[:, :, 0:E], vals, m_out[:].unsqueeze(2).to_broadcast([P, NT, E]), ALU.is_equal))
                then(nc.vector.tensor_tensor(RC[:, :, 0:E], RC[:, :, 0:E], rank, ALU.mult))
                then(nc.vector.tensor_reduce(r16[3][:], RC[:, :, 0:E], AX.X, ALU.max))
                then(nc.vector.tensor_tensor(RM[:, c, :, 0:E], RC[:, :, 0:E],
                                             r16[3][:].unsqueeze(2).to_broadcast([P, NT, E]), ALU.is_equal))

            def route(m):
                q, E, n = ms[m], MOE[m]["E"], MOE[m]["n"]
                off = 0 if m == 0 else E0
                rank = const("ranks")[:, off:off + E].unsqueeze(1).to_broadcast([P, NT, E])
                L = LG[:, :, 0:E]
                V = RB[:, :, 0:E]
                dve.wait_ge(q["lg_sb"], NT)
                if m == 0:
                    then(nc.vector.tensor_scalar(V, L, 1.0 / TAU, None, ALU.mult))
                else:
                    then(nc.vector.tensor_reduce(r16[2][:], L, AX.X, ALU.max))
                    nc.vector.tensor_tensor(V, L, r16[2][:].unsqueeze(2).to_broadcast([P, NT, E]),
                                            ALU.subtract).then_inc(q["gate"], 1)
                    dve.wait_ge(q["gate_e"], 1)
                    then(nc.vector.tensor_reduce(r16[2][:], V, AX.X, ALU.add))
                    then(nc.vector.reciprocal(r16[2][:], r16[2][:]))
                    then(nc.vector.tensor_tensor(V, V, r16[2][:].unsqueeze(2).to_broadcast([P, NT, E]), ALU.mult))
                pick(V, rank, 0, E, r16[0])
                then(nc.vector.tensor_scalar(RA[:, :, 0:E], RM[:, 0, :, 0:E], NEG, None, ALU.mult))
                then(nc.vector.tensor_tensor(RA[:, :, 0:E], RA[:, :, 0:E], V, ALU.add))
                pick(RA[:, :, 0:E], rank, 1, E, r16[1])
                nc.vector.tensor_tensor(RC[:, :, 0:E], RM[:, 0, :, 0:E], RM[:, 1, :, 0:E], ALU.add).then_inc(q["onehot"], 1)
                if m == 0:
                    nc.vector.tensor_tensor(r16[2][:], r16[1][:], r16[0][:], ALU.subtract).then_inc(q["gate"], 1)
                    dve.wait_ge(q["gate_e"], 1)
                    then(nc.vector.tensor_scalar(r16[3][:], r16[2][:], 1.0, None, ALU.add))
                    then(nc.vector.reciprocal(wts[:, 0, :], r16[3][:]))
                    then(nc.vector.tensor_tensor(wts[:, 1, :], wts[:, 0, :], r16[2][:], ALU.mult))
                else:
                    then(nc.vector.tensor_copy(wts[:, 0, :], r16[0][:]))
                    then(nc.vector.tensor_copy(wts[:, 1, :], r16[1][:]))
                dve.wait_ge(q["rank_ps"], 1)
                within = bank[2][:, 0:NT * E].rearrange("p (t e) -> p t e", e=E)
                total = bank[3][:, 0:NT * E].rearrange("p (t e) -> p t e", e=E)
                O = RO[:, :, 0:E]
                then(nc.vector.memset(RO[:, 0:1, 0:E], 0.0))
                for t in range(1, NT):
                    then(nc.vector.tensor_tensor(RO[:, t:t + 1, 0:E], RO[:, t - 1:t, 0:E], total[:, t - 1:t, :], ALU.add))
                cnt, ends, base = (r[:, 0:E] for r in re_)
                then(nc.vector.tensor_tensor(cnt, RO[:, NT - 1, 0:E], total[:, NT - 1, :], ALU.add))
                then(nc.vector.tensor_scalar(rei[:, 0:E], cnt, float(P - 1), None, ALU.add))
                then(nc.vector.tensor_scalar(rei[:, 0:E], rei[:, 0:E], 7, None, ALU.arith_shift_right))
                then(nc.vector.tensor_copy(cnt, rei[:, 0:E]))
                tril = const("tril").rearrange("p (a b) -> p a b", a=E0)[:, 0:E, 0:E]
                then(nc.vector.tensor_tensor(RX[:, 0:E, 0:E], cnt.unsqueeze(1).to_broadcast([P, E, E]), tril, ALU.mult))
                then(nc.vector.tensor_reduce(ends, RX[:, 0:E, 0:E], AX.X, ALU.add))
                then(nc.vector.tensor_tensor(base, ends, cnt, ALU.subtract))
                then(nc.vector.tensor_scalar(base, base, float(P), None, ALU.mult))
                then(nc.vector.tensor_tensor(O, O, within, ALU.add))
                then(nc.vector.tensor_tensor(O, O, base.unsqueeze(1).to_broadcast([P, NT, E]), ALU.add))
                for c in range(2):
                    then(nc.vector.tensor_tensor(RC[:, :, 0:E], RM[:, c, :, 0:E], O, ALU.mult))
                    then(nc.vector.tensor_reduce(r16[3][:], RC[:, :, 0:E], AX.X, ALU.add))
                    last = nc.vector.tensor_copy(pos[:, c, :], r16[3][:])
                    if c == 0:
                        then(last)
                    else:
                        last.then_inc(q["pos"], 1)
                then(nc.vector.tensor_tensor(RE[:, 0:n, 0:E], ends.unsqueeze(1).to_broadcast([P, n, E]),
                                             const("slots")[:, 0:n].unsqueeze(2).to_broadcast([P, n, E]), ALU.is_le))
                then(nc.vector.tensor_reduce(rsl[:, 0:n], RE[:, 0:n, 0:E], AX.X, ALU.add))
                nc.vector.tensor_scalar(slot_e[0:1, 0:n], rsl[0:1, 0:n], float(E - 1), None, ALU.min).then_inc(q["pos"], 1)

            def shared_group(g):
                for j in range(4):
                    dve.wait_ge(sh["a_ps"], 4 * g + j + 1)
                    dve.wait_ge(sh["gate"], 4 * g + j + 1)
                    nc.vector.scalar_tensor_tensor(out=SH[:, j, :], in0=bank[2 + j % 2][:], scalar=bs1[:, j:j + 1],
                                                   in1=SG[:, j % 2, :], op0=ALU.add, op1=ALU.mult).then_inc(sh["hid"], 1)
                for t in range(4):
                    dve.wait_ge(sh["y_ps"], 4 * g + t + 1)
                    nc.vector.tensor_tensor(X[:, one(4 * g + t), :], X[:, one(4 * g + t), :],
                                            bank[6 + t % 2][:, 0:D].unsqueeze(1), ALU.add).then_inc(sh["res"], 1)

            def expert_step(m, at):
                st, u, mid = at.st, at.u, at.mid
                q, n, R = ms[m], MOE[m]["n"], MOE[m]["R"]
                if live(st, mid, n):
                    b1_at = C2 * 2 * MOE[m]["hid"]
                    for r in range(R):
                        par = (R * u + r) % 2
                        need(dve, q["a_ps"], R * st + r + 1)
                        need(dve, q["gate_sb"], R * st + r + 1)
                        for i in range(2):
                            bias = W1[:, u, b1_at + 2 * r + i:b1_at + 2 * r + i + 1]
                            last = nc.vector.scalar_tensor_tensor(
                                out=HB[:, u, 2 * r + i, :], in0=bank[3 + par][:, i * P:(i + 1) * P], scalar=bias,
                                in1=GS[:, par, i, :], op0=ALU.add, op1=ALU.mult)
                        last.then_inc(q["hid"] if m == 0 else q["u"], 1)

            def combine(t, u, half):
                q = ms[0]
                dve.wait_ge(q["gy"][u], 32 * (half + 1))
                nc.vector.scalar_tensor_tensor(out=X[:, one(t), :], in0=GY[:, u, 0:1, :], scalar=wts[:, 0, one(t)],
                                               in1=X[:, one(t), :], op0=ALU.mult, op1=ALU.add).then_inc(q["mix"], 1)
                dve.wait_ge(q["mix"], 2 * t + 1)
                nc.vector.scalar_tensor_tensor(out=X[:, one(t), :], in0=GY[:, u, 1:2, :], scalar=wts[:, 1, one(t)],
                                               in1=X[:, one(t), :], op0=ALU.mult, op1=ALU.add).then_inc(q["mix"], 1)
                dve.wait_ge(q["mix"], 2 * t + 2)
                nc.vector.tensor_copy(hold[:], hold[:]).then_inc(q["comb"], 2)

            def final_step(at):
                st, u, mid = at.st, at.u, at.mid
                q = ms[1]
                if live(st, mid):
                    dve.wait_ge(q["gy"][u], 32 * (at.half(0) + 1))
                    need(dve, fin["xt_ps"], st - 1)
                    nc.vector.tensor_scalar(XN[:, u, :], GY[:, u, 0, :], wts[:, 0, one(st)], None, ALU.mult
                                            ).then_inc(q["mix"], 1)
                    dve.wait_ge(q["mix"], 2 * st + 1)
                    nc.vector.scalar_tensor_tensor(out=XN[:, u, :], in0=GY[:, u, 1, :], scalar=wts[:, 1, one(st)],
                                                   in1=XN[:, u, :], op0=ALU.mult, op1=ALU.add).then_inc(q["mix"], 1)
                if live(st - 1, mid):
                    need(dve, fin["y_ps"], st)
                    nc.vector.tensor_tensor(X[:, one(st - 1), :], X[:, one(st - 1), :], bank[1][:, 0:D].unsqueeze(1),
                                            ALU.add).then_inc(fin["out"], 1)

            def moe(m):
                token_steps(dve, lambda at: route_step(m, at), -1)
                route(m)
                if m == 0:
                    dve.wait_ge(s_load[2], 16 * len(MLP_LOADS))
                    shared_group(0)
                    with dve.Fori(1, 4) as g:
                        shared_group(g)
                row_steps(dve, MOE[m]["n"], 0, lambda at: expert_step(m, at))
                if m == 0:
                    dve.wait_ge(sh["res"], NT)
                    with dve.Fori(0, NT // 2) as j:
                        for u in range(2):
                            combine(2 * j + u, u, j)
                else:
                    token_steps(dve, final_step, 0, NT + 1)

            for name in plan:
                k = int(name[1])
                if name[0] == "A":
                    steps(dve, k, lambda at: attention_step(k, at))
                else:
                    moe(k)

        @block.tensor
        def _(pe):
            mm = nc.tensor.matmul
            pe.wait_ge(s_load[0], 16 * 9)
            pe.wait_ge(s_prep, 6)
            pe.wait_ge(s_clear, 4)
            ident = const("ident")

            def transpose_tile(dst, src):
                for c in range(C2):
                    last = nc.tensor.transpose(dst[:, c * P:(c + 1) * P], src[:, c * P:(c + 1) * P], ident)
                return last

            def project(dst, w, src):
                for j in range(C2):
                    for c in range(C2):
                        last = mm(dst[:, j * P:(j + 1) * P], w[:, c, j * P:(j + 1) * P], src[:, c, :],
                                  start=(c == 0), stop=(c == C2 - 1))
                return last

            def project_rows(dst, w, src, bias=None, n=D):
                for c in range(C2):
                    last = mm(dst, src[:, c, :], w[:, c, 0:n], start=(c == 0), stop=(c == C2 - 1 and bias is None))
                if bias is not None:
                    last = mm(dst, ones[:], bias, start=False, stop=True)
                return last

            def scores(k, u, c):
                masked = k != 2
                if masked and c == 0:
                    mm(bank[4][:], ident_bf[:], causal_bf[:], start=True, stop=False, skip_group_check=True)
                for b in range(BT):
                    last = mm(bank[4][32 * b:32 * b + 32, c * HC * T:(c + 1) * HC * T], QK[:, u, c, 32 * b:32 * b + 32],
                              KB[:, u, c, :, 32 * b:32 * b + 32], start=not masked, stop=True, skip_group_check=True)
                return last

            def attention_step(k, at):
                st, u, mid = at.st, at.u, at.mid
                tf, tc, ta, tb = tiles_of(k, st)
                tx, ux = (tc, 1 - u) if k == 2 else (ta, u)
                if live(tx, mid):
                    wait(pe, "xn", k, tx + 1)
                    wait(pe, "xt_sb", k, tx)
                    if k == 2:
                        wait(pe, "mt_sb", 2, tx - 1)
                    transpose_tile(bank[0][:, 0:2 * P], XN[:, ux, :]).then_inc(s["xt_ps"], 1)
                if live(tb, mid):
                    wait(pe, "prob", k, tb + 1)
                    wait(pe, "pt_sb", k, tb)
                    for g in range(4):
                        last = nc.tensor.transpose(bank[5][:, g * P:(g + 1) * P], PR[:, 1 - u, g * P:(g + 1) * P], ident)
                    last.then_inc(s["pt_ps"], 1)
                if k == 2 and live(tc, mid):
                    wait(pe, "xt_sb", 2, tc + 1)
                    project(bank[1][:, 0:2 * P], W["Wq2"], XT[:, 1 - u, :, :]).then_inc(s["q_ps"], 1)
                if k == 2 and live(ta, mid):
                    wait_dma(pe, "mem", 2, at, 0)
                    wait(pe, "xt_sb", 2, min(ta + 2, NT) if not mid else ta + 2)
                    transpose_tile(bank[0][:, 2 * P:4 * P], MEM[:, u, :]).then_inc(s["mt_ps"], 1)
                if k == 0 and live(ta, mid):
                    wait(pe, "xt_sb", 0, ta + 1)
                    wait_dma(pe, "ctx", 0, at, 0)
                    project(bank[1][:, 0:2 * P], W["Wq0"], XT[:, u, :, :])
                    project(bank[1][:, 2 * P:4 * P], W["Wk0"], CT[:, u, :, :]).then_inc(s["qk_ps"], 1)
                if k == 3 and live(ta, mid):
                    wait(pe, "xt_sb", 3, ta + 1)
                    wait(pe, "rope", 3, ta)
                    project(bank[1][:, 0:2 * P], W["Wq3"], XT[:, u, :, :])
                    project(bank[1][:, 2 * P:4 * P], W["Wk3"], XT[:, u, :, :])
                    project(bank[2][:, 0:2 * P], W["Wqs3"], XT[:, u, :, :])
                    project(bank[2][:, 2 * P:4 * P], W["Wks3"], XT[:, u, :, :]).then_inc(s["qk_ps"], 1)
                if k in (0, 3) and live(ta, mid):
                    wait(pe, "v_sb", k, ta)
                    if k == 0:
                        project_rows(bank[3][:, 0:D], W["Wv0"], CT[:, u, :, :], rows0[:, 0, :]).then_inc(s["v_ps"], 1)
                    else:
                        project_rows(bank[3][:, 0:D], W["Wv3"], XT[:, u, :, :]).then_inc(s["v_ps"], 1)
                if live(tb, mid):
                    wait(pe, "pt_sb", k, tb + 1)
                    wait_dma(pe, "vb", k, at, -1)
                    wait(pe, "o_sb", k, tb)
                    for g in range(4):
                        for b in range(BT):
                            last = mm(bank[6][32 * b:32 * b + 32, g * 64:(g + 1) * 64], PT[:, 1 - u, g, 32 * b:32 * b + 32],
                                      VB[:, 1 - u, b, :, g * HD:(g + 1) * HD], start=True, stop=True,
                                      skip_group_check=True)
                    if k != 1:
                        for g in range(4):
                            last = mm(bank[6][:, D + 4 * g:D + 4 * g + 4], PT[:, 1 - u, g, :], const("block_ones"),
                                      start=True, stop=True, skip_group_check=True)
                    last.then_inc(s["o_ps"], 1)
                if k == 2 and live(tc, mid):
                    wait(pe, "q_sb", 2, tc + 1)
                    wait_dma(pe, "cxt", 2, at, 1)
                    wait(pe, "idx", 2, tc)
                    for c in range(C2):
                        for b in range(BT):
                            last = mm(bank[2][32 * b:32 * b + 32, 0:S], QK[:, 1 - u, c, 32 * b:32 * b + 32],
                                      CXT[:, 1 - u, c, b, :], start=(c == 0), stop=(c == 1), skip_group_check=True)
                    last.then_inc(s["cs_ps"], 1)
                if k == 2 and live(ta, mid):
                    wait(pe, "mt_sb", 2, ta + 1)
                    wait(pe, "q_sb", 2, min(ta + 2, NT) if not mid else ta + 2)
                    project(bank[1][:, 2 * P:4 * P], W["Wk2"], CT[:, u, :, :]).then_inc(s["k_ps"], 1)
                    wait(pe, "v_sb", 2, ta)
                    project_rows(bank[3][:, 0:D], W["Wv2"], CT[:, u, :, :]).then_inc(s["v_ps"], 1)
                if live(ta, mid):
                    wait(pe, "kb", k, ta + 1)
                    scores(k, u, 0)
                if k != 1 and live(tb, mid):
                    wait(pe, "o_sb", k, tb + 1)
                    wait(pe, "res", k, tb)
                    transpose_tile(bank[7][:, 0:2 * P], OS[:, 1 - u, :]).then_inc(s["ot_ps"], 1)
                if live(ta, mid):
                    scores(k, u, 1).then_inc(s["sc_ps"], 1)
                if k != 1 and live(tb, mid):
                    wait(pe, "ot_sb", k, tb + 1)
                    project_rows(bank[7][:, 2 * P:4 * P], W[f"Wo{k}"], OT[:],
                                 rows0[:, 1, :] if k == 0 else None).then_inc(s["y_ps"], 1)

            def route_step(m, at):
                st, u, mid = at.st, at.u, at.mid
                q = ms[m]
                if live(st, mid):
                    need(pe, q["xn"], st + 1)
                    need(pe, q["xta"] if m == 0 else q["xt_sb"], st)
                    transpose_tile(bank[0][:, 0:2 * P], XN[:, u, :]).then_inc(q["xt_ps"], 1)
                    need(pe, q["xt_sb"], st + 1)
                    need(pe, q["lg_sb"], st)
                    project_rows(bank[1][:, 0:MOE[m]["E"]], Wr[m], XT[:, u, :, :], br[m][:], MOE[m]["E"]
                                 ).then_inc(q["lg_ps"], 1)

            def shared_group(g, first):
                pe.wait_ge(ms[0]["xta"], 4 * g + 4)
                for j in range(4):
                    if not (first and j < 2):
                        pe.wait_ge(sh["gate"], 4 * g + j - 1)
                    for c in range(C2):
                        last = mm(bank[4 + j % 2][:], Ws1[:, c, HS + j * P:HS + (j + 1) * P], XTA[:, c, span(g, 512)],
                                  start=(c == 0), stop=(c == 1))
                    last.then_inc(sh["g_ps"], 1)
                    if not (first and j < 2):
                        pe.wait_ge(sh["hid"], 4 * g + j - 1)
                    for c in range(C2):
                        last = mm(bank[2 + j % 2][:], Ws1[:, c, j * P:(j + 1) * P], XTA[:, c, span(g, 512)],
                                  start=(c == 0), stop=(c == 1))
                    last.then_inc(sh["a_ps"], 1)
                pe.wait_ge(sh["hid"], 4 * g + 4)
                for t in range(4):
                    if not (first and t < 2):
                        pe.wait_ge(sh["res"], 4 * g + t - 1)
                    dst = bank[6 + t % 2][:, 0:D]
                    for j in range(4):
                        mm(dst, SH[:, j, t * P:(t + 1) * P], Ws2[:, j, :], start=(j == 0), stop=False)
                    mm(dst, ones[:], bs2[:], start=False, stop=True).then_inc(sh["y_ps"], 1)

            def expert_step(m, at):
                st, u, mid = at.st, at.u, at.mid
                q, n, R, hid = ms[m], MOE[m]["n"], MOE[m]["R"], MOE[m]["hid"]
                if live(st + 1, mid, n):
                    pe.wait_ge(q["xs"][1 - u], 16 * (at.half(1) + 1))
                    need(pe, q["t_sb"], st + 1)
                    transpose_tile(bank[0][:, 0:2 * P], XS[:, 1 - u, :]).then_inc(q["t_ps"], 1)
                if live(st, mid, n):
                    pe.wait_ge(q["w1"][u], 16 * (at.half(0) + 1))
                    need(pe, q["t_sb"], st + 1)
                    for r in range(R):
                        par = (R * u + r) % 2
                        for half, bk, freed, sem in ((1, 1 + par, "gate_sb", "g_ps"),
                                                     (0, 3 + par, "hid" if m == 0 else "u", "a_ps")):
                            need(pe, q[freed], R * st + r - 1)
                            for i in range(2):
                                for c in range(C2):
                                    col = c * 2 * hid + half * hid + (2 * r + i) * P
                                    last = mm(bank[bk][:, i * P:(i + 1) * P], W1[:, u, col:col + P], XT[:, u, c, :],
                                              start=(c == 0), stop=(c == 1))
                            last.then_inc(q[sem], 1)
                if live(st - 1, mid, n):
                    pe.wait_ge(q["w2"][1 - u], 32 * (at.half(-1) + 1))
                    need(pe, q["hid"], R * st)
                    need(pe, q["y_sb"], st - 2)
                    dst = bank[5 + (1 - u)][:, 0:D]
                    for j in range(2 * R):
                        mm(dst, HB[:, 1 - u, j, :], W2[:, 1 - u, j, :], start=(j == 0), stop=False)
                    mm(dst, ones[:], b2[0:1, 1 - u, :], start=False, stop=True).then_inc(q["y_ps"], 1)

            def final_step(at):
                st, u, mid = at.st, at.u, at.mid
                if live(st, mid):
                    need(pe, ms[1]["mix"], 2 * (st + 1))
                    need(pe, fin["xt_sb"], st)
                    transpose_tile(bank[0][:, 0:2 * P], XN[:, u, :]).then_inc(fin["xt_ps"], 1)
                    need(pe, fin["xt_sb"], st + 1)
                    need(pe, fin["out"], st)
                    project_rows(bank[1][:, 0:D], Wf, XT[:, u, :, :], bf[:]).then_inc(fin["y_ps"], 1)

            def moe(m):
                q, E = ms[m], MOE[m]["E"]
                pe.wait_ge(s_load[2], 16 * len(MLP_LOADS))
                token_steps(pe, lambda at: route_step(m, at))
                pe.wait_ge(q["onehot"], 1)
                mm(bank[2][:, 0:NT * E], const("before"), RC[:, :, 0:E], start=True, stop=True)
                mm(bank[3][:, 0:NT * E], ones_sq[:], RC[:, :, 0:E], start=True, stop=True).then_inc(q["rank_ps"], 1)
                if m == 0:
                    pe.wait_ge(q["pos"], 2)
                    shared_group(0, True)
                    with pe.Fori(1, 4) as g:
                        shared_group(g, False)
                row_steps(pe, MOE[m]["n"], -1, lambda at: expert_step(m, at))
                if m == 1:
                    token_steps(pe, final_step)

            for name in plan:
                k = int(name[1])
                if name[0] == "A":
                    if k >= 2:
                        pe.wait_ge(s_load[1], 16 * len(wname[4:]))
                    steps(pe, k, lambda at: attention_step(k, at))
                else:
                    moe(k)

    return nc


def kernel(**inputs):
    import concourse.bacc as bacc
    from concourse.bass_utils import run_bass_kernel_spmd as run

    g = {k: np.asarray(v) for k, v in inputs.items()}

    def chunks(w):
        return w.reshape(-1, P, w.shape[-1]).transpose(1, 0, 2)

    ctx = g["ctx_1024"]
    swap = np.arange(D) ^ 1
    v_order = np.arange(D).reshape(4, 4, HD).transpose(1, 0, 2).reshape(-1)
    kv = g["L1_xattn_Wkv"]
    arrays = {
        "cst": CONST,
        "x": g["x"].reshape(NT, P, D).transpose(1, 0, 2),
        "ctx32": ctx[:, :T, :].reshape(NT, P, C2, P).transpose(3, 0, 2, 1),
        "ctxT": ctx.reshape(NT, BT, S, C2, P).transpose(4, 0, 3, 1, 2),
        "ctx_rows": ctx.reshape(B * S, D),
        "Wq0": chunks(g["L0_xattn_Wq"]), "Wk0": chunks(g["L0_xattn_Wk"]), "Wv0": chunks(g["L0_xattn_Wv"][:, v_order]),
        "Wo0": chunks(g["L0_xattn_Wo"]),
        "qk_bias": np.concatenate([g["L0_xattn_bq"].reshape(C2, P), g["L0_xattn_bk"].reshape(C2, P)]).T,
        "rows0": np.stack([g["L0_xattn_bv"][v_order], g["L0_xattn_bo"]])[None],
        "sign_cols": np.stack([g["L0_attn_bv_q"].reshape(C2, P), g["L0_attn_bv_k"].reshape(C2, P)]).transpose(2, 0, 1),
        "sign_v": g["L0_attn_bv_v"].reshape(1, D),
        "Wq2": chunks(g["L1_xattn_Wq"].T), "Wk2": chunks(np.tile(kv[:HD].T, (1, H))),
        "Wv2": chunks(np.tile(kv[HD:].T, (1, H))), "Wo2": chunks(g["L1_xattn_Wc"].T),
        "Wq3": chunks(g["L1_attn_Wq"]), "Wk3": chunks(g["L1_attn_Wk"]),
        "Wqs3": chunks(g["L1_attn_Wq"][:, swap]), "Wks3": chunks(g["L1_attn_Wk"][:, swap]),
        "Wv3": chunks(g["L1_attn_Wv"][:, v_order]), "Wo3": chunks(g["L1_attn_Wo"]),
        "Wr0": chunks(g["L0_ffn_Wr"]), "br0": g["L0_ffn_br"][None], "Wr1": chunks(g["L1_ffn_Wg"]), "br1": g["L1_ffn_bg"][None],
        "Ws1": chunks(g["L0_ffn_Ws1"]), "Ws2": chunks(g["L0_ffn_Ws2"]), "bs1": g["L0_ffn_bs1"].reshape(-1, P).T,
        "bs2": g["L0_ffn_bs2"][None],
        "Wf": chunks(g["L1_ffn_Wf"]), "bf": g["L1_ffn_bf"][None],
    }

    def expert_weights(first, bias):
        e, _, n = first.shape
        w = first.reshape(e, C2, P, n).transpose(0, 2, 1, 3).reshape(e, P, C2 * n)
        return np.concatenate([w, bias.reshape(e, n // P, P).transpose(0, 2, 1)], axis=2)

    arrays["W1_0"] = expert_weights(g["L0_ffn_We1"], g["L0_ffn_be1"])
    arrays["W1_1"] = expert_weights(np.concatenate([g["L1_ffn_W3"], g["L1_ffn_W1"]], axis=2),
                                    np.concatenate([g["L1_ffn_b3"], g["L1_ffn_b1"]], axis=1))
    for m, w in enumerate((g["L0_ffn_We2"], g["L1_ffn_W2"])):
        arrays[f"W2_{m}"] = w.reshape(w.shape[0], -1, P, D).transpose(0, 2, 1, 3)
    arrays["b2_0"], arrays["b2_1"] = g["L0_ffn_be2"], g["L1_ffn_b2"]

    nc = bacc.Bacc("TRN2", target_bir_lowering=False, num_devices=1)
    arrays = {k: np.ascontiguousarray(v) for k, v in arrays.items()}
    aps = {k: nc.dram_tensor(f"in_{k}", v.shape, mybir.dt.from_np(v.dtype), kind="ExternalInput").ap()
           for k, v in arrays.items()}
    out = nc.dram_tensor("out", (P, NT, D), F32, kind="ExternalOutput").ap()
    build(nc, aps, out)
    r = run(nc, [{f"in_{k}": v for k, v in arrays.items()}], core_ids=[0])
    return r.results[0]["out"].transpose(1, 0, 2).reshape(B, T, D)
```

```python
from contextlib import ExitStack

import numpy as np
import concourse.bass as bass
from concourse import mybir

F32 = mybir.dt.float32
BF16 = mybir.dt.bfloat16
I32 = mybir.dt.int32
U32 = mybir.dt.uint32
ALU = mybir.AluOpType
ACT = mybir.ActivationFunctionType
AX = mybir.AxisListType

B, T, D = 64, 32, 256
S = 257
H, HD = 16, 16
P = 128
NT = B * T // P
BT = P // T
C2 = D // P
HC = P // HD
EPS = 1e-5
NEG = -1e30
E0, HR, HS = 12, 768, 512
E1, HX = 8, 512
PAIRS = 2 * B * T
M0_TILES = PAIRS // P + E0
M1_TILES = PAIRS // P + E1
TAU = 1.5
STOP = None


def constants():
    p = np.arange(P)
    ident = np.eye(P, dtype=np.float32)
    head_mask = (p[:, None] // HD == np.arange(HC)[None, :]).astype(np.float32)
    block_ones = (p[:, None] // T == np.arange(BT)[None, :]).astype(np.float32)
    key, tok = np.arange(T)[None, :], (p % T)[:, None]
    causal = np.tile(np.where(key <= tok, 0.0, NEG).astype(np.float32), (1, H))
    before = (p[:, None] < p[None, :]).astype(np.float32)
    dd = p % HD
    inv = (np.float32(1.0) / np.float32(10000.0) ** (np.arange(0, HD, 2, dtype=np.float32) / np.float32(HD))).astype(np.float32)
    ang = np.arange(T, dtype=np.float32)[None, :] * inv[dd // 2][:, None]
    cos = np.cos(ang).astype(np.float32)
    sin = (np.sin(ang) * np.where(dd % 2 == 0, -1.0, 1.0)[:, None]).astype(np.float32)
    row0 = ((np.arange(NT)[None, :] * BT + (p // T)[:, None]) * S).astype(np.float32)
    experts = np.zeros((P, E0, E0), np.float32)
    experts[:] = np.tril(np.ones((E0, E0), np.float32))[None]
    ranks = np.broadcast_to(np.concatenate([E0 - np.arange(E0), 1.0 + np.arange(E1)]).astype(np.float32), (P, E0 + E1))
    slots = np.broadcast_to(np.arange(M0_TILES, dtype=np.float32), (P, M0_TILES))
    cols = [("ident", ident), ("head_mask", head_mask), ("block_ones", block_ones), ("causal", causal),
            ("before", before), ("cos", cos), ("sin", sin), ("row0", row0), ("tril", experts.reshape(P, -1)),
            ("ranks", ranks), ("slots", slots)]
    at, where = 0, {}
    for name, a in cols:
        where[name] = (at, at + a.shape[1])
        at += a.shape[1]
    return np.ascontiguousarray(np.concatenate([a for _, a in cols], axis=1)), where


CONST, WHERE = constants()

ATTN = (0, 1, 2, 3)
USES = {
    "stat": ATTN, "mv": ATTN, "var": ATTN, "rstd": ATTN, "xn": ATTN, "xt_ps": ATTN, "xt_sb": ATTN,
    "ctx": (0,), "bias": (0,), "qk_ps": (0, 3), "q_ps": (2,), "q_sb": (2,), "k_ps": (2,), "qk_sb": (0, 2, 3), "rope": (3,),
    "v_ps": (0, 2, 3), "v_sb": ATTN, "vb": ATTN, "kb": ATTN, "kb1": ATTN, "sc_ps": ATTN, "mx": (0, 2, 3), "sub": (0, 2, 3),
    "prob": ATTN, "pt_ps": ATTN, "pt_sb": ATTN, "o_ps": ATTN, "rc": (0, 2, 3), "o_sb": ATTN,
    "ot_ps": (0, 2, 3), "ot_sb": (0, 2, 3), "y_ps": (0, 2, 3), "res": ATTN, "vd": ATTN,
    "cxt": (2,), "cs_ps": (2,), "top": (2,), "idx": (2,), "row": (2,), "mem": (2,), "mt_ps": (2,), "mt_sb": (2,),
}
PER = {"ctx": 16, "cxt": 16, "vd": 16, "vb": 64, "mem": 16}
LOOP_FROM = 4


def build(nc, a, out):
    ctx = ExitStack()
    with ctx:
        def sb(name, shape, dt=F32):
            return ctx.enter_context(nc.sbuf_tensor(name, shape, dt))

        def psum(name, shape, dt=F32):
            return ctx.enter_context(nc.psum_tensor(name, shape, dt))

        def new_sem(name):
            return ctx.enter_context(nc.semaphore(name))

        sorted_rows = [nc.dram_tensor(f"sorted_rows{m}", (n * P, D), F32).ap() for m, n in enumerate((M0_TILES, M1_TILES))]
        expert_rows = [nc.dram_tensor(f"expert_rows{m}", (n * P, D), F32).ap() for m, n in enumerate((M0_TILES, M1_TILES))]

        v_rows = nc.dram_tensor("v_rows", (2, P, D), F32).ap()

        cst = sb("cst", [P, CONST.shape[1]])

        def const(name, parts=P):
            lo, hi = WHERE[name]
            return cst[0:parts, lo:hi]

        X = sb("X", [P, NT, D])
        XN = sb("XN", [P, 2, D])
        XT = sb("XT", [P, 2, C2, P])
        QK = sb("QK", [P, 2, 4, P])
        KB = sb("KB", [P, 2, C2, HC, P])
        VS = sb("VS", [P, 2, D])
        VB = sb("VB", [P, 2, BT, 4, 64])
        PR = sb("PR", [P, 2, H * T])
        PT = sb("PT", [P, 2, 4, P])
        OS = sb("OS", [P, 2, D])
        OT = sb("OT", [P, C2, P])
        CT = sb("CT", [P, 2, C2, P])
        CXT = sb("CXT", [P, 2, C2, BT, S])
        MEM = sb("MEM", [P, 2, D])
        RT = sb("RT", [P, 2, 4 * P])
        stats = sb("stats", [P, 2, 6])
        mv = sb("mv", [P, 2, 2])
        var = sb("var", [P, 2, 1])
        rstd = sb("rstd", [P, 2, 1])
        minus_half = sb("minus_half", [P, 1])
        mx = sb("mx", [P, H])
        rc = sb("rc", [P, H])
        hold = sb("hold", [P, 1])
        stats_all = sb("stats_all", [P, NT, 6])
        mv_all = sb("mv_all", [P, NT, 2])
        var_all = sb("var_all", [P, NT])
        rstd_all = sb("rstd_all", [P, NT])
        top8 = sb("top8", [P, 8])
        idx8 = sb("idx8", [P, 8], U32)
        idxf = sb("idxf", [P, 1])
        row = sb("row", [P, 2], I32)
        ones = sb("ones", [1, P])
        ident_bf = sb("ident_bf", [P, P], BF16)
        causal_bf = sb("causal_bf", [P, H * T], BF16)
        sign_cols = sb("sign_cols", [P, 2, C2])
        sign_qk = sb("sign_qk", [P, C2])
        sign_mask = sb("sign_mask", [P, C2, HC])
        sign_v = sb("sign_v", [P, D])
        wname = ["Wq0", "Wk0", "Wv0", "Wo0", "Wq2", "Wk2", "Wv2", "Wo2", "Wq3", "Wk3", "Wqs3", "Wks3", "Wv3", "Wo3"]
        first_w = sb("first_w", [P, 4, C2, D])
        W = {n: first_w[:, i] for i, n in enumerate(wname[:4])} | {n: sb(n, [P, C2, D])[:] for n in wname[4:]}
        qk_bias = sb("qk_bias", [P, 4])
        rows0 = sb("rows0", [P, 2, D])
        XNA = sb("XNA", [P, NT, D])
        LG = sb("LG", [P, NT, E0])
        Wr = [sb(f"Wr{m}", [P, C2, e]) for m, e in enumerate((E0, E1))]
        br = [sb(f"br{m}", [1, e]) for m, e in enumerate((E0, E1))]
        wts = sb("wts", [P, 2, NT])
        pos = sb("pos", [P, 2, NT], I32)
        slot_e = sb("slot_e", [1, M0_TILES], I32)
        zeros = sb("zeros", [P, D])
        W1F, W1X = C2 * 2 * HR + 2 * HR // P, C2 * 2 * HX + 2 * HX // P
        W1 = sb("W1", [P, 2, max(W1F, W1X)])
        W2 = sb("W2", [P, 2, HR // P * D])
        b2 = sb("b2", [P, 2, D])
        XS = sb("XS", [P, 2, D])
        GS = sb("GS", [P, 2, 2, P])
        HB = sb("HB", [P, 2, HR // P, P])
        YS = sb("YS", [P, 2, D])
        GY = sb("GY", [P, 2, 2, D])
        Wf = sb("Wf", [P, C2, D])
        bf = sb("bf", [P, D])
        XTA = CXT[:].rearrange("p a c b s -> p (a c b s)")[:, 0:C2 * NT * P].rearrange("p (c n) -> p c n", c=C2)
        Ws1 = first_w[:].rearrange("p i c n -> p (i c n)").rearrange("p (c n) -> p c n", c=C2)
        Ws2 = sb("Ws2", [P, HS // P, D])
        bs1 = sb("bs1", [P, 2 * HS // P])
        bs2 = sb("bs2", [P, D])
        kb_flat = KB[:].rearrange("p a c h n -> p (a c h n)")
        SG = kb_flat[:, 0:1024].rearrange("p (a n) -> p a n", a=2)
        SH = kb_flat[:, 1024:1024 + 4 * HS].rearrange("p (a n) -> p a n", n=512)
        pt_flat, pr_flat = PT[:].rearrange("p a g n -> p (a g n)"), PR[:].rearrange("p a n -> p (a n)")

        def scratch(buf, at, n, e):
            return buf[:, at:at + n * e].rearrange("p (n e) -> p n e", e=e)

        RA, RB, RO = (scratch(pt_flat, i * NT * E0, NT, E0) for i in range(3))
        RX = scratch(pt_flat, 3 * NT * E0, E0, E0)
        RE = scratch(pr_flat, 0, M0_TILES, E0)
        RM = sb("RM", [P, 2, NT, E0])
        RC = sb("RC", [P, NT, E0])
        r16 = [sb(f"r16_{i}", [P, NT]) for i in range(4)]
        re_ = [sb(f"re_{i}", [P, E0]) for i in range(3)]
        rei = sb("rei", [P, E0], I32)
        rsl = sb("rsl", [P, M0_TILES])

        ones_sq = sb("ones_sq", [P, P])
        MLP_LOADS = ((Wr[0][:], "Wr0"), (br[0][:], "br0"), (Wr[1][:], "Wr1"), (br[1][:], "br1"), (Ws1, "Ws1"), (Ws2[:], "Ws2"),
                     (bs1[:], "bs1"), (bs2[:], "bs2"), (Wf[:], "Wf"), (bf[:], "bf"))

        bank = [psum(f"bank{i}", [P, 512]) for i in range(8)]

        s = {n: [new_sem(f"s_{n}{i}") for i in range(2)] if n in PER else new_sem("s_" + n) for n in USES}

        def need(eng, sem, v):
            if not isinstance(v, int) or v > 0:
                eng.wait_ge(sem, v)

        def n_before(name, k):
            return NT * len([q for q in USES[name] if q < k])

        def wait(eng, name, k, count):
            need(eng, s[name], n_before(name, k) + count)

        def dma_count(name, k, at, d):
            return (n_before(name, k) // 2 + at.half(d) + 1) * PER[name]

        def wait_dma(eng, name, k, at, d):
            need(eng, s[name][at.par(d)], dma_count(name, k, at, d))

        s_load = [new_sem(f"s_load{i}") for i in range(3)]
        s_dump = new_sem("s_dump")
        s_prep = new_sem("s_prep")
        s_sign = new_sem("s_sign")
        s_clear = new_sem("s_clear")
        s_zero_rows = new_sem("s_zero_rows")
        s_route_step = new_sem("s_route_step")
        s_x = [new_sem(f"s_x{i}") for i in range(4)]

        PAIRED = ["xs", "w1", "w2", "b2", "y_out", "gy"]
        MSEM = ["stat", "mv", "var", "rstd", "xn", "xt_ps", "xt_sb", "xna", "xta", "lg_ps", "lg_sb", "gate", "gate_e", "onehot", "rank_ps",
                "pos", "scat", "xs", "w1", "w2", "b2", "t_ps", "t_sb", "g_ps", "a_ps", "gate_sb", "u", "hid", "y_ps", "y_sb",
                "y_out", "gy", "mix"]
        ms = [{n: [new_sem(f"m{m}_{n}{i}") for i in range(2)] if n in PAIRED else new_sem(f"m{m}_{n}") for n in MSEM}
              for m in range(2)]
        sh = {n: new_sem("sh_" + n) for n in ("g_ps", "a_ps", "gate", "hid", "y_ps", "bias", "res")}
        fin = {n: new_sem("fin_" + n) for n in ("bias", "xt_ps", "xt_sb", "y_ps", "out", "dma")}

        def tiles_of(k, st):
            return (st + 2, st + 1, st, st - 1, st - 2, st - 3) if k == 2 else (st + 1, None, st, st - 1, st - 2, st - 3)

        class At:

            def __init__(self, st, u, h, mid):
                self.st, self.u, self.h, self.mid = st, u, h, mid

            def half(self, d):
                return self.h + (self.u + d) // 2

            def par(self, d):
                return (self.u + d) % 2

        def alone(body, *sts):
            for st in sts:
                body(At(st, st % 2, st // 2, False))

        def run_steps(eng, first, end, body, loop_end):
            alone(body, *range(first, LOOP_FROM))
            with eng.Fori(0, (loop_end - LOOP_FROM) // 2) as j:
                for u in range(2):
                    body(At(LOOP_FROM + 2 * j + u, u, LOOP_FROM // 2 + j, True))
            alone(body, *range(loop_end, end))

        def steps(eng, k, body):
            run_steps(eng, -2 if k == 2 else -1, NT + 3, body, NT - 2)

        def row_steps(eng, n, first, body):
            run_steps(eng, first, n + 1, body, n - 2)

        def token_steps(eng, body, first=0, end=NT):
            run_steps(eng, first, end, body, NT - 2)

        def live(t, mid, n=NT):
            return t is not None and (mid or 0 <= t < n)

        def row_tile(at, d, n):
            return at.par(d) * (n // 2) + at.half(d)

        def one(t):
            return bass.ds(t, 1)

        def span(t, w):
            return bass.ds(t * w, w)

        ORDER = ["A0", "A1", "M0", "A2", "A3", "M1"]
        plan = ORDER[:ORDER.index(STOP) + 1] if STOP else ORDER

        MOE = [dict(E=E0, n=M0_TILES, hid=HR, R=HR // P // 2, W1=a["W1_0"], W2=a["W2_0"], b2=a["b2_0"]),
               dict(E=E1, n=M1_TILES, hid=HX, R=HX // P // 2, W1=a["W1_1"], W2=a["W2_1"], b2=a["b2_1"])]

        block = ctx.enter_context(nc.Block())

        @block.sync
        def _(sp):
            sp.dma_start(cst[:], a["cst"]).then_inc(s_load[0], 16)
            sp.dma_start(X[:, 0:4, :], a["x"][:, 0:4, :]).then_inc(s_x[0], 16)
            for n in wname[:4]:
                sp.dma_start(W[n], a[n]).then_inc(s_load[0], 16)
            sp.dma_start(qk_bias[:], a["qk_bias"]).then_inc(s_load[0], 16)
            sp.dma_start(rows0[:], a["rows0"].to_broadcast([P, 2, D])).then_inc(s_load[0], 16)
            sp.dma_start(sign_cols[:], a["sign_cols"]).then_inc(s_load[0], 16)
            sp.dma_start(sign_v[:], a["sign_v"].to_broadcast([P, D])).then_inc(s_load[0], 16)
            for q in range(1, 4):
                sp.dma_start(X[:, 4 * q:4 * q + 4, :], a["x"][:, 4 * q:4 * q + 4, :]).then_inc(s_x[q], 16)

            def ahead(v):
                return v if isinstance(v, int) else sp.to_reg(v)

            def attention_step(k, at):
                st, u, mid = at.st, at.u, at.mid
                tf, tc, ta, tb, tv, to = tiles_of(k, st)
                if live(ta, mid):
                    n_source, n_used = ahead(n_before("v_sb", k) + ta + 1), ahead(n_before("o_ps", k) + ta - 1)
                    n_stored, n_spread = ahead(dma_count("vd", k, at, 0)), ahead(dma_count("vb", k, at, -2))
                if k == 0 and live(tf, mid):
                    wait(sp, "v_ps", 0, tf - 1)
                    sp.dma_start(CT[:, 1 - u, :, :], a["ctx32"][:, one(tf), :, :]).then_inc(s["ctx"][at.par(1)], 16)
                if k == 2 and live(tf, mid):
                    wait(sp, "cs_ps", 2, tf - 1)
                    sp.dma_start(CXT[:, u, :, :, :], a["ctxT"][:, one(tf), :, :, :]).then_inc(s["cxt"][u], 16)
                if live(ta, mid):
                    need(sp, s["v_sb"], n_source)
                    need(sp, s["vb"][u], n_spread)
                    sp.dma_start(v_rows[u], VS[:, u, :]).then_inc(s["vd"][u], 16)
                    need(sp, s["vd"][u], n_stored)
                    need(sp, s["o_ps"], n_used)
                    for h in range(4):
                        sp.dma_start(VB[32 * h:32 * h + 32, u, :, h, :],
                                     v_rows[u].rearrange("(b k) (h e) -> h k b e", b=BT, h=4)[h]).then_inc(s["vb"][u], 16)

            def load_if_new(e, held, dst, table, sem):
                def load():
                    sp.dma_start(dst, table[one(e), :, :]).then_inc(sem, 16)

                if held is None:
                    load()
                else:
                    with sp.If(e != held):
                        load()
                    with sp.Else():
                        sp.sem_inc(sem, 16)

            def expert_step(m, at):
                st, u, mid = at.st, at.u, at.mid
                q, n = ms[m], MOE[m]["n"]
                def expert(t):
                    return sp.value_load(slot_e[0:1, one(t)], min_val=0, max_val=MOE[m]["E"] - 1)

                if live(st + 1, mid, n):
                    e_next = expert(row_tile(at, 1, n))
                    e_next_held = expert(row_tile(at, 1, n) - 1) if mid or st + 1 >= 2 else None
                    n_first, n_rows = ahead(MOE[m]["R"] * st), ahead(st + 1)
                if live(st, mid, n):
                    e_this = expert(row_tile(at, 0, n))
                    e_this_held = expert(row_tile(at, 0, n) - 1) if mid or st >= 2 else None
                if live(st + 1, mid, n):
                    need(sp, q["hid" if m == 0 else "u"], n_first)
                if live(st + 2, mid, n):
                    n_rows = n_rows if live(st + 1, mid, n) else st + 1
                    need(sp, q["t_ps"], n_rows)
                    sp.dma_start(XS[:, u, :], sorted_rows[m].rearrange("(n p) d -> p n d", p=P)[:, one(row_tile(at, 2, n)), :]
                                 ).then_inc(q["xs"][u], 16)
                if live(st + 1, mid, n):
                    load_if_new(e_next, e_next_held, W1[:, 1 - u, 0:MOE[m]["W1"].shape[2]], MOE[m]["W1"], q["w1"][1 - u])
                if live(st, mid, n):
                    need(sp, q["y_sb"], st - 1)
                    sp.dma_start(b2[:, u, :], MOE[m]["b2"][one(e_this), :].to_broadcast([P, D])).then_inc(q["b2"][u], 16)
                    load_if_new(e_this, e_this_held, W2[:, u, 0:MOE[m]["W2"].shape[2]], MOE[m]["W2"], q["w2"][u])
                if live(st - 2, mid, n):
                    sp.wait_ge(q["y_sb"], st - 1)
                    sp.dma_start(expert_rows[m].rearrange("(n p) d -> p n d", p=P)[:, one(row_tile(at, -2, n)), :], YS[:, u, :]
                                 ).then_inc(q["y_out"][u], 16)

            def experts(m):
                q, n = ms[m], MOE[m]["n"]
                sp.wait_ge(q["pos"], 2)
                sp.wait_ge(q["scat"], 32 * NT)
                row_steps(sp, n, -2, lambda at: expert_step(m, at))
                sp.wait_ge(q["y_sb"], n)
                sp.dma_start(expert_rows[m].rearrange("(n p) d -> p n d", p=P)[:, n - 1:n, :], YS[:, (n - 1) % 2, :]
                             ).then_inc(q["y_out"][(n - 1) % 2], 16)

            for name in plan:
                k = int(name[1])
                if name[0] == "A":
                    steps(sp, k, lambda at: attention_step(k, at))
                else:
                    experts(k)
            if STOP is None or STOP == "M1":
                sp.wait_ge(fin["out"], 1)
                with sp.Fori(1, NT + 1) as t1:
                    sp.wait_ge(fin["out"], t1)
                    sp.dma_start(out[:, one(t1 - 1), :], X[:, one(t1 - 1), :]).then_inc(fin["dma"], 16)
                sp.wait_ge(fin["dma"], 16 * NT)
            else:
                k = int(STOP[1])
                sp.wait_ge(s["res"] if STOP[0] == "A" else ms[k]["comb"], n_before("res", k) + NT if STOP[0] == "A" else 2 * NT)
                sp.dma_start(out, X[:]).then_inc(s_dump, 16)
                sp.wait_ge(s_dump, 16)
                sp.wait_ge(s_load[1], 16 * len(wname[4:]))
                sp.wait_ge(s_load[2], 16 * len(MLP_LOADS))
                sp.wait_ge(s_zero_rows, 32 * NT)

        @block.gpsimd
        def _(pool):
            nc.gpsimd.memset(minus_half[:], -0.5).then_inc(s_clear, 1)
            nc.gpsimd.memset(zeros[:], 0.0).then_inc(s_clear, 1)
            nc.gpsimd.memset(VB[:], 0.0).then_inc(s_clear, 1)
            nc.gpsimd.memset(ones_sq[:], 1.0).then_inc(s_clear, 1)
            pool.wait_ge(s_clear, 4)
            pool.wait_ge(s_load[0], 16 * 9)

            def root(sem_in, sem_out, sems, base, t, par):
                need(pool, sems[sem_in], base + t + 1)
                nc.gpsimd.tensor_tensor(rstd[:, par, :], var[:, par, :], minus_half[:], ALU.pow).then_inc(sems[sem_out], 1)

            def attention_step(k, at):
                st, u, mid = at.st, at.u, at.mid
                tf, tc, ta, tb, tv, to = tiles_of(k, st)
                if k == 2 and live(tf + 1, mid):
                    gather_results(0, tf + 1)
                if k == 2 and live(tc, mid):
                    wait(pool, "row", 2, tc + 1)
                if live(tf, mid):
                    root("var", "rstd", s, n_before("var", k), tf, u if k == 2 else 1 - u)
                if k == 0 and live(ta, mid):
                    if not mid:
                        wait(pool, "xn", 0, ta + 1)
                    nc.gpsimd.tensor_tensor(X[:, one(ta), :], X[:, one(ta), :], rows0[:, 1, :].unsqueeze(1), ALU.add
                                            ).then_inc(s["bias"], 1)
                if k == 3 and live(ta, mid):
                    wait(pool, "rope", 3, ta + 1)
                    nc.gpsimd.tensor_tensor(QK[:, u, :, :].rearrange("p a n -> p (a n)"), RT[:, 0, :], RT[:, 1, :],
                                            ALU.add).then_inc(s["qk_sb"], 1)
                if k == 2 and live(tc, mid):
                    nc.gpsimd.indirect_dma_start(
                        out=MEM[:, 1 - u, :], out_offset=None, in_=a["ctx_rows"],
                        in_offset=bass.IndirectOffsetOnAxis(ap=row[:, 1 - u:2 - u], axis=0)).then_inc(s["mem"][1 - u], 16)

            def gather_results(m, t):
                q = ms[m]
                if t >= 2:
                    pool.wait_ge(q["mix"], 2 * (t - 1))
                for c in range(2):
                    nc.gpsimd.indirect_dma_start(
                        out=GY[:, t % 2, c, :], out_offset=None, in_=expert_rows[m],
                        in_offset=bass.IndirectOffsetOnAxis(ap=pos[:, c, t:t + 1], axis=0)).then_inc(q["gy"][t % 2], 16)

            def moe(m):
                q = ms[m]
                pool.wait_ge(q["var"], 1)
                nc.gpsimd.tensor_tensor(rstd_all[:], var_all[:], minus_half[:].to_broadcast([P, NT]), ALU.pow
                                        ).then_inc(q["rstd"], 1)
                pool.wait_ge(q["pos"], 2)
                pool.wait_ge(q["xna"], NT)
                pool.wait_ge(s_zero_rows, 32 * NT)
                for t in range(NT):
                    for c in range(2):
                        nc.gpsimd.indirect_dma_start(
                            out=sorted_rows[m], out_offset=bass.IndirectOffsetOnAxis(ap=pos[:, c, t:t + 1], axis=0),
                            in_=XNA[:, t, :], in_offset=None).then_inc(q["scat"], 16)
                for par in range(2):
                    pool.wait_ge(q["y_out"][par], 8 * MOE[m]["n"])
                for t in range(1 if m == 0 else NT):
                    gather_results(m, t)

            for name in plan:
                k = int(name[1])
                if name[0] == "A":
                    if k == 2:
                        alone(lambda at: attention_step(2, at), *range(-2, NT + 3))
                    else:
                        steps(pool, k, lambda at: attention_step(k, at))
                else:
                    moe(k)

        @block.scalar
        def _(act):
            act.wait_ge(s_load[0], 16 * 9)
            act.wait_ge(s_clear, 4)
            nc.scalar.activation(sign_cols[:], sign_cols[:], ACT.Sign).then_inc(s_sign, 1)
            nc.scalar.activation(sign_v[:], sign_v[:], ACT.Sign).then_inc(s_sign, 1)

            def weight_loads(names):
                for n in names:
                    act.dma_start(W[n], a[n]).then_inc(s_load[1], 16)

            def mlp_loads():
                wait(act, "y_ps", 0, NT)
                for dst, n in MLP_LOADS:
                    src = a[n].to_broadcast([P, D]) if n in ("bs2", "bf") else a[n]
                    act.dma_start(dst, src).then_inc(s_load[2], 16)

            def zero_sorted_rows(m, at):
                rows = sorted_rows[m].rearrange("(t p j) d -> p t j d", t=NT, p=32)
                j = MOE[m]["n"] * P // NT // 32
                act.dma_start(rows[:, one(at.st), :, :].rearrange("p t j d -> p (t j) d"),
                              zeros[0:32, None, :].to_broadcast([32, j, D])).then_inc(s_zero_rows, 16)

            def move(out_, in_):
                return nc.scalar.copy(out_, in_)

            def attention_step(k, at):
                st, u, mid = at.st, at.u, at.mid
                tf, tc, ta, tb, tv, to = tiles_of(k, st)
                if k < 2 and live(ta, mid):
                    zero_sorted_rows(k, at)
                tx, ux = (tc, 1 - u) if k == 2 else (ta, u)
                if k == 1 and live(tb, mid):
                    wait(act, "sc_ps", 1, tb + 1)
                    wait(act, "pt_ps", 1, tb - 1)
                    nc.scalar.activation(PR[:, 1 - u, :], bank[4][:], ACT.Sigmoid,
                                         scale=4.0 * HD ** -0.5).then_inc(s["prob"], 1)
                if k != 1 and live(to, mid):
                    wait(act, "ot_ps", k, to + 1)
                    move(OT[:], bank[7][:, 0:2 * P].rearrange("p (c n) -> p c n", c=2)).then_inc(s["ot_sb"], 1)
                if live(tx, mid):
                    wait(act, "xt_ps", k, tx + 1)
                    dst = QK[:, ux, 0:2, :] if k == 1 else XT[:, ux, :, :]
                    move(dst, bank[0][:, 0:2 * P].rearrange("p (c n) -> p c n", c=2)).then_inc(s["xt_sb"], 1)
                if live(tv, mid):
                    wait(act, "pt_ps", k, tv + 1)
                    move(PT[:, u, :, :], bank[5][:].rearrange("p (g n) -> p g n", g=4)).then_inc(s["pt_sb"], 1)
                if k != 1 and live(tb, mid):
                    wait(act, "sub", k, tb + 1)
                    nc.scalar.activation(PR[:, 1 - u, :], PR[:, 1 - u, :], ACT.Exp, scale=HD ** -0.5).then_inc(s["prob"], 1)
                if k == 2 and live(tc, mid):
                    wait(act, "q_ps", 2, tc + 1)
                    move(QK[:, 1 - u, 0:2, :], bank[1][:, 0:2 * P].rearrange("p (c n) -> p c n", c=2)).then_inc(s["q_sb"], 1)
                if k == 2 and live(ta, mid):
                    wait(act, "mt_ps", 2, ta + 1)
                    move(CT[:, u, :, :], bank[0][:, 2 * P:4 * P].rearrange("p (c n) -> p c n", c=2)).then_inc(s["mt_sb"], 1)
                    wait(act, "k_ps", 2, ta + 1)
                    move(QK[:, u, 2:4, :], bank[1][:, 2 * P:4 * P].rearrange("p (c n) -> p c n", c=2)).then_inc(s["qk_sb"], 1)
                if k == 0 and live(ta, mid):
                    wait(act, "qk_ps", 0, ta + 1)
                    for i in range(4):
                        last = nc.scalar.activation(QK[:, u, i, :], bank[1][:, i * P:(i + 1) * P], ACT.Identity,
                                                    bias=qk_bias[:, i:i + 1])
                    last.then_inc(s["qk_sb"], 1)
                if k != 0 and live(ta, mid):
                    wait(act, "xn" if k == 1 else "v_ps", k, ta + 1)
                    wait_dma(act, "vd", k, at, -2)
                    if k == 1:
                        move(VS[:, u, :].rearrange("p (h g d) -> p h g d", h=4, g=4),
                             XN[:, u, :].rearrange("p (g h d) -> p h g d", g=4, h=4)).then_inc(s["v_sb"], 1)
                    else:
                        move(VS[:, u, :], bank[3][:, 0:D]).then_inc(s["v_sb"], 1)

            def route_step(m, at):
                st, u, mid = at.st, at.u, at.mid
                q = ms[m]
                if live(st, mid):
                    need(act, q["xt_ps"], st + 1)
                    src = bank[0][:, 0:2 * P].rearrange("p (c n) -> p c n", c=2)
                    move(XT[:, u, :, :], src).then_inc(q["xt_sb"], 1)
                    if m == 0:
                        move(XTA[:, :, span(st, P)], src).then_inc(q["xta"], 1)
                    move(XNA[:, one(st), :], XN[:, u, :]).then_inc(q["xna"], 1)

            def shared_group(g, first):
                for j in range(4):
                    need(act, sh["g_ps"], 4 * g + j + 1)
                    if not (first and j < 2):
                        act.wait_ge(sh["hid"], 4 * g + j - 1)
                    nc.scalar.activation(SG[:, j % 2, :], bank[4 + j % 2][:], ACT.Gelu,
                                         bias=bs1[:, 4 + j:5 + j]).then_inc(sh["gate"], 1)

            def expert_step(m, at):
                st, u, mid = at.st, at.u, at.mid
                q, n, R = ms[m], MOE[m]["n"], MOE[m]["R"]
                hc = 2 * R
                if live(st + 1, mid, n):
                    need(act, q["t_ps"], st + 2)
                    move(XT[:, 1 - u, :, :], bank[0][:, 0:2 * P].rearrange("p (c n) -> p c n", c=2)).then_inc(q["t_sb"], 1)
                if live(st, mid, n):
                    b1_at = C2 * 2 * MOE[m]["hid"]
                    for r in range(R):
                        par = (R * u + r) % 2
                        need(act, q["g_ps"], R * st + r + 1)
                        need(act, q["hid"] if m == 0 else q["u"], R * st + r - 1)
                        for i in range(2):
                            bias = W1[:, u, b1_at + hc + 2 * r + i:b1_at + hc + 2 * r + i + 1]
                            last = nc.scalar.activation(GS[:, par, i, :], bank[1 + par][:, i * P:(i + 1) * P],
                                                        ACT.Gelu if m == 0 else ACT.Identity, bias=bias)
                        last.then_inc(q["gate_sb"], 1)
                    if m == 1:
                        for r in range(R):
                            need(act, q["u"], R * st + r + 1)
                            nc.scalar.activation(HB[:, u, 2 * r:2 * r + 2, :], HB[:, u, 2 * r:2 * r + 2, :],
                                                 ACT.Silu).then_inc(q["hid"], 1)

            def final_step(at):
                st, u, mid = at.st, at.u, at.mid
                if live(st, mid):
                    need(act, fin["xt_ps"], st + 1)
                    move(XT[:, u, :, :], bank[0][:, 0:2 * P].rearrange("p (c n) -> p c n", c=2)).then_inc(fin["xt_sb"], 1)

            def moe(m):
                q = ms[m]
                token_steps(act, lambda at: route_step(m, at), 0)
                act.wait_ge(q["gate"], 1)
                if m == 0:
                    nc.scalar.activation(r16[2][:], r16[2][:], ACT.Exp).then_inc(q["gate_e"], 1)
                    act.preload_act_table(ACT.Gelu)
                    act.wait_ge(s_load[2], 16 * len(MLP_LOADS))
                    shared_group(0, True)
                    with act.Fori(1, 4) as g:
                        shared_group(g, False)
                else:
                    nc.scalar.activation(RB[:, :, 0:E1], RB[:, :, 0:E1], ACT.Exp).then_inc(q["gate_e"], 1)
                    act.preload_act_table(ACT.Silu)
                row_steps(act, MOE[m]["n"], -1, lambda at: expert_step(m, at))
                if m == 1:
                    token_steps(act, final_step)

            for name in plan:
                k = int(name[1])
                if name[0] == "A":
                    act.preload_act_table(ACT.Sigmoid if k == 1 else ACT.Exp)
                    if k == 1:
                        weight_loads(wname[4:8])
                    elif k == 2:
                        weight_loads(wname[8:])
                    steps(act, k, lambda at: attention_step(k, at))
                    if k == 0:
                        mlp_loads()
                else:
                    moe(k)

        @block.vector
        def _(dve):
            nc.vector.memset(hold[:], 0.0).then_inc(s_prep, 1)
            nc.vector.memset(ones[:], 1.0).then_inc(s_prep, 1)
            dve.wait_ge(s_load[0], 16 * 9)
            nc.vector.tensor_copy(ident_bf[:], const("ident")).then_inc(s_prep, 1)
            nc.vector.tensor_copy(causal_bf[:], const("causal")).then_inc(s_prep, 1)
            dve.wait_ge(s_sign, 2)
            nc.vector.tensor_tensor(sign_qk[:], sign_cols[:, 0, :], sign_cols[:, 1, :], ALU.mult).then_inc(s_prep, 1)
            dve.wait_ge(s_prep, 5)
            nc.vector.tensor_tensor(sign_mask[:], const("head_mask").unsqueeze(1).to_broadcast([P, C2, HC]),
                                    sign_qk[:].unsqueeze(2).to_broadcast([P, C2, HC]), ALU.mult).then_inc(s_prep, 1)
            dve.wait_ge(s_prep, 6)

            def hold_until(sem, v):
                need(dve, sem, v)
                nc.vector.tensor_copy(hold[:], hold[:])

            def norm_stats(q, base, t, par):
                nc.vector.bn_stats(stats[:, par, :], X[:, one(t), :]).then_inc(q["stat"], 1)
                hold_until(q["stat"], base + t + 1)
                nc.vector.bn_aggr(mv[:, par, :], stats[:, par, :]).then_inc(q["mv"], 1)
                dve.wait_ge(q["mv"], base + t + 1)
                nc.vector.tensor_scalar(var[:, par, :], mv[:, par, 1:2], EPS, None, ALU.add).then_inc(q["var"], 1)

            def norm_apply(q, base, t, par):
                dve.wait_ge(q["rstd"], base + t + 1)
                nc.vector.tensor_scalar(XN[:, par, :], X[:, one(t), :], mv[:, par, 0:1], rstd[:, par, 0:1],
                                        ALU.subtract, ALU.mult).then_inc(q["xn"], 1)

            def combine(t, at):
                q = ms[0]
                dve.wait_ge(q["gy"][at.par(2)], 32 * (at.half(2) + 1))
                for c in range(2):
                    nc.vector.scalar_tensor_tensor(out=X[:, one(t), :], in0=GY[:, at.par(2), c:c + 1, :],
                                                   scalar=wts[:, c, one(t)], in1=X[:, one(t), :], op0=ALU.mult,
                                                   op1=ALU.add).then_inc(q["mix"], 1)
                    hold_until(q["mix"], 2 * t + c + 1)

            def attention_step(k, at):
                st, u, mid = at.st, at.u, at.mid
                tf, tc, ta, tb, tv, to = tiles_of(k, st)
                uf = u if k == 2 else 1 - u

                def softmax_less_max():
                    if k != 1 and live(tb, mid):
                        wait(dve, "sc_ps", k, tb + 1)
                        sc = bank[4][:].rearrange("p (h t) -> p h t", h=H)
                        nc.vector.tensor_reduce(mx[:], sc, AX.X, ALU.max).then_inc(s["mx"], 1)
                        wait(dve, "mx", k, tb + 1)
                        wait(dve, "pt_ps", k, tb - 1)
                        nc.vector.tensor_tensor(PR[:, 1 - u, :].rearrange("p (h t) -> p h t", h=H), sc,
                                                mx[:].unsqueeze(2).to_broadcast([P, H, T]), ALU.subtract).then_inc(s["sub"], 1)

                def normalise_stats():
                    if live(tf, mid):
                        if k == 0:
                            if not mid:
                                for q in ([0] if tf < 4 else range(4)):
                                    dve.wait_ge(s_x[q], 16)
                        elif k == 2:
                            combine(tf, at)
                        else:
                            wait(dve, "res", k - 1, tf + 1)
                        norm_stats(s, n_before("stat", k), tf, uf)

                def normalise():
                    if live(tf, mid):
                        if k == 1:
                            wait(dve, "v_sb", 1, tf - 1)
                        norm_apply(s, n_before("stat", k), tf, uf)

                def residual():
                    if k != 1 and live(to, mid):
                        wait(dve, "y_ps", k, to + 1)
                        if k == 0:
                            wait(dve, "bias", 0, to + 1)
                        nc.vector.tensor_tensor(X[:, one(to), :], X[:, one(to), :], bank[7][:, 2 * P:4 * P].unsqueeze(1),
                                                ALU.add).then_inc(s["res"], 1)

                def rotate():
                    if k == 3 and live(ta, mid):
                        wait(dve, "qk_ps", 3, ta + 1)
                        for i, (b_, tab) in enumerate(((1, "cos"), (2, "sin"))):
                            last = nc.vector.tensor_tensor(RT[:, i, :].rearrange("p (a t) -> p a t", t=T),
                                                           bank[b_][:].rearrange("p (a t) -> p a t", t=T),
                                                           const(tab).unsqueeze(1).to_broadcast([P, 4 * BT, T]), ALU.mult)
                        last.then_inc(s["rope"], 1)

                def v_bias():
                    if k == 0 and live(ta, mid):
                        wait(dve, "v_ps", 0, ta + 1)
                        wait_dma(dve, "vd", 0, at, -2)
                        nc.vector.tensor_tensor(VS[:, u, :], bank[3][:, 0:D], rows0[:, 0, :], ALU.add).then_inc(s["v_sb"], 1)

                def spread_k():
                    if live(ta, mid):
                        wait(dve, "xt_sb" if k == 1 else "qk_sb", k, ta + 1)
                        wait(dve, "sc_ps", k, ta - 1)
                        for c in range(C2):
                            src = QK[:, u, c if k == 1 else 2 + c, :]
                            m_ = sign_mask[:, c, :] if k == 1 else const("head_mask")
                            nc.vector.tensor_tensor(KB[:, u, c, :, :], src.unsqueeze(1).to_broadcast([P, HC, P]),
                                                    m_.unsqueeze(2).to_broadcast([P, HC, P]), ALU.mult
                                                    ).then_inc(s["kb1" if c else "kb"], 1)

                def attention_out():
                    if live(tv, mid):
                        wait(dve, "o_ps", k, tv + 1)
                        if k == 1:
                            nc.vector.tensor_tensor(OS[:, u, :], bank[6][:, 0:D], sign_v[:], ALU.mult).then_inc(s["o_sb"], 1)
                            wait(dve, "o_sb", 1, tv + 1)
                            nc.vector.tensor_tensor(X[:, one(tv), :], X[:, one(tv), :], OS[:, u, :].unsqueeze(1),
                                                    ALU.add).then_inc(s["res"], 1)
                        else:
                            wait(dve, "ot_ps", k, tv - 1)
                            nc.vector.reciprocal(rc[:], bank[6][:, D:D + H]).then_inc(s["rc"], 1)
                            wait(dve, "rc", k, tv + 1)
                            nc.vector.tensor_tensor(OS[:, u, :].rearrange("p (h d) -> p h d", h=H),
                                                    bank[6][:, 0:D].rearrange("p (h d) -> p h d", h=H),
                                                    rc[:].unsqueeze(2).to_broadcast([P, H, HD]), ALU.mult).then_inc(s["o_sb"], 1)

                def look_up():
                    if k == 2 and live(tc, mid):
                        v = n_before("cs_ps", 2) + tc + 1
                        hold_until(s["cs_ps"], v)
                        nc.vector.max(top8[:], bank[2][:, 0:S]).then_inc(s["top"], 1)
                        hold_until(s["top"], v)
                        nc.vector.max_index(idx8[:], top8[:], bank[2][:, 0:S]).then_inc(s["idx"], 1)
                        dve.wait_ge(s["idx"], v)
                        wait_dma(dve, "mem", 2, at, -1)
                        nc.vector.tensor_tensor(row[:, 1 - u:2 - u], idx8[:, 0:1], const("row0")[:, one(tc)],
                                                ALU.add).then_inc(s["row"], 1)

                softmax_less_max()
                normalise_stats()
                if k == 2:
                    residual()
                    attention_out()
                    spread_k()
                    look_up()
                    normalise()
                else:
                    normalise()
                    residual()
                    rotate()
                    v_bias()
                    spread_k()
                    attention_out()

            def route_step(m, at):
                st, u, mid = at.st, at.u, at.mid
                q = ms[m]
                if live(st + 1, mid):
                    need(dve, q["xna"], st)
                    nc.vector.tensor_scalar(XN[:, 1 - u, :], X[:, one(st + 1), :], mv_all[:, one(st + 1), 0],
                                            rstd_all[:, one(st + 1)], ALU.subtract, ALU.mult).then_inc(q["xn"], 1)
                if live(st, mid):
                    need(dve, q["lg_ps"], st + 1)
                    nc.vector.tensor_copy(LG[:, one(st), 0:MOE[m]["E"]], bank[1][:, 0:MOE[m]["E"]].unsqueeze(1)
                                          ).then_inc(q["lg_sb"], 1)

            done = [0]

            def then(ins):
                done[0] += 1
                ins.then_inc(s_route_step, 1)
                dve.wait_ge(s_route_step, done[0])

            def pick(vals, rank, c, E, m_out):
                then(nc.vector.tensor_reduce(m_out[:], vals, AX.X, ALU.max))
                then(nc.vector.tensor_tensor(RC[:, :, 0:E], vals, m_out[:].unsqueeze(2).to_broadcast([P, NT, E]), ALU.is_equal))
                then(nc.vector.tensor_tensor(RC[:, :, 0:E], RC[:, :, 0:E], rank, ALU.mult))
                then(nc.vector.tensor_reduce(r16[3][:], RC[:, :, 0:E], AX.X, ALU.max))
                then(nc.vector.tensor_tensor(RM[:, c, :, 0:E], RC[:, :, 0:E],
                                             r16[3][:].unsqueeze(2).to_broadcast([P, NT, E]), ALU.is_equal))

            def route(m):
                q, E, n = ms[m], MOE[m]["E"], MOE[m]["n"]
                off = 0 if m == 0 else E0
                rank = const("ranks")[:, off:off + E].unsqueeze(1).to_broadcast([P, NT, E])
                L = LG[:, :, 0:E]
                V = RB[:, :, 0:E]
                dve.wait_ge(q["lg_sb"], NT)
                if m == 0:
                    then(nc.vector.tensor_scalar(V, L, 1.0 / TAU, None, ALU.mult))
                else:
                    then(nc.vector.tensor_reduce(r16[2][:], L, AX.X, ALU.max))
                    nc.vector.tensor_tensor(V, L, r16[2][:].unsqueeze(2).to_broadcast([P, NT, E]),
                                            ALU.subtract).then_inc(q["gate"], 1)
                    dve.wait_ge(q["gate_e"], 1)
                    then(nc.vector.tensor_reduce(r16[2][:], V, AX.X, ALU.add))
                    then(nc.vector.reciprocal(r16[2][:], r16[2][:]))
                    then(nc.vector.tensor_tensor(V, V, r16[2][:].unsqueeze(2).to_broadcast([P, NT, E]), ALU.mult))
                pick(V, rank, 0, E, r16[0])
                then(nc.vector.tensor_scalar(RA[:, :, 0:E], RM[:, 0, :, 0:E], NEG, None, ALU.mult))
                then(nc.vector.tensor_tensor(RA[:, :, 0:E], RA[:, :, 0:E], V, ALU.add))
                pick(RA[:, :, 0:E], rank, 1, E, r16[1])
                nc.vector.tensor_tensor(RC[:, :, 0:E], RM[:, 0, :, 0:E], RM[:, 1, :, 0:E], ALU.add).then_inc(q["onehot"], 1)
                if m == 0:
                    nc.vector.tensor_tensor(r16[2][:], r16[1][:], r16[0][:], ALU.subtract).then_inc(q["gate"], 1)
                    dve.wait_ge(q["gate_e"], 1)
                    then(nc.vector.tensor_scalar(r16[3][:], r16[2][:], 1.0, None, ALU.add))
                    then(nc.vector.reciprocal(wts[:, 0, :], r16[3][:]))
                    then(nc.vector.tensor_tensor(wts[:, 1, :], wts[:, 0, :], r16[2][:], ALU.mult))
                else:
                    then(nc.vector.tensor_copy(wts[:, 0, :], r16[0][:]))
                    then(nc.vector.tensor_copy(wts[:, 1, :], r16[1][:]))
                dve.wait_ge(q["rank_ps"], 1)
                within = bank[2][:, 0:NT * E].rearrange("p (t e) -> p t e", e=E)
                total = bank[3][:, 0:NT * E].rearrange("p (t e) -> p t e", e=E)
                O = RO[:, :, 0:E]
                then(nc.vector.memset(RO[:, 0:1, 0:E], 0.0))
                for t in range(1, NT):
                    then(nc.vector.tensor_tensor(RO[:, t:t + 1, 0:E], RO[:, t - 1:t, 0:E], total[:, t - 1:t, :], ALU.add))
                cnt, ends, base = (r[:, 0:E] for r in re_)
                then(nc.vector.tensor_tensor(cnt, RO[:, NT - 1, 0:E], total[:, NT - 1, :], ALU.add))
                then(nc.vector.tensor_scalar(rei[:, 0:E], cnt, float(P - 1), None, ALU.add))
                then(nc.vector.tensor_scalar(rei[:, 0:E], rei[:, 0:E], 7, None, ALU.arith_shift_right))
                then(nc.vector.tensor_copy(cnt, rei[:, 0:E]))
                tril = const("tril").rearrange("p (a b) -> p a b", a=E0)[:, 0:E, 0:E]
                then(nc.vector.tensor_tensor(RX[:, 0:E, 0:E], cnt.unsqueeze(1).to_broadcast([P, E, E]), tril, ALU.mult))
                then(nc.vector.tensor_reduce(ends, RX[:, 0:E, 0:E], AX.X, ALU.add))
                then(nc.vector.tensor_tensor(base, ends, cnt, ALU.subtract))
                then(nc.vector.tensor_scalar(base, base, float(P), None, ALU.mult))
                then(nc.vector.tensor_tensor(O, O, within, ALU.add))
                then(nc.vector.tensor_tensor(O, O, base.unsqueeze(1).to_broadcast([P, NT, E]), ALU.add))
                for c in range(2):
                    then(nc.vector.tensor_tensor(RC[:, :, 0:E], RM[:, c, :, 0:E], O, ALU.mult))
                    then(nc.vector.tensor_reduce(r16[3][:], RC[:, :, 0:E], AX.X, ALU.add))
                    last = nc.vector.tensor_copy(pos[:, c, :], r16[3][:])
                    if c == 0:
                        then(last)
                    else:
                        last.then_inc(q["pos"], 1)
                then(nc.vector.tensor_tensor(RE[:, 0:n, 0:E], ends.unsqueeze(1).to_broadcast([P, n, E]),
                                             const("slots")[:, 0:n].unsqueeze(2).to_broadcast([P, n, E]), ALU.is_le))
                then(nc.vector.tensor_reduce(rsl[:, 0:n], RE[:, 0:n, 0:E], AX.X, ALU.add))
                nc.vector.tensor_scalar(slot_e[0:1, 0:n], rsl[0:1, 0:n], float(E - 1), None, ALU.min).then_inc(q["pos"], 1)

            def shared_group(g):
                for j in range(4):
                    dve.wait_ge(sh["a_ps"], 4 * g + j + 1)
                    dve.wait_ge(sh["gate"], 4 * g + j + 1)
                    nc.vector.scalar_tensor_tensor(out=SH[:, j, :], in0=bank[2 + j % 2][:], scalar=bs1[:, j:j + 1],
                                                   in1=SG[:, j % 2, :], op0=ALU.add, op1=ALU.mult).then_inc(sh["hid"], 1)
                for t in range(4):
                    nc.vector.tensor_tensor(X[:, one(4 * g + t), :], X[:, one(4 * g + t), :], bs2[:].unsqueeze(1), ALU.add
                                            ).then_inc(sh["bias"], 1)
                    dve.wait_ge(sh["bias"], 4 * g + t + 1)
                    dve.wait_ge(sh["y_ps"], 4 * g + t + 1)
                    nc.vector.tensor_tensor(X[:, one(4 * g + t), :], X[:, one(4 * g + t), :],
                                            bank[6 + t % 2][:, 0:D].unsqueeze(1), ALU.add).then_inc(sh["res"], 1)

            def expert_step(m, at):
                st, u, mid = at.st, at.u, at.mid
                q, n, R = ms[m], MOE[m]["n"], MOE[m]["R"]
                if live(st, mid, n):
                    b1_at = C2 * 2 * MOE[m]["hid"]
                    for r in range(R):
                        par = (R * u + r) % 2
                        need(dve, q["a_ps"], R * st + r + 1)
                        need(dve, q["gate_sb"], R * st + r + 1)
                        for i in range(2):
                            bias = W1[:, u, b1_at + 2 * r + i:b1_at + 2 * r + i + 1]
                            last = nc.vector.scalar_tensor_tensor(
                                out=HB[:, u, 2 * r + i, :], in0=bank[3 + par][:, i * P:(i + 1) * P], scalar=bias,
                                in1=GS[:, par, i, :], op0=ALU.add, op1=ALU.mult)
                        last.then_inc(q["hid"] if m == 0 else q["u"], 1)
                if live(st - 1, mid, n):
                    need(dve, q["y_ps"], st)
                    dve.wait_ge(q["b2"][1 - u], 16 * (at.half(-1) + 1))
                    need(dve, q["y_out"][1 - u], 16 * (at.half(-3) + 1))
                    nc.vector.tensor_tensor(YS[:, 1 - u, :], bank[5 + (1 - u)][:, 0:D], b2[:, 1 - u, :], ALU.add
                                            ).then_inc(q["y_sb"], 1)

            def final_step(at):
                st, u, mid = at.st, at.u, at.mid
                q = ms[1]
                if live(st, mid):
                    nc.vector.tensor_tensor(X[:, one(st), :], X[:, one(st), :], bf[:].unsqueeze(1), ALU.add
                                            ).then_inc(fin["bias"], 1)
                    dve.wait_ge(q["gy"][u], 32 * (at.half(0) + 1))
                    need(dve, fin["xt_ps"], st - 1)
                    nc.vector.tensor_scalar(XN[:, u, :], GY[:, u, 0, :], wts[:, 0, one(st)], None, ALU.mult
                                            ).then_inc(q["mix"], 1)
                    dve.wait_ge(q["mix"], 2 * st + 1)
                    nc.vector.scalar_tensor_tensor(out=XN[:, u, :], in0=GY[:, u, 1, :], scalar=wts[:, 1, one(st)],
                                                   in1=XN[:, u, :], op0=ALU.mult, op1=ALU.add).then_inc(q["mix"], 1)
                if live(st - 1, mid):
                    need(dve, fin["y_ps"], st)
                    need(dve, fin["bias"], st)
                    nc.vector.tensor_tensor(X[:, one(st - 1), :], X[:, one(st - 1), :], bank[1][:, 0:D].unsqueeze(1),
                                            ALU.add).then_inc(fin["out"], 1)

            def moe(m):
                q = ms[m]
                wait(dve, "res", 1 + 2 * m, NT)
                for t in range(NT):
                    nc.vector.bn_stats(stats_all[:, t, :], X[:, t, :]).then_inc(q["stat"], 1)
                hold_until(q["stat"], NT)
                for t in range(NT):
                    nc.vector.bn_aggr(mv_all[:, t, :], stats_all[:, t, :]).then_inc(q["mv"], 1)
                dve.wait_ge(q["mv"], NT)
                nc.vector.tensor_scalar(var_all[:], mv_all[:, :, 1], EPS, None, ALU.add).then_inc(q["var"], 1)
                dve.wait_ge(q["rstd"], 1)
                token_steps(dve, lambda at: route_step(m, at), -1)
                route(m)
                if m == 0:
                    dve.wait_ge(s_load[2], 16 * len(MLP_LOADS))
                    shared_group(0)
                    with dve.Fori(1, 4) as g:
                        shared_group(g)
                row_steps(dve, MOE[m]["n"], 0, lambda at: expert_step(m, at))
                if m == 1:
                    token_steps(dve, final_step, 0, NT + 1)

            for name in plan:
                k = int(name[1])
                if name[0] == "A":
                    steps(dve, k, lambda at: attention_step(k, at))
                else:
                    moe(k)

        @block.tensor
        def _(pe):
            mm = nc.tensor.matmul
            pe.wait_ge(s_load[0], 16 * 9)
            pe.wait_ge(s_prep, 6)
            pe.wait_ge(s_clear, 4)
            ident = const("ident")

            def transpose_tile(dst, src):
                for c in range(C2):
                    last = nc.tensor.transpose(dst[:, c * P:(c + 1) * P], src[:, c * P:(c + 1) * P], ident)
                return last

            def project(dst, w, src):
                for j in range(C2):
                    for c in range(C2):
                        last = mm(dst[:, j * P:(j + 1) * P], w[:, c, j * P:(j + 1) * P], src[:, c, :],
                                  start=(c == 0), stop=(c == C2 - 1))
                return last

            def project_rows(dst, w, src, bias=None, n=D):
                for c in range(C2):
                    last = mm(dst, src[:, c, :], w[:, c, 0:n], start=(c == 0), stop=(c == C2 - 1 and bias is None))
                if bias is not None:
                    last = mm(dst, ones[:], bias, start=False, stop=True)
                return last

            def scores(k, u, c):
                masked = k != 2
                if masked and c == 0:
                    mm(bank[4][:], ident_bf[:], causal_bf[:], start=True, stop=False, skip_group_check=True)
                for b in range(BT):
                    last = mm(bank[4][32 * b:32 * b + 32, c * HC * T:(c + 1) * HC * T], QK[:, u, c, 32 * b:32 * b + 32],
                              KB[:, u, c, :, 32 * b:32 * b + 32], start=not masked, stop=True, skip_group_check=True)
                return last

            def attention_step(k, at):
                st, u, mid = at.st, at.u, at.mid
                tf, tc, ta, tb, tv, to = tiles_of(k, st)
                tx, ux = (tc, 1 - u) if k == 2 else (ta, u)
                if live(tb, mid):
                    wait(pe, "kb", k, tb + 1)
                    wait(pe, "prob" if k == 1 else "sub", k, tb)
                    scores(k, 1 - u, 0)
                    wait(pe, "kb1", k, tb + 1)
                    scores(k, 1 - u, 1).then_inc(s["sc_ps"], 1)
                if k != 1 and live(to, mid):
                    wait(pe, "o_sb", k, to + 1)
                    wait(pe, "res", k, to)
                    transpose_tile(bank[7][:, 0:2 * P], OS[:, 1 - u, :]).then_inc(s["ot_ps"], 1)
                if live(tx, mid):
                    wait(pe, "xn", k, tx + 1)
                    wait(pe, "xt_sb", k, tx)
                    if k == 2:
                        wait(pe, "mt_sb", 2, tx - 1)
                    transpose_tile(bank[0][:, 0:2 * P], XN[:, ux, :]).then_inc(s["xt_ps"], 1)
                if live(tv, mid):
                    wait(pe, "prob", k, tv + 1)
                    wait(pe, "pt_sb", k, tv)
                    for g in range(4):
                        last = nc.tensor.transpose(bank[5][:, g * P:(g + 1) * P], PR[:, u, g * P:(g + 1) * P], ident)
                    last.then_inc(s["pt_ps"], 1)
                if k != 1 and live(to, mid):
                    wait(pe, "ot_sb", k, to + 1)
                    project_rows(bank[7][:, 2 * P:4 * P], W[f"Wo{k}"], OT[:]).then_inc(s["y_ps"], 1)
                if k == 2 and live(tc, mid):
                    wait(pe, "xt_sb", 2, tc + 1)
                    wait(pe, "qk_sb", 2, tc - 1)
                    project(bank[1][:, 0:2 * P], W["Wq2"], XT[:, 1 - u, :, :]).then_inc(s["q_ps"], 1)
                if k == 2 and live(ta, mid):
                    wait_dma(pe, "mem", 2, at, 0)
                    wait(pe, "xt_sb", 2, min(ta + 2, NT) if not mid else ta + 2)
                    transpose_tile(bank[0][:, 2 * P:4 * P], MEM[:, u, :]).then_inc(s["mt_ps"], 1)
                if k == 0 and live(ta, mid):
                    wait(pe, "xt_sb", 0, ta + 1)
                    wait(pe, "qk_sb", 0, ta)
                    wait_dma(pe, "ctx", 0, at, 0)
                    project(bank[1][:, 0:2 * P], W["Wq0"], XT[:, u, :, :])
                    project(bank[1][:, 2 * P:4 * P], W["Wk0"], CT[:, u, :, :]).then_inc(s["qk_ps"], 1)
                if k == 3 and live(ta, mid):
                    wait(pe, "xt_sb", 3, ta + 1)
                    wait(pe, "rope", 3, ta)
                    project(bank[1][:, 0:2 * P], W["Wq3"], XT[:, u, :, :])
                    project(bank[1][:, 2 * P:4 * P], W["Wk3"], XT[:, u, :, :])
                    project(bank[2][:, 0:2 * P], W["Wqs3"], XT[:, u, :, :])
                    project(bank[2][:, 2 * P:4 * P], W["Wks3"], XT[:, u, :, :]).then_inc(s["qk_ps"], 1)
                if k in (0, 3) and live(ta, mid):
                    wait(pe, "v_sb", k, ta)
                    if k == 0:
                        project_rows(bank[3][:, 0:D], W["Wv0"], CT[:, u, :, :]).then_inc(s["v_ps"], 1)
                    else:
                        project_rows(bank[3][:, 0:D], W["Wv3"], XT[:, u, :, :]).then_inc(s["v_ps"], 1)
                if live(tv, mid):
                    wait(pe, "pt_sb", k, tv + 1)
                    wait_dma(pe, "vb", k, at, -2)
                    wait(pe, "o_sb", k, tv)
                    for g in range(4):
                        for b in range(BT):
                            last = mm(bank[6][32 * b:32 * b + 32, g * 64:(g + 1) * 64], PT[:, u, g, 32 * b:32 * b + 32],
                                      VB[:, u, b, :, g * HD:(g + 1) * HD], start=True, stop=True,
                                      skip_group_check=True)
                    if k != 1:
                        for g in range(4):
                            last = mm(bank[6][:, D + 4 * g:D + 4 * g + 4], PT[:, u, g, :], const("block_ones"),
                                      start=True, stop=True, skip_group_check=True)
                    last.then_inc(s["o_ps"], 1)
                if k == 2 and live(ta, mid):
                    wait(pe, "mt_sb", 2, ta + 1)
                    wait(pe, "q_sb", 2, min(ta + 2, NT) if not mid else ta + 2)
                    project(bank[1][:, 2 * P:4 * P], W["Wk2"], CT[:, u, :, :]).then_inc(s["k_ps"], 1)
                if k == 2 and live(tc, mid):
                    wait(pe, "q_sb", 2, tc + 1)
                    wait_dma(pe, "cxt", 2, at, 1)
                    wait(pe, "idx", 2, tc)
                    for c in range(C2):
                        for b in range(BT):
                            last = mm(bank[2][32 * b:32 * b + 32, 0:S], QK[:, 1 - u, c, 32 * b:32 * b + 32],
                                      CXT[:, 1 - u, c, b, :], start=(c == 0), stop=(c == 1), skip_group_check=True)
                    last.then_inc(s["cs_ps"], 1)
                if k == 2 and live(ta, mid):
                    wait(pe, "v_sb", 2, ta)
                    project_rows(bank[3][:, 0:D], W["Wv2"], CT[:, u, :, :]).then_inc(s["v_ps"], 1)

            def route_step(m, at):
                st, u, mid = at.st, at.u, at.mid
                q = ms[m]
                if live(st, mid):
                    need(pe, q["xn"], st + 1)
                    need(pe, q["xta"] if m == 0 else q["xt_sb"], st)
                    transpose_tile(bank[0][:, 0:2 * P], XN[:, u, :]).then_inc(q["xt_ps"], 1)
                    need(pe, q["xt_sb"], st + 1)
                    need(pe, q["lg_sb"], st)
                    project_rows(bank[1][:, 0:MOE[m]["E"]], Wr[m], XT[:, u, :, :], br[m][:], MOE[m]["E"]
                                 ).then_inc(q["lg_ps"], 1)

            def shared_group(g, first):
                pe.wait_ge(ms[0]["xta"], 4 * g + 4)
                for j in range(4):
                    if not (first and j < 2):
                        pe.wait_ge(sh["gate"], 4 * g + j - 1)
                    for c in range(C2):
                        last = mm(bank[4 + j % 2][:], Ws1[:, c, HS + j * P:HS + (j + 1) * P], XTA[:, c, span(g, 512)],
                                  start=(c == 0), stop=(c == 1))
                    last.then_inc(sh["g_ps"], 1)
                    if not (first and j < 2):
                        pe.wait_ge(sh["hid"], 4 * g + j - 1)
                    for c in range(C2):
                        last = mm(bank[2 + j % 2][:], Ws1[:, c, j * P:(j + 1) * P], XTA[:, c, span(g, 512)],
                                  start=(c == 0), stop=(c == 1))
                    last.then_inc(sh["a_ps"], 1)
                pe.wait_ge(sh["hid"], 4 * g + 4)
                for t in range(4):
                    if not (first and t < 2):
                        pe.wait_ge(sh["res"], 4 * g + t - 1)
                    dst = bank[6 + t % 2][:, 0:D]
                    for j in range(4):
                        last = mm(dst, SH[:, j, t * P:(t + 1) * P], Ws2[:, j, :], start=(j == 0), stop=(j == 3))
                    last.then_inc(sh["y_ps"], 1)

            def expert_step(m, at):
                st, u, mid = at.st, at.u, at.mid
                q, n, R, hid = ms[m], MOE[m]["n"], MOE[m]["R"], MOE[m]["hid"]
                if live(st + 1, mid, n):
                    pe.wait_ge(q["xs"][1 - u], 16 * (at.half(1) + 1))
                    need(pe, q["t_sb"], st + 1)
                    transpose_tile(bank[0][:, 0:2 * P], XS[:, 1 - u, :]).then_inc(q["t_ps"], 1)
                if live(st, mid, n):
                    pe.wait_ge(q["w1"][u], 16 * (at.half(0) + 1))
                    need(pe, q["t_sb"], st + 1)
                    for r in range(R):
                        par = (R * u + r) % 2
                        for half, bk, freed, sem in ((1, 1 + par, "gate_sb", "g_ps"),
                                                     (0, 3 + par, "hid" if m == 0 else "u", "a_ps")):
                            need(pe, q[freed], R * st + r - 1)
                            for i in range(2):
                                for c in range(C2):
                                    col = c * 2 * hid + half * hid + (2 * r + i) * P
                                    last = mm(bank[bk][:, i * P:(i + 1) * P], W1[:, u, col:col + P], XT[:, u, c, :],
                                              start=(c == 0), stop=(c == 1))
                            last.then_inc(q[sem], 1)
                if live(st - 1, mid, n):
                    pe.wait_ge(q["w2"][1 - u], 16 * (at.half(-1) + 1))
                    need(pe, q["hid"], R * st)
                    need(pe, q["y_sb"], st - 2)
                    dst = bank[5 + (1 - u)][:, 0:D]
                    for j in range(2 * R):
                        last = mm(dst, HB[:, 1 - u, j, :], W2[:, 1 - u, j * D:(j + 1) * D], start=(j == 0),
                                  stop=(j == 2 * R - 1))
                    last.then_inc(q["y_ps"], 1)

            def final_step(at):
                st, u, mid = at.st, at.u, at.mid
                if live(st, mid):
                    need(pe, ms[1]["mix"], 2 * (st + 1))
                    need(pe, fin["xt_sb"], st)
                    transpose_tile(bank[0][:, 0:2 * P], XN[:, u, :]).then_inc(fin["xt_ps"], 1)
                    need(pe, fin["xt_sb"], st + 1)
                    need(pe, fin["out"], st)
                    project_rows(bank[1][:, 0:D], Wf, XT[:, u, :, :]).then_inc(fin["y_ps"], 1)

            def moe(m):
                q, E = ms[m], MOE[m]["E"]
                pe.wait_ge(s_load[2], 16 * len(MLP_LOADS))
                token_steps(pe, lambda at: route_step(m, at))
                pe.wait_ge(q["onehot"], 1)
                mm(bank[2][:, 0:NT * E], const("before"), RC[:, :, 0:E], start=True, stop=True)
                mm(bank[3][:, 0:NT * E], ones_sq[:], RC[:, :, 0:E], start=True, stop=True).then_inc(q["rank_ps"], 1)
                if m == 0:
                    pe.wait_ge(q["pos"], 2)
                    shared_group(0, True)
                    with pe.Fori(1, 4) as g:
                        shared_group(g, False)
                row_steps(pe, MOE[m]["n"], -1, lambda at: expert_step(m, at))
                if m == 1:
                    token_steps(pe, final_step)

            for name in plan:
                k = int(name[1])
                if name[0] == "A":
                    if k >= 2:
                        pe.wait_ge(s_load[1], 16 * len(wname[4:8] if k == 2 else wname[4:]))
                    steps(pe, k, lambda at: attention_step(k, at))
                else:
                    moe(k)

    return nc


def kernel(**inputs):
    import concourse.bacc as bacc
    from concourse.bass_utils import run_bass_kernel_spmd as run

    g = {k: np.asarray(v) for k, v in inputs.items()}

    def chunks(w):
        return w.reshape(-1, P, w.shape[-1]).transpose(1, 0, 2)

    ctx = g["ctx_1024"]
    swap = np.arange(D) ^ 1
    v_order = np.arange(D).reshape(4, 4, HD).transpose(1, 0, 2).reshape(-1)
    kv = g["L1_xattn_Wkv"]
    arrays = {
        "cst": CONST,
        "x": g["x"].reshape(NT, P, D).transpose(1, 0, 2),
        "ctx32": ctx[:, :T, :].reshape(NT, P, C2, P).transpose(3, 0, 2, 1),
        "ctxT": ctx.reshape(NT, BT, S, C2, P).transpose(4, 0, 3, 1, 2),
        "ctx_rows": ctx.reshape(B * S, D),
        "Wq0": chunks(g["L0_xattn_Wq"]), "Wk0": chunks(g["L0_xattn_Wk"]), "Wv0": chunks(g["L0_xattn_Wv"][:, v_order]),
        "Wo0": chunks(g["L0_xattn_Wo"]),
        "qk_bias": np.concatenate([g["L0_xattn_bq"].reshape(C2, P), g["L0_xattn_bk"].reshape(C2, P)]).T,
        "rows0": np.stack([g["L0_xattn_bv"][v_order], g["L0_xattn_bo"]])[None],
        "sign_cols": np.stack([g["L0_attn_bv_q"].reshape(C2, P), g["L0_attn_bv_k"].reshape(C2, P)]).transpose(2, 0, 1),
        "sign_v": g["L0_attn_bv_v"].reshape(1, D),
        "Wq2": chunks(g["L1_xattn_Wq"].T), "Wk2": chunks(np.tile(kv[:HD].T, (1, H))),
        "Wv2": chunks(np.tile(kv[HD:].T, (1, H))), "Wo2": chunks(g["L1_xattn_Wc"].T),
        "Wq3": chunks(g["L1_attn_Wq"]), "Wk3": chunks(g["L1_attn_Wk"]),
        "Wqs3": chunks(g["L1_attn_Wq"][:, swap]), "Wks3": chunks(g["L1_attn_Wk"][:, swap]),
        "Wv3": chunks(g["L1_attn_Wv"][:, v_order]), "Wo3": chunks(g["L1_attn_Wo"]),
        "Wr0": chunks(g["L0_ffn_Wr"]), "br0": g["L0_ffn_br"][None], "Wr1": chunks(g["L1_ffn_Wg"]), "br1": g["L1_ffn_bg"][None],
        "Ws1": chunks(g["L0_ffn_Ws1"]), "Ws2": chunks(g["L0_ffn_Ws2"]), "bs1": g["L0_ffn_bs1"].reshape(-1, P).T,
        "bs2": g["L0_ffn_bs2"][None],
        "Wf": chunks(g["L1_ffn_Wf"]), "bf": g["L1_ffn_bf"][None],
    }

    def expert_weights(first, bias):
        e, _, n = first.shape
        w = first.reshape(e, C2, P, n).transpose(0, 2, 1, 3).reshape(e, P, C2 * n)
        return np.concatenate([w, bias.reshape(e, n // P, P).transpose(0, 2, 1)], axis=2)

    arrays["W1_0"] = expert_weights(g["L0_ffn_We1"], g["L0_ffn_be1"])
    arrays["W1_1"] = expert_weights(np.concatenate([g["L1_ffn_W3"], g["L1_ffn_W1"]], axis=2),
                                    np.concatenate([g["L1_ffn_b3"], g["L1_ffn_b1"]], axis=1))
    for m, w in enumerate((g["L0_ffn_We2"], g["L1_ffn_W2"])):
        arrays[f"W2_{m}"] = w.reshape(w.shape[0], -1, P, D).transpose(0, 2, 1, 3).reshape(w.shape[0], P, -1)
    arrays["b2_0"], arrays["b2_1"] = g["L0_ffn_be2"], g["L1_ffn_b2"]

    nc = bacc.Bacc("TRN2", target_bir_lowering=False, num_devices=1)
    arrays = {k: np.ascontiguousarray(v) for k, v in arrays.items()}
    aps = {k: nc.dram_tensor(f"in_{k}", v.shape, mybir.dt.from_np(v.dtype), kind="ExternalInput").ap()
           for k, v in arrays.items()}
    out = nc.dram_tensor("out", (P, NT, D), F32, kind="ExternalOutput").ap()
    build(nc, aps, out)
    r = run(nc, [{f"in_{k}": v for k, v in arrays.items()}], core_ids=[0])
    return r.results[0]["out"].transpose(1, 0, 2).reshape(B, T, D)
```

```python
from contextlib import ExitStack

import numpy as np
import concourse.bass as bass
from concourse import mybir

F32 = mybir.dt.float32
BF16 = mybir.dt.bfloat16
I32 = mybir.dt.int32
U32 = mybir.dt.uint32
ALU = mybir.AluOpType
ACT = mybir.ActivationFunctionType
AX = mybir.AxisListType

B, T, D = 64, 32, 256
S = 257
H, HD = 16, 16
P = 128
NT = B * T // P
BT = P // T
C2 = D // P
HC = P // HD
EPS = 1e-5
NEG = -1e30
E0, HR, HS = 12, 768, 512
E1, HX = 8, 512
PAIRS = 2 * B * T
M0_TILES = PAIRS // P + E0
M1_TILES = PAIRS // P + E1
TAU = 1.5


def constants():
    p = np.arange(P)
    ident = np.eye(P, dtype=np.float32)
    head_mask = (p[:, None] // HD == np.arange(HC)[None, :]).astype(np.float32)
    block_ones = (p[:, None] // T == np.arange(BT)[None, :]).astype(np.float32)
    key, tok = np.arange(T)[None, :], (p % T)[:, None]
    causal = np.tile(np.where(key <= tok, 0.0, NEG).astype(np.float32), (1, H))
    before = (p[:, None] < p[None, :]).astype(np.float32)
    dd = p % HD
    inv = (np.float32(1.0) / np.float32(10000.0) ** (np.arange(0, HD, 2, dtype=np.float32) / np.float32(HD))).astype(np.float32)
    ang = np.arange(T, dtype=np.float32)[None, :] * inv[dd // 2][:, None]
    cos = np.cos(ang).astype(np.float32)
    sin = (np.sin(ang) * np.where(dd % 2 == 0, -1.0, 1.0)[:, None]).astype(np.float32)
    row0 = ((np.arange(NT)[None, :] * BT + (p // T)[:, None]) * S).astype(np.float32)
    experts = np.zeros((P, E0, E0), np.float32)
    experts[:] = np.tril(np.ones((E0, E0), np.float32))[None]
    ranks = np.broadcast_to(np.concatenate([E0 - np.arange(E0), 1.0 + np.arange(E1)]).astype(np.float32), (P, E0 + E1))
    slots = np.broadcast_to(np.arange(M0_TILES, dtype=np.float32), (P, M0_TILES))
    cols = [("ident", ident), ("head_mask", head_mask), ("block_ones", block_ones), ("causal", causal),
            ("before", before), ("cos", cos), ("sin", sin), ("row0", row0), ("tril", experts.reshape(P, -1)),
            ("ranks", ranks), ("slots", slots)]
    at, where = 0, {}
    for name, a in cols:
        where[name] = (at, at + a.shape[1])
        at += a.shape[1]
    return np.ascontiguousarray(np.concatenate([a for _, a in cols], axis=1)), where


CONST, WHERE = constants()

ATTN = (0, 1, 2, 3)
USES = {
    "stat": ATTN, "mv": ATTN, "var": ATTN, "rstd": ATTN, "xn": ATTN, "xt_ps": ATTN, "xt_sb": ATTN,
    "ctx": (0,), "bias": (0,), "qk_ps": (0, 3), "q_ps": (2,), "q_sb": (2,), "k_ps": (2,), "qk_sb": (0, 2, 3), "rope": (3,),
    "v_ps": (0, 2, 3), "v_sb": ATTN, "vb": ATTN, "kb": ATTN, "kb1": ATTN, "sc_ps": ATTN, "mx": (0, 2, 3), "sub": (0, 2, 3),
    "prob": ATTN, "pt_ps": ATTN, "pt_sb": ATTN, "o_ps": ATTN, "rc": (0, 2, 3), "o_sb": (0, 2, 3),
    "ot_ps": (0, 2, 3), "ot_sb": (0, 2, 3), "y_ps": (0, 2, 3), "res": ATTN, "vd": ATTN,
    "cxt": (2,), "cs_ps": (2,), "top": (2,), "idx": (2,), "row": (2,), "mem": (2,), "mt_ps": (2,), "mt_sb": (2,),
}
PER = {"ctx": 16, "cxt": 16, "vd": 16, "vb": 64, "mem": 16}
NORM_TILES = ((0, 4), (4, NT))
LOOP_FROM = 4


def build(nc, a, out):
    ctx = ExitStack()
    with ctx:
        def sb(name, shape, dt=F32):
            return ctx.enter_context(nc.sbuf_tensor(name, shape, dt))

        def psum(name, shape, dt=F32):
            return ctx.enter_context(nc.psum_tensor(name, shape, dt))

        def new_sem(name):
            return ctx.enter_context(nc.semaphore(name))

        sorted_rows = [nc.dram_tensor(f"sorted_rows{m}", (n * P, D), F32).ap() for m, n in enumerate((M0_TILES, M1_TILES))]
        expert_rows = [nc.dram_tensor(f"expert_rows{m}", (n * P, D), F32).ap() for m, n in enumerate((M0_TILES, M1_TILES))]

        v_rows = nc.dram_tensor("v_rows", (2, P, D), F32).ap()

        cst = sb("cst", [P, CONST.shape[1]])

        def const(name, parts=P):
            lo, hi = WHERE[name]
            return cst[0:parts, lo:hi]

        X = sb("X", [P, NT, D])
        XN = sb("XN", [P, 2, D])
        XT = sb("XT", [P, 2, C2, P])
        QK = sb("QK", [P, 2, 4, P])
        KB = sb("KB", [P, 2, C2, HC, P])
        VS = sb("VS", [P, 2, D])
        VB = sb("VB", [P, 2, BT, 4, 64])
        PR = sb("PR", [P, 2, H * T])
        PT = sb("PT", [P, 2, 4, P])
        OS = sb("OS", [P, 2, D])
        OT = sb("OT", [P, C2, P])
        CT = sb("CT", [P, 2, C2, P])
        CXT = sb("CXT", [P, 2, C2, BT, S])
        MEM = sb("MEM", [P, 2, D])
        RT = sb("RT", [P, 2, 4 * P])
        stats = sb("stats", [P, 2, 6])
        mv = sb("mv", [P, 2, 2])
        var = sb("var", [P, 2, 1])
        rstd = sb("rstd", [P, 2, 1])
        minus_half = sb("minus_half", [P, 1])
        mx = sb("mx", [P, H])
        rc = sb("rc", [P, H])
        hold = sb("hold", [P, 1])
        stats_all = sb("stats_all", [P, NT, 6])
        mv_all = sb("mv_all", [P, NT, 2])
        var_all = sb("var_all", [P, NT])
        rstd_all = sb("rstd_all", [P, NT])
        top8 = sb("top8", [P, 8])
        idx8 = sb("idx8", [P, 8], U32)
        row = sb("row", [P, 2], I32)
        ident_bf = sb("ident_bf", [P, P], BF16)
        causal_bf = sb("causal_bf", [P, H * T], BF16)
        sign_cols = sb("sign_cols", [P, 2, C2])
        sign_qk = sb("sign_qk", [P, C2])
        sign_mask = sb("sign_mask", [P, C2, HC])
        sign_v = sb("sign_v", [P, D])
        wname = ["Wq0", "Wk0", "Wv0", "Wo0", "Wq2", "Wk2", "Wv2", "Wo2", "Wq3", "Wk3", "Wqs3", "Wks3", "Wv3", "Wo3"]
        first_w = sb("first_w", [P, 4, C2, D])
        W = {n: first_w[:, i] for i, n in enumerate(wname[:4])} | {n: sb(n, [P, C2, D])[:] for n in wname[4:]}
        qk_bias = sb("qk_bias", [P, 4])
        rows0 = sb("rows0", [P, 2, D])
        XNA = sb("XNA", [P, NT, D])
        LG = sb("LG", [P, NT, E0])
        Wr = [sb(f"Wr{m}", [P, C2, e]) for m, e in enumerate((E0, E1))]
        br = [sb(f"br{m}", [P, e]) for m, e in enumerate((E0, E1))]
        wts = sb("wts", [P, 2, NT])
        pos = sb("pos", [P, 2, NT], I32)
        slot_e = sb("slot_e", [1, M0_TILES], I32)
        zeros = sb("zeros", [P, D])
        W1F, W1X = C2 * 2 * HR + 2 * HR // P, C2 * 2 * HX + 2 * HX // P
        W1 = sb("W1", [P, 2, max(W1F, W1X)])
        W2 = sb("W2", [P, 2, HR // P * D])
        b2 = sb("b2", [P, 2, D])
        XS = sb("XS", [P, 2, D])
        GS = sb("GS", [P, 2, 2, P])
        HB = sb("HB", [P, 2, HR // P, P])
        YS = sb("YS", [P, 2, D])
        GY = sb("GY", [P, 2, 2, D])
        Wf = sb("Wf", [P, C2, D])
        bf = sb("bf", [P, D])
        XTA = CXT[:].rearrange("p a c b s -> p (a c b s)")[:, 0:C2 * NT * P].rearrange("p (c n) -> p c n", c=C2)
        Ws1 = first_w[:].rearrange("p i c n -> p (i c n)").rearrange("p (c n) -> p c n", c=C2)
        Ws2 = sb("Ws2", [P, HS // P, D])
        bs1 = sb("bs1", [P, 2 * HS // P])
        bs2 = sb("bs2", [P, D])
        kb_flat = KB[:].rearrange("p a c h n -> p (a c h n)")
        SG = kb_flat[:, 0:1024].rearrange("p (a n) -> p a n", a=2)
        SH = kb_flat[:, 1024:1024 + 4 * HS].rearrange("p (a n) -> p a n", n=512)
        pt_flat, pr_flat = PT[:].rearrange("p a g n -> p (a g n)"), PR[:].rearrange("p a n -> p (a n)")

        def scratch(buf, at, n, e):
            return buf[:, at:at + n * e].rearrange("p (n e) -> p n e", e=e)

        RA, RB, RO = (scratch(pt_flat, i * NT * E0, NT, E0) for i in range(3))
        RX = scratch(pt_flat, 3 * NT * E0, E0, E0)
        RE = scratch(pr_flat, 0, M0_TILES, E0)
        RM = sb("RM", [P, 2, NT, E0])
        RC = sb("RC", [P, NT, E0])
        r16 = [sb(f"r16_{i}", [P, NT]) for i in range(4)]
        re_ = [sb(f"re_{i}", [P, E0]) for i in range(3)]
        rei = sb("rei", [P, E0], I32)
        rsl = sb("rsl", [P, M0_TILES])

        ones_sq = sb("ones_sq", [P, P])
        MLP_LOADS = ((Wr[0][:], "Wr0"), (br[0][:], "br0"), (Wr[1][:], "Wr1"), (br[1][:], "br1"), (Ws2[:], "Ws2"),
                     (bs1[:], "bs1"), (bs2[:], "bs2"), (Wf[:], "Wf"), (bf[:], "bf"), (Ws1, "Ws1"))

        bank = [psum(f"bank{i}", [P, 512]) for i in range(8)]

        s = {n: [new_sem(f"s_{n}{i}") for i in range(2)] if n in PER else new_sem("s_" + n) for n in USES}

        def need(eng, sem, v):
            if not isinstance(v, int) or v > 0:
                eng.wait_ge(sem, v)

        def n_before(name, k):
            return NT * len([q for q in USES[name] if q < k])

        def wait(eng, name, k, count):
            need(eng, s[name], n_before(name, k) + count)

        def dma_count(name, k, at, d):
            return (n_before(name, k) // 2 + at.half(d) + 1) * PER[name]

        def wait_dma(eng, name, k, at, d):
            need(eng, s[name][at.par(d)], dma_count(name, k, at, d))

        s_load = [new_sem(f"s_load{i}") for i in range(3)]
        s_prep = new_sem("s_prep")
        s_sign = new_sem("s_sign")
        s_clear = new_sem("s_clear")
        s_zero_rows = new_sem("s_zero_rows")
        s_route_step = new_sem("s_route_step")
        s_x = [new_sem(f"s_x{i}") for i in range(4)]

        PAIRED = ["xs", "w1", "w2", "b2", "y_out", "gy"]
        MSEM = ["stat", "mv", "var", "rstd", "xn", "xt_ps", "xt_sb", "xna", "xta", "lg_ps", "lg_sb", "gate", "gate_e", "onehot", "rank_ps",
                "pos", "scat", "xs", "w1", "w2", "b2", "t_ps", "t_sb", "g_ps", "a_ps", "gate_sb", "u", "hid", "y_ps", "y_sb",
                "y_out", "gy", "mix"]
        ms = [{n: [new_sem(f"m{m}_{n}{i}") for i in range(2)] if n in PAIRED else new_sem(f"m{m}_{n}") for n in MSEM}
              for m in range(2)]
        sh = {n: new_sem("sh_" + n) for n in ("g_ps", "a_ps", "gate", "hid", "y_ps", "bias", "res")}
        fin = {n: new_sem("fin_" + n) for n in ("bias", "xt_ps", "xt_sb", "y_ps", "out", "dma")}

        def tiles_of(k, st):
            return (st + 2, st + 1, st, st - 1, st - 2, st - 3) if k == 2 else (st + 1, None, st, st - 1, st - 2, st - 3)

        class At:

            def __init__(self, st, u, h, mid):
                self.st, self.u, self.h, self.mid = st, u, h, mid

            def half(self, d):
                return self.h + (self.u + d) // 2

            def par(self, d):
                return (self.u + d) % 2

        def alone(body, *sts):
            for st in sts:
                body(At(st, st % 2, st // 2, False))

        def run_steps(eng, first, end, body, loop_end):
            alone(body, *range(first, LOOP_FROM))
            with eng.Fori(0, (loop_end - LOOP_FROM) // 2) as j:
                for u in range(2):
                    body(At(LOOP_FROM + 2 * j + u, u, LOOP_FROM // 2 + j, True))
            alone(body, *range(loop_end, end))

        def attention_pair(eng, k, body, loops=True):
            first = -2 if k == 2 else -1
            if loops:
                run_steps(eng, first, NT - 2, lambda at: body(k, at), NT - 2)
            else:
                alone(lambda at: body(k, at), *range(first, NT - 2))
            for i in range(-2, 3):
                alone(lambda at: body(k, at), NT + i)
                if i >= -1:
                    alone(lambda at: body(k + 1, at), i)
            run_steps(eng, 3, NT + 3, lambda at: body(k + 1, at), NT - 2)

        def row_steps(eng, n, first, body):
            run_steps(eng, first, n + 1, body, n - 2)

        def token_steps(eng, body, first=0, end=NT):
            run_steps(eng, first, end, body, NT - 2)

        def live(t, mid, n=NT):
            return t is not None and (mid or 0 <= t < n)

        def row_tile(at, d, n):
            return at.par(d) * (n // 2) + at.half(d)

        def one(t):
            return bass.ds(t, 1)

        def span(t, w):
            return bass.ds(t * w, w)

        MOE = [dict(E=E0, n=M0_TILES, hid=HR, R=HR // P // 2, W1=a["W1_0"], W2=a["W2_0"], b2=a["b2_0"]),
               dict(E=E1, n=M1_TILES, hid=HX, R=HX // P // 2, W1=a["W1_1"], W2=a["W2_1"], b2=a["b2_1"])]

        block = ctx.enter_context(nc.Block())

        @block.sync
        def _(sp):
            sp.dma_start(X[:, 0:4, :], a["x"][:, 0:4, :]).then_inc(s_x[0], 16)
            sp.dma_start(cst[:], a["cst"]).then_inc(s_load[0], 16)
            for n in wname[:4]:
                sp.dma_start(W[n], a[n]).then_inc(s_load[0], 16)
            sp.dma_start(qk_bias[:], a["qk_bias"]).then_inc(s_load[0], 16)
            sp.dma_start(rows0[:], a["rows0"].to_broadcast([P, 2, D])).then_inc(s_load[0], 16)
            sp.dma_start(sign_cols[:], a["sign_cols"]).then_inc(s_load[0], 16)
            sp.dma_start(sign_v[:], a["sign_v"].to_broadcast([P, D])).then_inc(s_load[0], 16)
            for q in range(1, 4):
                sp.dma_start(X[:, 4 * q:4 * q + 4, :], a["x"][:, 4 * q:4 * q + 4, :]).then_inc(s_x[q], 16)

            def ahead(v):
                return v if isinstance(v, int) else sp.to_reg(v)

            def attention_step(k, at):
                st, u, mid = at.st, at.u, at.mid
                tf, tc, ta, tb, tv, to = tiles_of(k, st)
                if live(ta, mid):
                    n_source, n_used = ahead(n_before("v_sb", k) + ta + 1), ahead(n_before("o_ps", k) + ta - 1)
                    n_stored, n_spread = ahead(dma_count("vd", k, at, 0)), ahead(dma_count("vb", k, at, -2))
                if k == 0 and live(tf, mid):
                    wait(sp, "v_ps", 0, tf - 1)
                    sp.dma_start(CT[:, 1 - u, :, :], a["ctx32"][:, one(tf), :, :]).then_inc(s["ctx"][at.par(1)], 16)
                if k == 2 and live(tf, mid):
                    wait(sp, "cs_ps", 2, tf - 1)
                    sp.dma_start(CXT[:, u, :, :, :], a["ctxT"][:, one(tf), :, :, :]).then_inc(s["cxt"][u], 16)
                if live(ta, mid):
                    need(sp, s["v_sb"], n_source)
                    need(sp, s["vb"][u], n_spread)
                    sp.dma_start(v_rows[u], VS[:, u, :]).then_inc(s["vd"][u], 16)
                    need(sp, s["vd"][u], n_stored)
                    need(sp, s["o_ps"], n_used)
                    for h in range(4):
                        sp.dma_start(VB[32 * h:32 * h + 32, u, :, h, :],
                                     v_rows[u].rearrange("(b k) (h e) -> h k b e", b=BT, h=4)[h]).then_inc(s["vb"][u], 16)

            def expert(m, t):
                return sp.value_load(slot_e[0:1, one(t)], min_val=0, max_val=MOE[m]["E"] - 1)

            def load_if_new(e, held, dst, table, sem):
                def load():
                    sp.dma_start(dst, table[one(e), :, :]).then_inc(sem, 16)

                if held is None:
                    load()
                else:
                    with sp.If(e != held):
                        load()
                    with sp.Else():
                        sp.sem_inc(sem, 16)

            def expert_step(m, at):
                st, u, mid = at.st, at.u, at.mid
                q, n = ms[m], MOE[m]["n"]
                if live(st + 1, mid, n):
                    e_next = expert(m, row_tile(at, 1, n))
                    e_next_held = expert(m, row_tile(at, 1, n) - 1) if mid or st + 1 >= 2 else None
                    n_first, n_rows = ahead(MOE[m]["R"] * st), ahead(st + 1)
                if live(st, mid, n):
                    e_this = expert(m, row_tile(at, 0, n))
                    e_this_held = expert(m, row_tile(at, 0, n) - 1) if mid or st >= 2 else None
                if live(st + 1, mid, n):
                    need(sp, q["hid" if m == 0 else "u"], n_first)
                if live(st + 2, mid, n):
                    n_rows = n_rows if live(st + 1, mid, n) else st + 1
                    need(sp, q["t_ps"], n_rows)
                    sp.dma_start(XS[:, u, :], sorted_rows[m].rearrange("(n p) d -> p n d", p=P)[:, one(row_tile(at, 2, n)), :]
                                 ).then_inc(q["xs"][u], 16)
                if live(st + 1, mid, n) and (mid or st >= 0):
                    load_if_new(e_next, e_next_held, W1[:, 1 - u, 0:MOE[m]["W1"].shape[2]], MOE[m]["W1"], q["w1"][1 - u])
                if live(st, mid, n):
                    need(sp, q["y_sb"], st - 1)
                    sp.dma_start(b2[:, u, :], MOE[m]["b2"][one(e_this), :].to_broadcast([P, D])).then_inc(q["b2"][u], 16)
                    load_if_new(e_this, e_this_held, W2[:, u, 0:MOE[m]["W2"].shape[2]], MOE[m]["W2"], q["w2"][u])
                if live(st - 2, mid, n):
                    sp.wait_ge(q["y_sb"], st - 1)
                    sp.dma_start(expert_rows[m].rearrange("(n p) d -> p n d", p=P)[:, one(row_tile(at, -2, n)), :], YS[:, u, :]
                                 ).then_inc(q["y_out"][u], 16)

            def experts(m):
                q, n = ms[m], MOE[m]["n"]
                sp.wait_ge(q["pos"], 3)
                load_if_new(expert(m, 0), None, W1[:, 0, 0:MOE[m]["W1"].shape[2]], MOE[m]["W1"], q["w1"][0])
                sp.wait_ge(q["scat"], 32 * NT)
                row_steps(sp, n, -2, lambda at: expert_step(m, at))
                sp.wait_ge(q["y_sb"], n)
                sp.dma_start(expert_rows[m].rearrange("(n p) d -> p n d", p=P)[:, n - 1:n, :], YS[:, (n - 1) % 2, :]
                             ).then_inc(q["y_out"][(n - 1) % 2], 16)

            for m in range(2):
                attention_pair(sp, 2 * m, attention_step)
                experts(m)
            sp.wait_ge(fin["out"], 1)
            with sp.Fori(1, NT + 1) as t1:
                sp.wait_ge(fin["out"], t1)
                sp.dma_start(out[:, one(t1 - 1), :], X[:, one(t1 - 1), :]).then_inc(fin["dma"], 16)
            sp.wait_ge(fin["dma"], 16 * NT)

        @block.gpsimd
        def _(pool):
            nc.gpsimd.memset(minus_half[:], -0.5).then_inc(s_clear, 1)
            nc.gpsimd.memset(zeros[:], 0.0).then_inc(s_clear, 1)
            nc.gpsimd.memset(VB[:], 0.0).then_inc(s_clear, 1)
            nc.gpsimd.memset(ones_sq[:], 1.0).then_inc(s_clear, 1)
            pool.wait_ge(s_clear, 4)

            def root(sem_in, sem_out, sems, base, t, par):
                need(pool, sems[sem_in], base + t + 1)
                nc.gpsimd.tensor_tensor(rstd[:, par, :], var[:, par, :], minus_half[:], ALU.pow).then_inc(sems[sem_out], 1)

            def attention_step(k, at):
                st, u, mid = at.st, at.u, at.mid
                tf, tc, ta, tb, tv, to = tiles_of(k, st)
                if live(tf, mid):
                    root("var", "rstd", s, n_before("var", k), tf, u if k == 2 else 1 - u)
                if k == 0 and not mid and st == 0:
                    pool.wait_ge(s_load[0], 16 * 9)
                    pool.wait_ge(s_sign, 2)
                if k == 0 and live(ta, mid):
                    if not mid:
                        wait(pool, "xn", 0, ta + 1)
                    nc.gpsimd.tensor_tensor(X[:, one(ta), :], X[:, one(ta), :], rows0[:, 1, :].unsqueeze(1), ALU.add
                                            ).then_inc(s["bias"], 1)
                if k == 1 and live(ta, mid):
                    wait(pool, "xn", 1, ta + 1)
                    wait_dma(pool, "vd", 1, at, -2)
                    nc.gpsimd.tensor_tensor(VS[:, u, :].rearrange("p (h g d) -> p h g d", h=4, g=4),
                                            XN[:, u, :].rearrange("p (g h d) -> p h g d", g=4, h=4),
                                            sign_v[:].rearrange("p (g h d) -> p h g d", g=4, h=4), ALU.mult
                                            ).then_inc(s["v_sb"], 1)
                if k == 3 and live(ta, mid):
                    wait(pool, "rope", 3, ta + 1)
                    nc.gpsimd.tensor_tensor(QK[:, u, :, :].rearrange("p a n -> p (a n)"), RT[:, 0, :], RT[:, 1, :],
                                            ALU.add).then_inc(s["qk_sb"], 1)
                if k == 2 and live(tf + 1, mid):
                    gather_results(0, tf + 1)
                if k == 2 and live(tc, mid):
                    wait(pool, "row", 2, tc + 1)
                    nc.gpsimd.indirect_dma_start(
                        out=MEM[:, 1 - u, :], out_offset=None, in_=a["ctx_rows"],
                        in_offset=bass.IndirectOffsetOnAxis(ap=row[:, 1 - u:2 - u], axis=0)).then_inc(s["mem"][1 - u], 16)

            def gather_results(m, t):
                q = ms[m]
                if t >= 2:
                    pool.wait_ge(q["mix"], 2 * (t - 1))
                for c in range(2):
                    nc.gpsimd.indirect_dma_start(
                        out=GY[:, t % 2, c, :], out_offset=None, in_=expert_rows[m],
                        in_offset=bass.IndirectOffsetOnAxis(ap=pos[:, c, t:t + 1], axis=0)).then_inc(q["gy"][t % 2], 16)

            def moe(m):
                q = ms[m]
                for part, (t0, t1) in enumerate(NORM_TILES):
                    pool.wait_ge(q["var"], part + 1)
                    nc.gpsimd.tensor_tensor(rstd_all[:, t0:t1], var_all[:, t0:t1], minus_half[:].to_broadcast([P, t1 - t0]),
                                            ALU.pow).then_inc(q["rstd"], 1)
                pool.wait_ge(q["xna"], NT)
                pool.wait_ge(s_zero_rows, 32 * NT)
                for c in range(2):
                    pool.wait_ge(q["pos"], c + 1)
                    for t in range(NT):
                        nc.gpsimd.indirect_dma_start(
                            out=sorted_rows[m], out_offset=bass.IndirectOffsetOnAxis(ap=pos[:, c, t:t + 1], axis=0),
                            in_=XNA[:, t, :], in_offset=None).then_inc(q["scat"], 16)
                for par in range(2):
                    pool.wait_ge(q["y_out"][par], 8 * MOE[m]["n"])
                for t in range(1 if m == 0 else NT):
                    gather_results(m, t)

            for m in range(2):
                attention_pair(pool, 2 * m, attention_step, loops=(m == 0))
                moe(m)

        @block.scalar
        def _(act):
            act.wait_ge(s_load[0], 16 * 9)
            act.wait_ge(s_clear, 4)
            nc.scalar.activation(sign_cols[:], sign_cols[:], ACT.Sign).then_inc(s_sign, 1)
            nc.scalar.activation(sign_v[:], sign_v[:], ACT.Sign).then_inc(s_sign, 1)

            def weight_loads():
                for n in wname[4:]:
                    act.dma_start(W[n], a[n]).then_inc(s_load[1], 16)

            def mlp_loads(loads):
                for dst, n in loads:
                    src = a[n].to_broadcast(list(dst.shape)) if n in ("bs2", "bf", "br0", "br1") else a[n]
                    act.dma_start(dst, src).then_inc(s_load[2], 16)

            def zero_sorted_rows(m, at):
                rows = sorted_rows[m].rearrange("(t p j) d -> p t j d", t=NT, p=32)
                j = MOE[m]["n"] * P // NT // 32
                act.dma_start(rows[:, one(at.st), :, :].rearrange("p t j d -> p (t j) d"),
                              zeros[0:32, None, :].to_broadcast([32, j, D])).then_inc(s_zero_rows, 16)

            def move(out_, in_):
                return nc.scalar.copy(out_, in_)

            def attention_step(k, at):
                st, u, mid = at.st, at.u, at.mid
                tf, tc, ta, tb, tv, to = tiles_of(k, st)
                if not mid:
                    if k in (0, 2) and st == -1:
                        act.preload_act_table(ACT.Exp)
                    if k == 1 and st == 1:
                        act.preload_act_table(ACT.Sigmoid)
                    if k == 0 and 1 <= st <= 3:
                        mlp_loads(MLP_LOADS[3 * st - 3:3 * st])
                    if k == 1 and st == 3:
                        wait(act, "y_ps", 0, NT)
                        mlp_loads(MLP_LOADS[9:])
                if k < 2 and live(ta, mid):
                    zero_sorted_rows(k, at)
                tx, ux = (tc, 1 - u) if k == 2 else (ta, u)
                if k != 1 and live(to, mid):
                    wait(act, "ot_ps", k, to + 1)
                    move(OT[:], bank[7][:, 0:2 * P].rearrange("p (c n) -> p c n", c=2)).then_inc(s["ot_sb"], 1)
                def move_xt():
                    if live(tx, mid):
                        wait(act, "xt_ps", k, tx + 1)
                        dst = QK[:, ux, 0:2, :] if k == 1 else XT[:, ux, :, :]
                        move(dst, bank[0][:, 0:2 * P].rearrange("p (c n) -> p c n", c=2)).then_inc(s["xt_sb"], 1)

                if k != 2:
                    move_xt()
                if k == 1 and live(tb, mid):
                    wait(act, "sc_ps", 1, tb + 1)
                    wait(act, "pt_ps", 1, tb - 1)
                    nc.scalar.activation(PR[:, 1 - u, :], bank[4][:], ACT.Sigmoid,
                                         scale=4.0 * HD ** -0.5).then_inc(s["prob"], 1)
                if live(tv, mid):
                    wait(act, "pt_ps", k, tv + 1)
                    move(PT[:, u, :, :], bank[5][:].rearrange("p (g n) -> p g n", g=4)).then_inc(s["pt_sb"], 1)
                if k == 2:
                    move_xt()
                if k != 1 and live(tb, mid):
                    wait(act, "sub", k, tb + 1)
                    nc.scalar.activation(PR[:, 1 - u, :], PR[:, 1 - u, :], ACT.Exp, scale=HD ** -0.5).then_inc(s["prob"], 1)
                if k == 2 and live(tc, mid):
                    wait(act, "q_ps", 2, tc + 1)
                    move(QK[:, 1 - u, 0:2, :], bank[1][:, 0:2 * P].rearrange("p (c n) -> p c n", c=2)).then_inc(s["q_sb"], 1)
                if k == 2 and live(ta, mid):
                    wait(act, "mt_ps", 2, ta + 1)
                    move(CT[:, u, :, :], bank[0][:, 2 * P:4 * P].rearrange("p (c n) -> p c n", c=2)).then_inc(s["mt_sb"], 1)
                    wait(act, "k_ps", 2, ta + 1)
                    move(QK[:, u, 2:4, :], bank[1][:, 2 * P:4 * P].rearrange("p (c n) -> p c n", c=2)).then_inc(s["qk_sb"], 1)
                if k == 0 and live(ta, mid):
                    wait(act, "qk_ps", 0, ta + 1)
                    for i in range(4):
                        last = nc.scalar.activation(QK[:, u, i, :], bank[1][:, i * P:(i + 1) * P], ACT.Identity,
                                                    bias=qk_bias[:, i:i + 1])
                    last.then_inc(s["qk_sb"], 1)
                if k >= 2 and live(ta, mid):
                    wait(act, "v_ps", k, ta + 1)
                    wait_dma(act, "vd", k, at, -2)
                    move(VS[:, u, :], bank[3][:, 0:D]).then_inc(s["v_sb"], 1)

            def route_step(m, at):
                st, u, mid = at.st, at.u, at.mid
                q = ms[m]
                if live(st + 1, mid):
                    need(act, q["xt_ps"], st + 2)
                    need(act, q["lg_ps"], st)
                    src = bank[0][:, 0:2 * P].rearrange("p (c n) -> p c n", c=2)
                    move(XT[:, 1 - u, :, :], src).then_inc(q["xt_sb"], 1)
                    if m == 0:
                        move(XTA[:, :, span(st + 1, P)], src).then_inc(q["xta"], 1)
                    move(XNA[:, one(st + 1), :], XN[:, 1 - u, :]).then_inc(q["xna"], 1)

            def shared_group(g, first):
                for j in range(4):
                    need(act, sh["g_ps"], 4 * g + j + 1)
                    if not (first and j < 2):
                        act.wait_ge(sh["hid"], 4 * g + j - 1)
                    nc.scalar.activation(SG[:, j % 2, :], bank[4 + j % 2][:], ACT.Gelu,
                                         bias=bs1[:, 4 + j:5 + j]).then_inc(sh["gate"], 1)

            def expert_step(m, at):
                st, u, mid = at.st, at.u, at.mid
                q, n, R = ms[m], MOE[m]["n"], MOE[m]["R"]
                hc = 2 * R
                if live(st + 1, mid, n):
                    need(act, q["t_ps"], st + 2)
                    move(XT[:, 1 - u, :, :], bank[0][:, 0:2 * P].rearrange("p (c n) -> p c n", c=2)).then_inc(q["t_sb"], 1)
                if live(st, mid, n):
                    b1_at = C2 * 2 * MOE[m]["hid"]
                    for r in range(R):
                        par = (R * u + r) % 2
                        need(act, q["g_ps"], R * st + r + 1)
                        need(act, q["hid"] if m == 0 else q["u"], R * st + r - 1)
                        for i in range(2):
                            bias = W1[:, u, b1_at + hc + 2 * r + i:b1_at + hc + 2 * r + i + 1]
                            last = nc.scalar.activation(GS[:, par, i, :], bank[1 + par][:, i * P:(i + 1) * P],
                                                        ACT.Gelu if m == 0 else ACT.Identity, bias=bias)
                        last.then_inc(q["gate_sb"], 1)
                    if m == 1:
                        for r in range(R):
                            need(act, q["u"], R * st + r + 1)
                            nc.scalar.activation(HB[:, u, 2 * r:2 * r + 2, :], HB[:, u, 2 * r:2 * r + 2, :],
                                                 ACT.Silu).then_inc(q["hid"], 1)

            def final_step(at):
                st, u, mid = at.st, at.u, at.mid
                if live(st, mid):
                    need(act, fin["xt_ps"], st + 1)
                    move(XT[:, u, :, :], bank[0][:, 0:2 * P].rearrange("p (c n) -> p c n", c=2)).then_inc(fin["xt_sb"], 1)

            def moe(m):
                q = ms[m]
                token_steps(act, lambda at: route_step(m, at), -1)
                if m == 0:
                    weight_loads()
                act.wait_ge(q["gate"], 1)
                if m == 0:
                    nc.scalar.activation(r16[2][:], r16[2][:], ACT.Exp).then_inc(q["gate_e"], 1)
                    act.preload_act_table(ACT.Gelu)
                    act.wait_ge(s_load[2], 16 * len(MLP_LOADS))
                    shared_group(0, True)
                    with act.Fori(1, 4) as g:
                        shared_group(g, False)
                else:
                    nc.scalar.activation(RB[:, :, 0:E1], RB[:, :, 0:E1], ACT.Exp).then_inc(q["gate_e"], 1)
                    act.preload_act_table(ACT.Silu)
                row_steps(act, MOE[m]["n"], -1, lambda at: expert_step(m, at))
                if m == 1:
                    token_steps(act, final_step)

            for m in range(2):
                attention_pair(act, 2 * m, attention_step)
                moe(m)

        @block.vector
        def _(dve):
            nc.vector.memset(hold[:], 0.0).then_inc(s_prep, 1)
            dve.wait_ge(s_prep, 1)

            def prepare():
                dve.wait_ge(s_load[0], 16 * 9)
                nc.vector.tensor_copy(ident_bf[:], const("ident")).then_inc(s_prep, 1)
                nc.vector.tensor_copy(causal_bf[:], const("causal")).then_inc(s_prep, 1)
                dve.wait_ge(s_sign, 2)
                nc.vector.tensor_tensor(sign_qk[:], sign_cols[:, 0, :], sign_cols[:, 1, :], ALU.mult).then_inc(s_prep, 1)
                dve.wait_ge(s_prep, 4)
                nc.vector.tensor_tensor(sign_mask[:], const("head_mask").unsqueeze(1).to_broadcast([P, C2, HC]),
                                        sign_qk[:].unsqueeze(2).to_broadcast([P, C2, HC]), ALU.mult).then_inc(s_prep, 1)
                dve.wait_ge(s_prep, 5)

            def hold_until(sem, v):
                need(dve, sem, v)
                nc.vector.tensor_copy(hold[:], hold[:])

            def norm_stats(q, base, t, par):
                nc.vector.bn_stats(stats[:, par, :], X[:, one(t), :]).then_inc(q["stat"], 1)
                hold_until(q["stat"], base + t + 1)
                nc.vector.bn_aggr(mv[:, par, :], stats[:, par, :]).then_inc(q["mv"], 1)
                dve.wait_ge(q["mv"], base + t + 1)
                nc.vector.tensor_scalar(var[:, par, :], mv[:, par, 1:2], EPS, None, ALU.add).then_inc(q["var"], 1)

            def norm_apply(q, base, t, par):
                dve.wait_ge(q["rstd"], base + t + 1)
                nc.vector.tensor_scalar(XN[:, par, :], X[:, one(t), :], mv[:, par, 0:1], rstd[:, par, 0:1],
                                        ALU.subtract, ALU.mult).then_inc(q["xn"], 1)

            def combine(t, at):
                q = ms[0]
                dve.wait_ge(q["gy"][at.par(2)], 32 * (at.half(2) + 1))
                for c in range(2):
                    nc.vector.scalar_tensor_tensor(out=X[:, one(t), :], in0=GY[:, at.par(2), c:c + 1, :],
                                                   scalar=wts[:, c, one(t)], in1=X[:, one(t), :], op0=ALU.mult,
                                                   op1=ALU.add).then_inc(q["mix"], 1)
                    hold_until(q["mix"], 2 * t + c + 1)

            def attention_step(k, at):
                st, u, mid = at.st, at.u, at.mid
                tf, tc, ta, tb, tv, to = tiles_of(k, st)
                uf = u if k == 2 else 1 - u
                if k == 0 and not mid and st == 0:
                    prepare()

                def softmax_less_max():
                    if k != 1 and live(tb, mid):
                        wait(dve, "sc_ps", k, tb + 1)
                        sc = bank[4][:].rearrange("p (h t) -> p h t", h=H)
                        nc.vector.tensor_reduce(mx[:], sc, AX.X, ALU.max).then_inc(s["mx"], 1)
                        wait(dve, "mx", k, tb + 1)
                        wait(dve, "pt_ps", k, tb - 1)
                        nc.vector.tensor_tensor(PR[:, 1 - u, :].rearrange("p (h t) -> p h t", h=H), sc,
                                                mx[:].unsqueeze(2).to_broadcast([P, H, T]), ALU.subtract).then_inc(s["sub"], 1)

                def normalise_stats():
                    if live(tf, mid):
                        if k == 0:
                            if not mid:
                                for q in ([0] if tf < 4 else range(4)):
                                    dve.wait_ge(s_x[q], 16)
                        elif k == 2:
                            combine(tf, at)
                        else:
                            wait(dve, "res", k - 1, tf + 1)
                        norm_stats(s, n_before("stat", k), tf, uf)

                def normalise():
                    if live(tf, mid):
                        if k == 1:
                            wait(dve, "v_sb", 1, tf - 1)
                        norm_apply(s, n_before("stat", k), tf, uf)

                def residual():
                    if k != 1 and live(to, mid):
                        wait(dve, "y_ps", k, to + 1)
                        if k == 0:
                            wait(dve, "bias", 0, to + 1)
                        nc.vector.tensor_tensor(X[:, one(to), :], X[:, one(to), :], bank[7][:, 2 * P:4 * P].unsqueeze(1),
                                                ALU.add).then_inc(s["res"], 1)

                def router_stats():
                    if k == 3 and live(to, mid):
                        hold_until(s["res"], n_before("res", 3) + to + 1)
                        nc.vector.bn_stats(stats_all[:, one(to), :], X[:, one(to), :]).then_inc(ms[1]["stat"], 1)

                def rotate():
                    if k == 3 and live(ta, mid):
                        wait(dve, "qk_ps", 3, ta + 1)
                        for i, (b_, tab) in enumerate(((1, "cos"), (2, "sin"))):
                            last = nc.vector.tensor_tensor(RT[:, i, :].rearrange("p (a t) -> p a t", t=T),
                                                           bank[b_][:].rearrange("p (a t) -> p a t", t=T),
                                                           const(tab).unsqueeze(1).to_broadcast([P, 4 * BT, T]), ALU.mult)
                        last.then_inc(s["rope"], 1)

                def v_bias():
                    if k == 0 and live(ta, mid):
                        wait(dve, "v_ps", 0, ta + 1)
                        wait_dma(dve, "vd", 0, at, -2)
                        nc.vector.tensor_tensor(VS[:, u, :], bank[3][:, 0:D], rows0[:, 0, :], ALU.add).then_inc(s["v_sb"], 1)

                def spread_k():
                    if live(ta, mid):
                        wait(dve, "xt_sb" if k == 1 else "qk_sb", k, ta + 1)
                        wait(dve, "sc_ps", k, ta - 1)
                        for c in range(C2):
                            src = QK[:, u, c if k == 1 else 2 + c, :]
                            m_ = sign_mask[:, c, :] if k == 1 else const("head_mask")
                            nc.vector.tensor_tensor(KB[:, u, c, :, :], src.unsqueeze(1).to_broadcast([P, HC, P]),
                                                    m_.unsqueeze(2).to_broadcast([P, HC, P]), ALU.mult
                                                    ).then_inc(s["kb1" if c else "kb"], 1)

                def attention_out():
                    if live(tv, mid):
                        wait(dve, "o_ps", k, tv + 1)
                        if k == 1:
                            nc.vector.tensor_tensor(X[:, one(tv), :], X[:, one(tv), :], bank[6][:, 0:D].unsqueeze(1),
                                                    ALU.add).then_inc(s["res"], 1)
                        else:
                            wait(dve, "ot_ps", k, tv - 1)
                            nc.vector.reciprocal(rc[:], bank[6][:, D:D + H]).then_inc(s["rc"], 1)
                            wait(dve, "rc", k, tv + 1)
                            nc.vector.tensor_tensor(OS[:, u, :].rearrange("p (h d) -> p h d", h=H),
                                                    bank[6][:, 0:D].rearrange("p (h d) -> p h d", h=H),
                                                    rc[:].unsqueeze(2).to_broadcast([P, H, HD]), ALU.mult).then_inc(s["o_sb"], 1)

                def look_up():
                    if k == 2 and live(tc, mid):
                        v = n_before("cs_ps", 2) + tc + 1
                        hold_until(s["cs_ps"], v)
                        nc.vector.max(top8[:], bank[2][:, 0:S]).then_inc(s["top"], 1)
                        hold_until(s["top"], v)
                        nc.vector.max_index(idx8[:], top8[:], bank[2][:, 0:S]).then_inc(s["idx"], 1)
                        dve.wait_ge(s["idx"], v)
                        wait_dma(dve, "mem", 2, at, -1)
                        nc.vector.tensor_tensor(row[:, 1 - u:2 - u], idx8[:, 0:1], const("row0")[:, one(tc)],
                                                ALU.add).then_inc(s["row"], 1)

                if k == 0:
                    order = (softmax_less_max, normalise_stats, normalise, residual, spread_k, v_bias, attention_out)
                elif k == 1:
                    order = (normalise_stats, spread_k, normalise, attention_out)
                elif k == 2:
                    order = (softmax_less_max, normalise_stats, residual, attention_out, normalise, spread_k, look_up)
                else:
                    order = (softmax_less_max, normalise_stats, normalise, rotate, residual, router_stats, spread_k, attention_out)
                for part in order:
                    part()

            def router_norm(m, part):
                q, (t0, t1) = ms[m], NORM_TILES[part]
                if m == 0:
                    for t in range(t0, t1):
                        nc.vector.bn_stats(stats_all[:, t, :], X[:, t, :]).then_inc(q["stat"], 1)
                hold_until(q["stat"], t1 if m == 0 else NT)
                for t in range(t0, t1):
                    nc.vector.bn_aggr(mv_all[:, t, :], stats_all[:, t, :]).then_inc(q["mv"], 1)
                dve.wait_ge(q["mv"], t1)
                nc.vector.tensor_scalar(var_all[:, t0:t1], mv_all[:, t0:t1, 1], EPS, None, ALU.add).then_inc(q["var"], 1)

            def route_step(m, at):
                st, u, mid = at.st, at.u, at.mid
                q = ms[m]
                if not mid and st == 1:
                    router_norm(m, 1)
                if not mid and st + 2 == NORM_TILES[1][0]:
                    dve.wait_ge(q["rstd"], 2)
                if live(st + 2, mid):
                    need(dve, q["xna"], st + 1)
                    nc.vector.tensor_scalar(XN[:, u, :], X[:, one(st + 2), :], mv_all[:, one(st + 2), 0],
                                            rstd_all[:, one(st + 2)], ALU.subtract, ALU.mult).then_inc(q["xn"], 1)
                if live(st, mid):
                    need(dve, q["lg_ps"], st + 1)
                    nc.vector.tensor_copy(LG[:, one(st), 0:MOE[m]["E"]], bank[1][:, 0:MOE[m]["E"]].unsqueeze(1)
                                          ).then_inc(q["lg_sb"], 1)

            done = [0]

            def then(ins):
                done[0] += 1
                ins.then_inc(s_route_step, 1)
                dve.wait_ge(s_route_step, done[0])

            def pick(vals, rank, c, E, m_out):
                then(nc.vector.tensor_reduce(m_out[:], vals, AX.X, ALU.max))
                then(nc.vector.tensor_tensor(RC[:, :, 0:E], vals, m_out[:].unsqueeze(2).to_broadcast([P, NT, E]), ALU.is_equal))
                then(nc.vector.tensor_tensor(RC[:, :, 0:E], RC[:, :, 0:E], rank, ALU.mult))
                then(nc.vector.tensor_reduce(r16[3][:], RC[:, :, 0:E], AX.X, ALU.max))
                then(nc.vector.tensor_tensor(RM[:, c, :, 0:E], RC[:, :, 0:E],
                                             r16[3][:].unsqueeze(2).to_broadcast([P, NT, E]), ALU.is_equal))

            def route(m):
                q, E, n = ms[m], MOE[m]["E"], MOE[m]["n"]
                off = 0 if m == 0 else E0
                rank = const("ranks")[:, off:off + E].unsqueeze(1).to_broadcast([P, NT, E])
                L = LG[:, :, 0:E]
                V = RB[:, :, 0:E]
                dve.wait_ge(q["lg_sb"], NT)
                dve.wait_ge(s_load[2], 16 * len(MLP_LOADS))
                then(nc.vector.tensor_tensor(L, L, br[m][:].unsqueeze(1).to_broadcast([P, NT, E]), ALU.add))
                if m == 0:
                    then(nc.vector.tensor_scalar(V, L, 1.0 / TAU, None, ALU.mult))
                else:
                    then(nc.vector.tensor_reduce(r16[2][:], L, AX.X, ALU.max))
                    nc.vector.tensor_tensor(V, L, r16[2][:].unsqueeze(2).to_broadcast([P, NT, E]),
                                            ALU.subtract).then_inc(q["gate"], 1)
                    dve.wait_ge(q["gate_e"], 1)
                    then(nc.vector.tensor_reduce(r16[2][:], V, AX.X, ALU.add))
                    then(nc.vector.reciprocal(r16[2][:], r16[2][:]))
                    then(nc.vector.tensor_tensor(V, V, r16[2][:].unsqueeze(2).to_broadcast([P, NT, E]), ALU.mult))
                pick(V, rank, 0, E, r16[0])
                then(nc.vector.tensor_scalar(RA[:, :, 0:E], RM[:, 0, :, 0:E], NEG, None, ALU.mult))
                then(nc.vector.tensor_tensor(RA[:, :, 0:E], RA[:, :, 0:E], V, ALU.add))
                pick(RA[:, :, 0:E], rank, 1, E, r16[1])
                nc.vector.tensor_tensor(RC[:, :, 0:E], RM[:, 0, :, 0:E], RM[:, 1, :, 0:E], ALU.add).then_inc(q["onehot"], 1)
                if m == 0:
                    nc.vector.tensor_tensor(r16[2][:], r16[1][:], r16[0][:], ALU.subtract).then_inc(q["gate"], 1)
                    dve.wait_ge(q["gate_e"], 1)
                    then(nc.vector.tensor_scalar(r16[3][:], r16[2][:], 1.0, None, ALU.add))
                    then(nc.vector.reciprocal(wts[:, 0, :], r16[3][:]))
                    then(nc.vector.tensor_tensor(wts[:, 1, :], wts[:, 0, :], r16[2][:], ALU.mult))
                else:
                    then(nc.vector.tensor_copy(wts[:, 0, :], r16[0][:]))
                    then(nc.vector.tensor_copy(wts[:, 1, :], r16[1][:]))
                dve.wait_ge(q["rank_ps"], 1)
                within = bank[6][:, 0:NT * E].rearrange("p (t e) -> p t e", e=E)
                total = bank[7][:, 0:NT * E].rearrange("p (t e) -> p t e", e=E)
                O, other = RA[:, :, 0:E], RO[:, :, 0:E]
                nc.vector.memset(O[:, 0:1, :], 0.0)
                then(nc.vector.tensor_copy(O[:, 1:NT, :], total[:, 0:NT - 1, :]))
                for back in (1, 2, 4, 8):
                    nc.vector.tensor_copy(other[:, 0:back, :], O[:, 0:back, :])
                    then(nc.vector.tensor_tensor(other[:, back:NT, :], O[:, back:NT, :], O[:, 0:NT - back, :], ALU.add))
                    O, other = other, O
                cnt, ends, base = (r[:, 0:E] for r in re_)
                then(nc.vector.tensor_tensor(cnt, O[:, NT - 1, :], total[:, NT - 1, :], ALU.add))
                then(nc.vector.tensor_scalar(rei[:, 0:E], cnt, float(P - 1), None, ALU.add))
                then(nc.vector.tensor_scalar(rei[:, 0:E], rei[:, 0:E], 7, None, ALU.arith_shift_right))
                then(nc.vector.tensor_copy(cnt, rei[:, 0:E]))
                tril = const("tril").rearrange("p (a b) -> p a b", a=E0)[:, 0:E, 0:E]
                then(nc.vector.tensor_tensor(RX[:, 0:E, 0:E], cnt.unsqueeze(1).to_broadcast([P, E, E]), tril, ALU.mult))
                then(nc.vector.tensor_reduce(ends, RX[:, 0:E, 0:E], AX.X, ALU.add))
                then(nc.vector.tensor_tensor(base, ends, cnt, ALU.subtract))
                then(nc.vector.tensor_scalar(base, base, float(P), None, ALU.mult))
                then(nc.vector.tensor_tensor(O, O, within, ALU.add))
                then(nc.vector.tensor_tensor(O, O, base.unsqueeze(1).to_broadcast([P, NT, E]), ALU.add))
                for c in range(2):
                    then(nc.vector.tensor_tensor(RC[:, :, 0:E], RM[:, c, :, 0:E], O, ALU.mult))
                    then(nc.vector.tensor_reduce(r16[3][:], RC[:, :, 0:E], AX.X, ALU.add))
                    nc.vector.tensor_copy(pos[:, c, :], r16[3][:]).then_inc(q["pos"], 1)
                    dve.wait_ge(q["pos"], c + 1)
                then(nc.vector.tensor_tensor(RE[:, 0:n, 0:E], ends.unsqueeze(1).to_broadcast([P, n, E]),
                                             const("slots")[:, 0:n].unsqueeze(2).to_broadcast([P, n, E]), ALU.is_le))
                then(nc.vector.tensor_reduce(rsl[:, 0:n], RE[:, 0:n, 0:E], AX.X, ALU.add))
                nc.vector.tensor_scalar(slot_e[0:1, 0:n], rsl[0:1, 0:n], float(E - 1), None, ALU.min).then_inc(q["pos"], 1)

            def shared_group(g):
                for j in range(4):
                    dve.wait_ge(sh["a_ps"], 4 * g + j + 1)
                    dve.wait_ge(sh["gate"], 4 * g + j + 1)
                    nc.vector.scalar_tensor_tensor(out=SH[:, j, :], in0=bank[2 + j % 2][:], scalar=bs1[:, j:j + 1],
                                                   in1=SG[:, j % 2, :], op0=ALU.add, op1=ALU.mult).then_inc(sh["hid"], 1)
                for t in range(4):
                    nc.vector.tensor_tensor(X[:, one(4 * g + t), :], X[:, one(4 * g + t), :], bs2[:].unsqueeze(1), ALU.add
                                            ).then_inc(sh["bias"], 1)
                    dve.wait_ge(sh["bias"], 4 * g + t + 1)
                    dve.wait_ge(sh["y_ps"], 4 * g + t + 1)
                    nc.vector.tensor_tensor(X[:, one(4 * g + t), :], X[:, one(4 * g + t), :],
                                            bank[6 + t % 2][:, 0:D].unsqueeze(1), ALU.add).then_inc(sh["res"], 1)

            def expert_step(m, at):
                st, u, mid = at.st, at.u, at.mid
                q, n, R = ms[m], MOE[m]["n"], MOE[m]["R"]
                if live(st, mid, n):
                    b1_at = C2 * 2 * MOE[m]["hid"]
                    for r in range(R):
                        par = (R * u + r) % 2
                        need(dve, q["a_ps"], R * st + r + 1)
                        need(dve, q["gate_sb"], R * st + r + 1)
                        for i in range(2):
                            bias = W1[:, u, b1_at + 2 * r + i:b1_at + 2 * r + i + 1]
                            last = nc.vector.scalar_tensor_tensor(
                                out=HB[:, u, 2 * r + i, :], in0=bank[3 + par][:, i * P:(i + 1) * P], scalar=bias,
                                in1=GS[:, par, i, :], op0=ALU.add, op1=ALU.mult)
                        last.then_inc(q["hid"] if m == 0 else q["u"], 1)
                if live(st - 1, mid, n):
                    need(dve, q["y_ps"], st)
                    dve.wait_ge(q["b2"][1 - u], 16 * (at.half(-1) + 1))
                    need(dve, q["y_out"][1 - u], 16 * (at.half(-3) + 1))
                    nc.vector.tensor_tensor(YS[:, 1 - u, :], bank[5 + (1 - u)][:, 0:D], b2[:, 1 - u, :], ALU.add
                                            ).then_inc(q["y_sb"], 1)

            def final_step(at):
                st, u, mid = at.st, at.u, at.mid
                q = ms[1]
                if live(st, mid):
                    dve.wait_ge(q["gy"][u], 32 * (at.half(0) + 1))
                    need(dve, fin["xt_ps"], st - 1)
                    nc.vector.tensor_scalar(XN[:, u, :], GY[:, u, 0, :], wts[:, 0, one(st)], None, ALU.mult
                                            ).then_inc(q["mix"], 1)
                    dve.wait_ge(q["mix"], 2 * st + 1)
                    nc.vector.scalar_tensor_tensor(out=XN[:, u, :], in0=GY[:, u, 1, :], scalar=wts[:, 1, one(st)],
                                                   in1=XN[:, u, :], op0=ALU.mult, op1=ALU.add).then_inc(q["mix"], 1)
                if live(st - 1, mid):
                    need(dve, fin["y_ps"], st)
                    nc.vector.tensor_tensor(X[:, one(st - 1), :], X[:, one(st - 1), :], bank[1][:, 0:D].unsqueeze(1),
                                            ALU.add).then_inc(fin["out"], 1)

            def moe(m):
                q = ms[m]
                wait(dve, "res", 1 + 2 * m, NT)
                router_norm(m, 0)
                dve.wait_ge(q["rstd"], 1)
                token_steps(dve, lambda at: route_step(m, at), -2)
                route(m)
                if m == 0:
                    dve.wait_ge(s_load[2], 16 * len(MLP_LOADS))
                    shared_group(0)
                    with dve.Fori(1, 4) as g:
                        shared_group(g)
                if m == 1:
                    nc.vector.tensor_tensor(X[:], X[:], bf[:].unsqueeze(1).to_broadcast([P, NT, D]), ALU.add
                                            ).then_inc(fin["bias"], 1)
                row_steps(dve, MOE[m]["n"], 0, lambda at: expert_step(m, at))
                if m == 1:
                    dve.wait_ge(fin["bias"], 1)
                    token_steps(dve, final_step, 0, NT + 1)

            for m in range(2):
                attention_pair(dve, 2 * m, attention_step)
                moe(m)

        @block.tensor
        def _(pe):
            mm = nc.tensor.matmul
            pe.wait_ge(s_load[0], 16 * 9)
            pe.wait_ge(s_clear, 4)
            ident = const("ident")

            def transpose_tile(dst, src):
                for c in range(C2):
                    last = nc.tensor.transpose(dst[:, c * P:(c + 1) * P], src[:, c * P:(c + 1) * P], ident)
                return last

            def project(dst, w, src):
                for j in range(C2):
                    for c in range(C2):
                        last = mm(dst[:, j * P:(j + 1) * P], w[:, c, j * P:(j + 1) * P], src[:, c, :],
                                  start=(c == 0), stop=(c == C2 - 1))
                return last

            def project_rows(dst, w, src, n=D):
                for c in range(C2):
                    last = mm(dst, src[:, c, :], w[:, c, 0:n], start=(c == 0), stop=(c == C2 - 1))
                return last

            def scores(k, u, c):
                masked = k != 2
                if masked and c == 0:
                    mm(bank[4][:], ident_bf[:], causal_bf[:], start=True, stop=False, skip_group_check=True)
                for b in range(BT):
                    last = mm(bank[4][32 * b:32 * b + 32, c * HC * T:(c + 1) * HC * T], QK[:, u, c, 32 * b:32 * b + 32],
                              KB[:, u, c, :, 32 * b:32 * b + 32], start=not masked, stop=True, skip_group_check=True)
                return last

            def attention_step(k, at):
                st, u, mid = at.st, at.u, at.mid
                tf, tc, ta, tb, tv, to = tiles_of(k, st)
                if k >= 2 and not mid and st == -1:
                    pe.wait_ge(s_load[1], 16 * len(wname[4:]))
                tx, ux = (tc, 1 - u) if k == 2 else (ta, u)

                if k == 0 and not mid and st == 1:
                    pe.wait_ge(s_prep, 5)

                def score():
                    if live(tb, mid):
                        wait(pe, "kb", k, tb + 1)
                        wait(pe, "prob" if k == 1 else "sub", k, tb)
                        scores(k, 1 - u, 0)
                        wait(pe, "kb1", k, tb + 1)
                        scores(k, 1 - u, 1).then_inc(s["sc_ps"], 1)

                def transpose_out():
                    if k != 1 and live(to, mid):
                        wait(pe, "o_sb", k, to + 1)
                        wait(pe, "res", k, to)
                        transpose_tile(bank[7][:, 0:2 * P], OS[:, 1 - u, :]).then_inc(s["ot_ps"], 1)

                def transpose_x():
                    if live(tx, mid):
                        wait(pe, "xn", k, tx + 1)
                        wait(pe, "xt_sb", k, tx)
                        if k == 2:
                            wait(pe, "mt_sb", 2, tx - 1)
                        transpose_tile(bank[0][:, 0:2 * P], XN[:, ux, :]).then_inc(s["xt_ps"], 1)

                def transpose_probs():
                    if live(tv, mid):
                        wait(pe, "prob", k, tv + 1)
                        wait(pe, "pt_sb", k, tv)
                        for g in range(4):
                            last = nc.tensor.transpose(bank[5][:, g * P:(g + 1) * P], PR[:, u, g * P:(g + 1) * P], ident)
                        last.then_inc(s["pt_ps"], 1)

                def project_out():
                    if k != 1 and live(to, mid):
                        wait(pe, "ot_sb", k, to + 1)
                        project_rows(bank[7][:, 2 * P:4 * P], W[f"Wo{k}"], OT[:]).then_inc(s["y_ps"], 1)

                def project_query():
                    if k == 2 and live(tc, mid):
                        wait(pe, "xt_sb", 2, tc + 1)
                        wait(pe, "qk_sb", 2, tc - 1)
                        project(bank[1][:, 0:2 * P], W["Wq2"], XT[:, 1 - u, :, :]).then_inc(s["q_ps"], 1)

                def transpose_context():
                    if k == 2 and live(ta, mid):
                        wait_dma(pe, "mem", 2, at, 0)
                        wait(pe, "xt_sb", 2, min(ta + 2, NT) if not mid else ta + 2)
                        transpose_tile(bank[0][:, 2 * P:4 * P], MEM[:, u, :]).then_inc(s["mt_ps"], 1)

                def project_qk():
                    if k == 0 and live(ta, mid):
                        wait(pe, "xt_sb", 0, ta + 1)
                        wait(pe, "qk_sb", 0, ta)
                        wait_dma(pe, "ctx", 0, at, 0)
                        project(bank[1][:, 0:2 * P], W["Wq0"], XT[:, u, :, :])
                        project(bank[1][:, 2 * P:4 * P], W["Wk0"], CT[:, u, :, :]).then_inc(s["qk_ps"], 1)
                    if k == 3 and live(ta, mid):
                        wait(pe, "xt_sb", 3, ta + 1)
                        wait(pe, "rope", 3, ta)
                        project(bank[1][:, 0:2 * P], W["Wq3"], XT[:, u, :, :])
                        project(bank[1][:, 2 * P:4 * P], W["Wk3"], XT[:, u, :, :])
                        project(bank[2][:, 0:2 * P], W["Wqs3"], XT[:, u, :, :])
                        project(bank[2][:, 2 * P:4 * P], W["Wks3"], XT[:, u, :, :]).then_inc(s["qk_ps"], 1)

                def project_v():
                    if k in (0, 3) and live(ta, mid):
                        wait(pe, "v_sb", k, ta)
                        if k == 0:
                            project_rows(bank[3][:, 0:D], W["Wv0"], CT[:, u, :, :]).then_inc(s["v_ps"], 1)
                        else:
                            project_rows(bank[3][:, 0:D], W["Wv3"], XT[:, u, :, :]).then_inc(s["v_ps"], 1)
                    if k == 2 and live(ta, mid):
                        wait(pe, "v_sb", 2, ta)
                        project_rows(bank[3][:, 0:D], W["Wv2"], CT[:, u, :, :]).then_inc(s["v_ps"], 1)

                def weigh_v():
                    if live(tv, mid):
                        wait(pe, "pt_sb", k, tv + 1)
                        wait_dma(pe, "vb", k, at, -2)
                        wait(pe, "res" if k == 1 else "o_sb", k, tv)
                        for g in range(4):
                            for b in range(BT):
                                last = mm(bank[6][32 * b:32 * b + 32, g * 64:(g + 1) * 64], PT[:, u, g, 32 * b:32 * b + 32],
                                          VB[:, u, b, :, g * HD:(g + 1) * HD], start=True, stop=True,
                                          skip_group_check=True)
                        if k != 1:
                            for g in range(4):
                                last = mm(bank[6][:, D + 4 * g:D + 4 * g + 4], PT[:, u, g, :], const("block_ones"),
                                          start=True, stop=True, skip_group_check=True)
                        last.then_inc(s["o_ps"], 1)

                def project_context_k():
                    if k == 2 and live(ta, mid):
                        wait(pe, "mt_sb", 2, ta + 1)
                        wait(pe, "q_sb", 2, min(ta + 2, NT) if not mid else ta + 2)
                        project(bank[1][:, 2 * P:4 * P], W["Wk2"], CT[:, u, :, :]).then_inc(s["k_ps"], 1)

                def score_context():
                    if k == 2 and live(tc, mid):
                        wait(pe, "q_sb", 2, tc + 1)
                        wait_dma(pe, "cxt", 2, at, 1)
                        wait(pe, "idx", 2, tc)
                        for c in range(C2):
                            for b in range(BT):
                                last = mm(bank[2][32 * b:32 * b + 32, 0:S], QK[:, 1 - u, c, 32 * b:32 * b + 32],
                                          CXT[:, 1 - u, c, b, :], start=(c == 0), stop=(c == 1), skip_group_check=True)
                        last.then_inc(s["cs_ps"], 1)

                if k == 0 or k == 3:
                    order = (score, transpose_out, transpose_x, transpose_probs, project_qk, project_out, project_v, weigh_v)
                elif k == 1:
                    order = (transpose_x, score, transpose_probs, weigh_v)
                else:
                    order = (score, transpose_out, transpose_probs, transpose_x, project_out, project_query, transpose_context,
                             weigh_v, project_context_k, score_context, project_v)
                for part in order:
                    part()

            def route_step(m, at):
                st, u, mid = at.st, at.u, at.mid
                q = ms[m]
                if live(st + 1, mid):
                    need(pe, q["xn"], st + 2)
                    need(pe, q["xta"] if m == 0 else q["xt_sb"], st + 1)
                    transpose_tile(bank[0][:, 0:2 * P], XN[:, 1 - u, :]).then_inc(q["xt_ps"], 1)
                if live(st, mid):
                    need(pe, q["xt_sb"], st + 1)
                    need(pe, q["lg_sb"], st)
                    project_rows(bank[1][:, 0:MOE[m]["E"]], Wr[m], XT[:, u, :, :], MOE[m]["E"]).then_inc(q["lg_ps"], 1)

            def shared_group(g, first):
                pe.wait_ge(ms[0]["xta"], 4 * g + 4)
                for j in range(4):
                    if not (first and j < 2):
                        pe.wait_ge(sh["gate"], 4 * g + j - 1)
                    for c in range(C2):
                        last = mm(bank[4 + j % 2][:], Ws1[:, c, HS + j * P:HS + (j + 1) * P], XTA[:, c, span(g, 512)],
                                  start=(c == 0), stop=(c == 1))
                    last.then_inc(sh["g_ps"], 1)
                    if not (first and j < 2):
                        pe.wait_ge(sh["hid"], 4 * g + j - 1)
                    for c in range(C2):
                        last = mm(bank[2 + j % 2][:], Ws1[:, c, j * P:(j + 1) * P], XTA[:, c, span(g, 512)],
                                  start=(c == 0), stop=(c == 1))
                    last.then_inc(sh["a_ps"], 1)
                pe.wait_ge(sh["hid"], 4 * g + 4)
                if first:
                    pe.wait_ge(ms[0]["pos"], 3)
                for t in range(4):
                    if not (first and t < 2):
                        pe.wait_ge(sh["res"], 4 * g + t - 1)
                    dst = bank[6 + t % 2][:, 0:D]
                    for j in range(4):
                        last = mm(dst, SH[:, j, t * P:(t + 1) * P], Ws2[:, j, :], start=(j == 0), stop=(j == 3))
                    last.then_inc(sh["y_ps"], 1)

            def expert_step(m, at):
                st, u, mid = at.st, at.u, at.mid
                q, n, R, hid = ms[m], MOE[m]["n"], MOE[m]["R"], MOE[m]["hid"]
                if live(st + 1, mid, n):
                    pe.wait_ge(q["xs"][1 - u], 16 * (at.half(1) + 1))
                    need(pe, q["t_sb"], st + 1)
                    transpose_tile(bank[0][:, 0:2 * P], XS[:, 1 - u, :]).then_inc(q["t_ps"], 1)
                if live(st, mid, n):
                    pe.wait_ge(q["w1"][u], 16 * (at.half(0) + 1))
                    need(pe, q["t_sb"], st + 1)
                    for r in range(R):
                        par = (R * u + r) % 2
                        for half, bk, freed, sem in ((1, 1 + par, "gate_sb", "g_ps"),
                                                     (0, 3 + par, "hid" if m == 0 else "u", "a_ps")):
                            need(pe, q[freed], R * st + r - 1)
                            for i in range(2):
                                for c in range(C2):
                                    col = c * 2 * hid + half * hid + (2 * r + i) * P
                                    last = mm(bank[bk][:, i * P:(i + 1) * P], W1[:, u, col:col + P], XT[:, u, c, :],
                                              start=(c == 0), stop=(c == 1))
                            last.then_inc(q[sem], 1)
                if live(st - 1, mid, n):
                    pe.wait_ge(q["w2"][1 - u], 16 * (at.half(-1) + 1))
                    need(pe, q["hid"], R * st)
                    need(pe, q["y_sb"], st - 2)
                    dst = bank[5 + (1 - u)][:, 0:D]
                    for j in range(2 * R):
                        last = mm(dst, HB[:, 1 - u, j, :], W2[:, 1 - u, j * D:(j + 1) * D], start=(j == 0),
                                  stop=(j == 2 * R - 1))
                    last.then_inc(q["y_ps"], 1)

            def final_step(at):
                st, u, mid = at.st, at.u, at.mid
                if live(st, mid):
                    need(pe, ms[1]["mix"], 2 * (st + 1))
                    need(pe, fin["xt_sb"], st)
                    transpose_tile(bank[0][:, 0:2 * P], XN[:, u, :]).then_inc(fin["xt_ps"], 1)
                    need(pe, fin["xt_sb"], st + 1)
                    need(pe, fin["out"], st)
                    project_rows(bank[1][:, 0:D], Wf, XT[:, u, :, :]).then_inc(fin["y_ps"], 1)

            def moe(m):
                q, E = ms[m], MOE[m]["E"]
                pe.wait_ge(s_load[2], 16 * len(MLP_LOADS))
                token_steps(pe, lambda at: route_step(m, at), -1)
                pe.wait_ge(q["onehot"], 1)
                mm(bank[6][:, 0:NT * E], const("before"), RC[:, :, 0:E], start=True, stop=True)
                mm(bank[7][:, 0:NT * E], ones_sq[:], RC[:, :, 0:E], start=True, stop=True).then_inc(q["rank_ps"], 1)
                if m == 0:
                    shared_group(0, True)
                    with pe.Fori(1, 4) as g:
                        shared_group(g, False)
                row_steps(pe, MOE[m]["n"], -1, lambda at: expert_step(m, at))
                if m == 1:
                    token_steps(pe, final_step)

            for m in range(2):
                attention_pair(pe, 2 * m, attention_step)
                moe(m)

    return nc


def kernel(**inputs):
    import concourse.bacc as bacc
    from concourse.bass_utils import run_bass_kernel_spmd as run

    g = {k: np.asarray(v) for k, v in inputs.items()}

    def chunks(w):
        return w.reshape(-1, P, w.shape[-1]).transpose(1, 0, 2)

    ctx = g["ctx_1024"]
    swap = np.arange(D) ^ 1
    v_order = np.arange(D).reshape(4, 4, HD).transpose(1, 0, 2).reshape(-1)
    kv = g["L1_xattn_Wkv"]
    arrays = {
        "cst": CONST,
        "x": g["x"].reshape(NT, P, D).transpose(1, 0, 2),
        "ctx32": ctx[:, :T, :].reshape(NT, P, C2, P).transpose(3, 0, 2, 1),
        "ctxT": ctx.reshape(NT, BT, S, C2, P).transpose(4, 0, 3, 1, 2),
        "ctx_rows": ctx.reshape(B * S, D),
        "Wq0": chunks(g["L0_xattn_Wq"]), "Wk0": chunks(g["L0_xattn_Wk"]), "Wv0": chunks(g["L0_xattn_Wv"][:, v_order]),
        "Wo0": chunks(g["L0_xattn_Wo"]),
        "qk_bias": np.concatenate([g["L0_xattn_bq"].reshape(C2, P), g["L0_xattn_bk"].reshape(C2, P)]).T,
        "rows0": np.stack([g["L0_xattn_bv"][v_order], g["L0_xattn_bo"]])[None],
        "sign_cols": np.stack([g["L0_attn_bv_q"].reshape(C2, P), g["L0_attn_bv_k"].reshape(C2, P)]).transpose(2, 0, 1),
        "sign_v": g["L0_attn_bv_v"].reshape(1, D),
        "Wq2": chunks(g["L1_xattn_Wq"].T), "Wk2": chunks(np.tile(kv[:HD].T, (1, H))),
        "Wv2": chunks(np.tile(kv[HD:].T, (1, H))), "Wo2": chunks(g["L1_xattn_Wc"].T),
        "Wq3": chunks(g["L1_attn_Wq"]), "Wk3": chunks(g["L1_attn_Wk"]),
        "Wqs3": chunks(g["L1_attn_Wq"][:, swap]), "Wks3": chunks(g["L1_attn_Wk"][:, swap]),
        "Wv3": chunks(g["L1_attn_Wv"][:, v_order]), "Wo3": chunks(g["L1_attn_Wo"]),
        "Wr0": chunks(g["L0_ffn_Wr"]), "br0": g["L0_ffn_br"][None], "Wr1": chunks(g["L1_ffn_Wg"]), "br1": g["L1_ffn_bg"][None],
        "Ws1": chunks(g["L0_ffn_Ws1"]), "Ws2": chunks(g["L0_ffn_Ws2"]), "bs1": g["L0_ffn_bs1"].reshape(-1, P).T,
        "bs2": g["L0_ffn_bs2"][None],
        "Wf": chunks(g["L1_ffn_Wf"]), "bf": g["L1_ffn_bf"][None],
    }

    def expert_weights(first, bias):
        e, _, n = first.shape
        w = first.reshape(e, C2, P, n).transpose(0, 2, 1, 3).reshape(e, P, C2 * n)
        return np.concatenate([w, bias.reshape(e, n // P, P).transpose(0, 2, 1)], axis=2)

    arrays["W1_0"] = expert_weights(g["L0_ffn_We1"], g["L0_ffn_be1"])
    arrays["W1_1"] = expert_weights(np.concatenate([g["L1_ffn_W3"], g["L1_ffn_W1"]], axis=2),
                                    np.concatenate([g["L1_ffn_b3"], g["L1_ffn_b1"]], axis=1))
    for m, w in enumerate((g["L0_ffn_We2"], g["L1_ffn_W2"])):
        arrays[f"W2_{m}"] = w.reshape(w.shape[0], -1, P, D).transpose(0, 2, 1, 3).reshape(w.shape[0], P, -1)
    arrays["b2_0"], arrays["b2_1"] = g["L0_ffn_be2"], g["L1_ffn_b2"]

    nc = bacc.Bacc("TRN2", target_bir_lowering=False, num_devices=1)
    arrays = {k: np.ascontiguousarray(v) for k, v in arrays.items()}
    aps = {k: nc.dram_tensor(f"in_{k}", v.shape, mybir.dt.from_np(v.dtype), kind="ExternalInput").ap()
           for k, v in arrays.items()}
    out = nc.dram_tensor("out", (P, NT, D), F32, kind="ExternalOutput").ap()
    build(nc, aps, out)
    r = run(nc, [{f"in_{k}": v for k, v in arrays.items()}], core_ids=[0])
    return r.results[0]["out"].transpose(1, 0, 2).reshape(B, T, D)
```
